# Optimizing a Trainium2 kernel written in Bass

```python
import numpy as np
import jax
import jax.numpy as jnp

def _softmax(x, axis=-1):
    return jax.nn.softmax(x, axis=axis)

def _gelu(x):
    return jax.nn.gelu(x, approximate=True)

def _silu(x):
    return jax.nn.silu(x)

def _sigmoid(x):
    return jax.nn.sigmoid(x)

def _layernorm(x, axis=-1, eps=1e-05):
    m = jnp.mean(x, axis=axis, keepdims=True)
    v = jnp.var(x, axis=axis, keepdims=True)
    return (x - m) / jnp.sqrt(v + eps)

def _scatter_add(tgt, idx, src, axis=0):
    return tgt.at[idx].add(src)

def _segment_sum(src, seg, n):
    return jax.ops.segment_sum(src, seg, n)
kernel_name = 'mk_flamingo_gated_d1_seqx_r4_3ad631'

def setup_inputs(seed: int=0):
    np.random.seed(seed)
    _w = jnp.asarray

    def _rec_inputs():
        import jax
        import jax.numpy as jnp
        _rk = jax.random.key(seed)
        x = -0.0003929 + 0.9999 * jax.random.normal(jax.random.fold_in(_rk, 1), (8, 512, 256), jnp.float32)
        _lenS = 512 - jax.random.randint(jax.random.fold_in(_rk, 7), (8,), 0, max(1, 512 // 4) + 1, jnp.int32)
        _lenS2 = 1024 - jax.random.randint(jax.random.fold_in(_rk, 8), (8,), 0, max(1, 1024 // 4) + 1, jnp.int32)
        _ctx_1024P = jax.random.normal(jax.random.fold_in(_rk, 11), (8, 16, 256), jnp.float32)
        _ctx_1024c = jax.random.dirichlet(jax.random.fold_in(_rk, 511), 0.3 * jnp.ones((16,), jnp.float32), (8, 1024))
        _ctx_1024t = jnp.einsum('bsk,bkd->bsd', _ctx_1024c, _ctx_1024P)
        _ctx_1024t = _ctx_1024t * jax.lax.rsqrt(jnp.mean(jnp.square(_ctx_1024t)) + 1e-12) * 0.953939
        ctx_1024 = 2.81802e-05 + 1.00001 * (_ctx_1024t + 0.3 * jax.random.normal(jax.random.fold_in(_rk, 611), (8, 1024, 256), jnp.float32))
        _g = jax.random.normal(jax.random.fold_in(_rk, 9001), (2, 1), jnp.float32)
        _g = jnp.sign(_g) * jnp.maximum(jnp.abs(_g), 1.0) + (_g == 0) * 1.0
        g_xattn = _g[0]
        g_ffn = _g[1]
        return (x, ctx_1024, g_xattn, g_ffn)
    x, ctx_1024, g_xattn, g_ffn = _rec_inputs()

    def _L0_xattn_setup():
        import jax, jax.numpy as jnp
        import numpy as np
        E = 256
        NUM_HEADS = 16
        DK = E // NUM_HEADS
        EPS = 1e-05
        NEG_INF = -jnp.inf

        def layer_norm(x, g, b):
            mu = jnp.mean(x, axis=-1, keepdims=True)
            var = jnp.var(x, axis=-1, keepdims=True)
            return (x - mu) * jax.lax.rsqrt(var + EPS) * g + b

        def self_attn(x, Wq, Wk, Wv):
            Q, K, V = (x @ Wq, x @ Wk, x @ Wv)
            energy = jnp.einsum('bqd,bkd->bqk', Q, K)
            S = energy.shape[-1]
            lengths = jnp.sum(energy[:, 0] != 0, axis=-1)
            kidx = jnp.arange(S)
            pad = kidx[None, None, :] >= lengths[:, None, None]
            causal = kidx[None, :] < kidx[:, None]
            causal = (kidx[None, :] > kidx[:, None])[None]
            energy = jnp.where(pad | causal, NEG_INF, energy)
            score = jax.nn.softmax(energy / np.sqrt(DK), axis=-1)
            return jnp.einsum('bqk,bkd->bqd', score, V)

        def cross_attn(x, context, Wq, Wk, Wv):
            Q = x @ Wq
            K, V = (context @ Wk, context @ Wv)
            energy = jnp.einsum('bqd,bkd->bqk', Q, K)
            Sk = energy.shape[-1]
            lengths = jnp.sum(energy[:, 0] != 0, axis=-1)
            kidx = jnp.arange(Sk)
            pad = kidx[None, None, :] >= lengths[:, None, None]
            energy = jnp.where(pad, NEG_INF, energy)
            score = jax.nn.softmax(energy / np.sqrt(DK), axis=-1)
            return jnp.einsum('bqk,bkd->bqd', score, V)
        key = jax.random.key(seed)
        ks = jax.random.split(key, 12)
        B, S = (8, 512)
        s = 1.0 / np.sqrt(E)
        inp = {'x': jax.random.normal(ks[0], (B, S, E), jnp.float32), 'context': jax.random.normal(ks[1], (B, S, E), jnp.float32), 'Wq1': jax.random.normal(ks[2], (E, E), jnp.float32) * s, 'Wk1': jax.random.normal(ks[3], (E, E), jnp.float32) * s, 'Wv1': jax.random.normal(ks[4], (E, E), jnp.float32) * s, 'Wq2': jax.random.normal(ks[5], (E, E), jnp.float32) * s, 'Wk2': jax.random.normal(ks[6], (E, E), jnp.float32) * s, 'Wv2': jax.random.normal(ks[7], (E, E), jnp.float32) * s, 'fc1_w': jax.random.normal(ks[8], (E, E), jnp.float32) * s, 'fc1_b': jnp.zeros((E,), jnp.float32), 'fc2_w': jax.random.normal(ks[9], (E, E), jnp.float32) * s, 'fc2_b': jnp.zeros((E,), jnp.float32), 'ln1_g': jnp.ones((E,), jnp.float32), 'ln1_b': jnp.zeros((E,), jnp.float32), 'ln2_g': jnp.ones((E,), jnp.float32), 'ln2_b': jnp.zeros((E,), jnp.float32), 'ln3_g': jnp.ones((E,), jnp.float32), 'ln3_b': jnp.zeros((E,), jnp.float32)}
        return inp
    _L0_xattn_all = _L0_xattn_setup()
    _L0_xattn_in = {k: v for k, v in _L0_xattn_all.items() if k in ('Wq1', 'Wk1', 'Wv1', 'Wq2', 'Wk2', 'Wv2', 'fc1_w', 'fc1_b', 'fc2_w', 'fc2_b', 'ln1_g', 'ln1_b', 'ln2_g', 'ln2_b', 'ln3_g', 'ln3_b')}
    del _L0_xattn_all

    def _L0_ffn_setup():
        import jax, jax.numpy as jnp
        import numpy as np
        DIM = 256
        N_EXPERTS = 8
        TOPK = 2
        CAPACITY_FACTOR = 1.25
        B, S = (2, 512)

        def _moe(x, Wr, W1, b1, W2, b2):
            Bsz, Sl, D = x.shape
            E = Wr.shape[1]
            T = Bsz * Sl
            capacity = max(1, int(T * CAPACITY_FACTOR / E))
            xt = x.reshape(T, D)
            probs_full = jax.nn.softmax(xt @ Wr, axis=-1)
            topv, topi = jax.lax.top_k(probs_full, TOPK)
            topv = topv / jnp.sum(topv, axis=-1, keepdims=True)
            onehot = jax.nn.one_hot(topi, E, dtype=x.dtype)
            rank = jnp.cumsum(onehot, axis=0)
            keep = (rank <= capacity).astype(x.dtype) * onehot
            w = jnp.einsum('tk,tke->te', topv, keep)
            h = jax.nn.gelu(jnp.einsum('td,edf->etf', xt, W1) + b1[:, None, :], approximate=False)
            y = jnp.einsum('etf,efd->etd', h, W2) + b2[:, None, :]
            out = jnp.einsum('te,etd->td', w, y)
            return out.reshape(Bsz, Sl, D)
        key = jax.random.key(seed)
        ks = jax.random.split(key, 6)
        D, E, F = (DIM, N_EXPERTS, 4 * DIM)
        x = jax.random.normal(ks[0], (B, S, D), dtype=jnp.float32)
        Wr = jax.random.normal(ks[1], (D, E), dtype=jnp.float32) * (1.0 / np.sqrt(D))
        W1 = jax.random.normal(ks[2], (E, D, F), dtype=jnp.float32) * (1.0 / np.sqrt(D))
        b1 = jnp.zeros((E, F), dtype=jnp.float32)
        W2 = jax.random.normal(ks[3], (E, F, D), dtype=jnp.float32) * (1.0 / np.sqrt(F))
        b2 = jnp.zeros((E, D), dtype=jnp.float32)
        return {'x': x, 'Wr': Wr, 'W1': W1, 'b1': b1, 'W2': W2, 'b2': b2}
    _L0_ffn_all = _L0_ffn_setup()
    _L0_ffn_in = {k: v for k, v in _L0_ffn_all.items() if k in ('Wr', 'W1', 'b1', 'W2', 'b2')}
    del _L0_ffn_all
    return {'x': x, 'ctx_1024': ctx_1024, 'g_xattn': g_xattn, 'g_ffn': g_ffn, 'L0_xattn_Wq1': _L0_xattn_in['Wq1'], 'L0_xattn_Wk1': _L0_xattn_in['Wk1'], 'L0_xattn_Wv1': _L0_xattn_in['Wv1'], 'L0_xattn_Wq2': _L0_xattn_in['Wq2'], 'L0_xattn_Wk2': _L0_xattn_in['Wk2'], 'L0_xattn_Wv2': _L0_xattn_in['Wv2'], 'L0_xattn_fc1_w': _L0_xattn_in['fc1_w'], 'L0_xattn_fc1_b': _L0_xattn_in['fc1_b'], 'L0_xattn_fc2_w': _L0_xattn_in['fc2_w'], 'L0_xattn_fc2_b': _L0_xattn_in['fc2_b'], 'L0_xattn_ln1_g': _L0_xattn_in['ln1_g'], 'L0_xattn_ln1_b': _L0_xattn_in['ln1_b'], 'L0_xattn_ln2_g': _L0_xattn_in['ln2_g'], 'L0_xattn_ln2_b': _L0_xattn_in['ln2_b'], 'L0_xattn_ln3_g': _L0_xattn_in['ln3_g'], 'L0_xattn_ln3_b': _L0_xattn_in['ln3_b'], 'L0_ffn_Wr': _L0_ffn_in['Wr'], 'L0_ffn_W1': _L0_ffn_in['W1'], 'L0_ffn_b1': _L0_ffn_in['b1'], 'L0_ffn_W2': _L0_ffn_in['W2'], 'L0_ffn_b2': _L0_ffn_in['b2']}

def reference(x, ctx_1024, g_xattn, g_ffn, L0_xattn_Wq1, L0_xattn_Wk1, L0_xattn_Wv1, L0_xattn_Wq2, L0_xattn_Wk2, L0_xattn_Wv2, L0_xattn_fc1_w, L0_xattn_fc1_b, L0_xattn_fc2_w, L0_xattn_fc2_b, L0_xattn_ln1_g, L0_xattn_ln1_b, L0_xattn_ln2_g, L0_xattn_ln2_b, L0_xattn_ln3_g, L0_xattn_ln3_b, L0_ffn_Wr, L0_ffn_W1, L0_ffn_b1, L0_ffn_W2, L0_ffn_b2):
    import jax
    import jax.numpy as jnp

    def _L0_xattn_ref(x, context, Wq1, Wk1, Wv1, Wq2, Wk2, Wv2, fc1_w, fc1_b, fc2_w, fc2_b, ln1_g, ln1_b, ln2_g, ln2_b, ln3_g, ln3_b):
        import jax, jax.numpy as jnp
        import numpy as np
        E = 256
        NUM_HEADS = 16
        DK = E // NUM_HEADS
        EPS = 1e-05
        NEG_INF = -jnp.inf

        def layer_norm(x, g, b):
            mu = jnp.mean(x, axis=-1, keepdims=True)
            var = jnp.var(x, axis=-1, keepdims=True)
            return (x - mu) * jax.lax.rsqrt(var + EPS) * g + b

        def self_attn(x, Wq, Wk, Wv):
            Q, K, V = (x @ Wq, x @ Wk, x @ Wv)
            energy = jnp.einsum('bqd,bkd->bqk', Q, K)
            S = energy.shape[-1]
            lengths = jnp.sum(energy[:, 0] != 0, axis=-1)
            kidx = jnp.arange(S)
            pad = kidx[None, None, :] >= lengths[:, None, None]
            causal = kidx[None, :] < kidx[:, None]
            causal = (kidx[None, :] > kidx[:, None])[None]
            energy = jnp.where(pad | causal, NEG_INF, energy)
            score = jax.nn.softmax(energy / np.sqrt(DK), axis=-1)
            return jnp.einsum('bqk,bkd->bqd', score, V)

        def cross_attn(x, context, Wq, Wk, Wv):
            Q = x @ Wq
            K, V = (context @ Wk, context @ Wv)
            energy = jnp.einsum('bqd,bkd->bqk', Q, K)
            Sk = energy.shape[-1]
            lengths = jnp.sum(energy[:, 0] != 0, axis=-1)
            kidx = jnp.arange(Sk)
            pad = kidx[None, None, :] >= lengths[:, None, None]
            energy = jnp.where(pad, NEG_INF, energy)
            score = jax.nn.softmax(energy / np.sqrt(DK), axis=-1)
            return jnp.einsum('bqk,bkd->bqd', score, V)
        z = self_attn(x, Wq1, Wk1, Wv1)
        x = layer_norm(x + z, ln1_g, ln1_b)
        z = cross_attn(x, context, Wq2, Wk2, Wv2)
        x = layer_norm(x + z, ln2_g, ln2_b)
        z = jax.nn.relu(x @ fc1_w + fc1_b)
        z = z @ fc2_w + fc2_b
        return layer_norm(x + z, ln3_g, ln3_b)

    def _L0_ffn_ref(x, Wr, W1, b1, W2, b2):
        import jax, jax.numpy as jnp
        import numpy as np
        DIM = 256
        N_EXPERTS = 8
        TOPK = 2
        CAPACITY_FACTOR = 1.25
        B, S = (2, 512)

        def _moe(x, Wr, W1, b1, W2, b2):
            Bsz, Sl, D = x.shape
            E = Wr.shape[1]
            T = Bsz * Sl
            capacity = max(1, int(T * CAPACITY_FACTOR / E))
            xt = x.reshape(T, D)
            probs_full = jax.nn.softmax(xt @ Wr, axis=-1)
            topv, topi = jax.lax.top_k(probs_full, TOPK)
            topv = topv / jnp.sum(topv, axis=-1, keepdims=True)
            onehot = jax.nn.one_hot(topi, E, dtype=x.dtype)
            rank = jnp.cumsum(onehot, axis=0)
            keep = (rank <= capacity).astype(x.dtype) * onehot
            w = jnp.einsum('tk,tke->te', topv, keep)
            h = jax.nn.gelu(jnp.einsum('td,edf->etf', xt, W1) + b1[:, None, :], approximate=False)
            y = jnp.einsum('etf,efd->etd', h, W2) + b2[:, None, :]
            out = jnp.einsum('te,etd->td', w, y)
            return out.reshape(Bsz, Sl, D)
        return _moe(x, Wr, W1, b1, W2, b2)
    x = x + jnp.tanh(g_xattn[0]) * _L0_xattn_ref(_layernorm(x, axis=-1), ctx_1024, L0_xattn_Wq1, L0_xattn_Wk1, L0_xattn_Wv1, L0_xattn_Wq2, L0_xattn_Wk2, L0_xattn_Wv2, L0_xattn_fc1_w, L0_xattn_fc1_b, L0_xattn_fc2_w, L0_xattn_fc2_b, L0_xattn_ln1_g, L0_xattn_ln1_b, L0_xattn_ln2_g, L0_xattn_ln2_b, L0_xattn_ln3_g, L0_xattn_ln3_b)
    x = x + jnp.tanh(g_ffn[0]) * _L0_ffn_ref(_layernorm(x, axis=-1), L0_ffn_Wr, L0_ffn_W1, L0_ffn_b1, L0_ffn_W2, L0_ffn_b2)
    return x

_drawn_inputs = setup_inputs


def setup_inputs(seed=0):
    import zlib

    import numpy as np

    out = dict(_drawn_inputs(seed))
    spreads = {'L0_xattn_fc1_b': (0.0, 0.1),
     'L0_xattn_fc2_b': (0.0, 0.1),
     'L0_xattn_ln1_g': (1.0, 0.2),
     'L0_xattn_ln1_b': (0.0, 0.1),
     'L0_xattn_ln2_g': (1.0, 0.2),
     'L0_xattn_ln2_b': (0.0, 0.1),
     'L0_xattn_ln3_g': (1.0, 0.2),
     'L0_xattn_ln3_b': (0.0, 0.1),
     'L0_ffn_b1': (0.0, 0.1),
     'L0_ffn_b2': (0.0, 0.1)}
    factors = {}
    for name, (base, spread) in spreads.items():
        noise = np.random.default_rng([zlib.crc32(name.encode()), seed]).standard_normal(out[name].shape)
        drawn = base * np.exp(spread * noise) if base else spread * noise
        out[name] = jnp.asarray(drawn.astype(out[name].dtype))
    for name, factor in factors.items():
        out[name] = (out[name] * factor).astype(out[name].dtype)
    return out
```

```python
from contextlib import ExitStack

import concourse.bass as bass
from concourse import mybir

F32 = mybir.dt.float32
F16 = mybir.dt.float16
I32 = mybir.dt.int32
U32 = mybir.dt.uint32
ALU = mybir.AluOpType
ACT = mybir.ActivationFunctionType
AX = mybir.AxisListType

P = 128
EPS = 1e-5
MASKED = -3.0e38
NEVER = 1.0e9
SKIP = 30000.0

ORDER = [
    "b_ctx", "c_x3T", "b_q2T", "a_ln0", "c_fc1", "b_len", "a_xnT", "b_s2a", "c_fc2", "b_s2b", "c_ln3",
    "a_q1T", "a_len", "a_s1", "b_p2T", "c_x4T", "b_c2T", "c_logits", "a_p1T", "c_rank", "a_c1T", "b_z2",
    "b_ln2", "a_z1", "c_slots", "a_ln1", "a_x2T", "c_gone",
]
LAG = {"a": 0, "b": 1, "c": 2}

FILLS = {
    "T": {"b_ctx": 4, "c_x3T": 2, "a_xnT": 2, "b_p2T": 8, "c_x4T": 2, "a_p1T": 4, "a_x2T": 2},
    "M": {"b_q2T": 2, "c_fc1": 2, "b_len": 2, "c_fc2": 2, "a_q1T": 2, "a_len": 2, "b_c2T": 2,
          "c_logits": 1, "a_c1T": 2, "c_rank": 1, "b_z2": 2, "a_z1": 2},
    "S": {"b_s2a": 2, "b_s2b": 2, "a_s1": 2},
}

EMPTIED = {
    "b_ctx": ("ctxT_l", range(4)), "c_x3T": ("x3T_l", range(2)), "a_xnT": ("xnT_l", range(2)),
    "b_p2T": ("p2T_l", range(8)), "c_x4T": ("x4T", range(2)), "a_p1T": ("p1T_l", range(4)),
    "a_x2T": ("x2T_l", range(2)), "b_q2T": ("q2T_l", range(2)), "c_fc1": ("fh", range(2)),
    "c_fc2": ("y3", range(2)), "a_q1T": ("q1T_l", range(2)), "b_c2T": ("c2T_l", range(2)),
    "c_logits": ("logits", [0]), "a_c1T": ("c1T_l", range(2)), "c_rank": ("route", [6]),
    "b_z2": ("y2", [1, 3]), "a_z1": ("y1", [1, 3]), "b_s2a": ("sm2", [0, 1]), "b_s2b": ("sm2", [2, 3]),
    "a_s1": ("sm1", [2, 3]), "b_len": (("nz2", "len2"), None), "a_len": (("nz1", "len1"), None),
}

SIGNALS = {
    "x_in": 1, "ctx_in": 1, "xr_in": 1, "x4_out": 1, "dispatched": 8,
    "bn0": 4, "mv0": 1, "ve0": 1, "rstd0": 1, "xn": 1, "xn_h": 1, "xn_l": 1,
    "xnT_p": 2, "xnT_h": 2, "xnT_l": 2, "q1T_p": 2, "q1T_h": 2, "q1T_l": 2,
    "e1_p": 1, "nz1": 1, "len1_p": 1, "len1": 1, "mask1": 1, "inv1": 3,
    "s1_p": 2, "sm1": 4, "nmax1": 1, "p1": 4, "p1T_p": 4, "p1T_h": 4, "p1T_l": 4,
    "c1T_p": 2, "c1T_h": 2, "c1T_l": 2, "z1_p": 2, "y1": 4,
    "bn1": 4, "mv1": 1, "ve1": 1, "rstd1": 1, "yn1": 1, "yg1": 1, "x2": 1,
    "x2T_p": 2, "x2T_h": 2, "x2T_l": 2,
    "ctx_h": 1, "ctx_l": 1, "ctxT_p": 4, "ctxT_h": 4, "ctxT_l": 4,
    "q2T_p": 2, "q2T_h": 2, "q2T_l": 2, "e2_p": 1, "nz2": 1, "len2_p": 1, "len2": 1, "mask2": 1,
    "inv2": 3, "s2_p": 4, "sm2": 4, "nmax2": 2, "p2": 4, "p2T_p": 8, "p2T_h": 8, "p2T_l": 8,
    "c2T_p": 2, "c2T_h": 2, "c2T_l": 2, "z2_p": 2, "y2": 4,
    "bn2": 4, "mv2": 1, "ve2": 1, "rstd2": 1, "yn2": 1, "yg2": 1, "x3": 1,
    "x3b": 1, "x3T_p": 2, "x3T_h": 2, "x3T_l": 2, "fc1_p": 2, "fh": 2, "fh_h": 2, "fh_l": 2,
    "fc2_p": 2, "y3": 2, "bn3": 4, "mv3": 1, "ve3": 1, "rstd3": 1, "yn3": 1, "yg3": 1, "yb3": 1, "x4": 1,
    "bn4": 4, "mv4": 1, "ve4": 1, "rstd4": 1, "rowx": 1, "x4T_p": 2, "x4T": 2,
    "logits_p": 1, "logits": 1, "route": 12, "gap": 1, "gate": 1, "rank_p": 1, "slots": 1, "rows_gone": 1,
}


class Iteration:

    def __init__(self, j, offset):
        self.j, self.offset = j, offset

    def times(self, n, plus):
        at = n * self.offset + plus
        return at if self.j is None else self.j * n + at


def flamingo_moe_kernel(nc, x, ctx_in, g_x, g_f, wq1, wk1, wv1, wq2, wk2, wv2, fc1_w, fc1_b, fc2_w, fc2_b,
                        ln1_g, ln1_b, ln2_g, ln2_b, ln3_g, ln3_b, wr, w1, b1, w2, b2, out, xs):
    B, S, D = x.shape
    SK = ctx_in.shape[1]
    E, _, F = w1.shape
    DC, QT, KT = D // P, S // P, SK // P
    FC = F // P
    T = B * S
    CAP = int(T * 1.25 / E)
    SLOTS = 2 * CAP
    ROW = xs.shape[1]
    TOKEN, WEIGHT = D, D + 1
    SCALE = 1.0 / 4.0
    SELF_W = P * QT * (QT + 1) // 2
    assert D == 256 and S == 512 and SK == 1024 and E == 8 and CAP % P == 0 and B > 2

    q_seg = [P * t * (t + 1) // 2 for t in range(QT)]
    k_seg = [P * (t * QT - t * (t - 1) // 2) for t in range(QT)]

    ctx = ExitStack()
    with ctx:
        def sb(name, shape, dt=F32):
            return ctx.enter_context(nc.sbuf_tensor(name, shape, dt))

        def sem(name):
            return ctx.enter_context(nc.semaphore(name))

        ident = sb("ident", [P, P])
        b1T = sb("b1T", [P, E * FC + DC])
        tanh_g = sb("tanh_g", [P, 2])
        w_raw = sb("w_raw", [P, DC * F + FC * D])

        w1_raw = w_raw[:, 0:DC * F].rearrange("p (c f) -> p c f", c=DC)
        w2_raw = w_raw[:, DC * F:].rearrange("p (c d) -> p c d", c=FC)
        w_in = sem("w_in")
        W_IN = 32

        def load_expert(eng, e):
            eng.dma_start(w1_raw, w1[e].rearrange("(c p) f -> p c f", p=P)).then_inc(w_in, 16)
            eng.dma_start(w2_raw, w2[e].rearrange("(c p) d -> p c d", p=P)).then_inc(w_in, 16)

        attention(nc, locals())
        experts(nc, locals())


def mm3(pe, out, left, right, first=True, last=True):
    (lh, ll), (rh, rl) = left, right
    pe.matmul(out, lh, rh, start=first, stop=False)
    pe.matmul(out, lh, rl, start=False, stop=False)
    return pe.matmul(out, ll, rh, start=False, stop=last)


def attention(nc, g):
    (x, ctx_in, g_x, g_f, wq1, wk1, wv1, wq2, wk2, wv2, fc1_w, fc1_b, fc2_w, fc2_b, ln1_g, ln1_b, ln2_g, ln2_b,
     ln3_g, ln3_b, wr, b1, out, xs) = (g[n] for n in (
         "x", "ctx_in", "g_x", "g_f", "wq1", "wk1", "wv1", "wq2", "wk2", "wv2", "fc1_w", "fc1_b", "fc2_w", "fc2_b",
         "ln1_g", "ln1_b", "ln2_g", "ln2_b", "ln3_g", "ln3_b", "wr", "b1", "out", "xs"))
    B, S, D, SK, E, F, DC, QT, KT, FC, T, CAP, SLOTS, ROW, TOKEN, WEIGHT, SCALE, SELF_W = (g[n] for n in (
        "B", "S", "D", "SK", "E", "F", "DC", "QT", "KT", "FC", "T", "CAP", "SLOTS", "ROW", "TOKEN", "WEIGHT",
        "SCALE", "SELF_W"))
    q_seg, k_seg, ident, b1T, tanh_g = (g[n] for n in ("q_seg", "k_seg", "ident", "b1T", "tanh_g"))

    with ExitStack() as ctx:
        def sb(name, shape, dt=F32):
            return ctx.enter_context(nc.sbuf_tensor(name, shape, dt))

        def pair(name, shape):
            return sb(name + "_h", shape, F16), sb(name + "_l", shape, F16)

        def psum(name, shape):
            return ctx.enter_context(nc.psum_tensor(name, shape, F32))

        def sem(name):
            return ctx.enter_context(nc.semaphore(name))

        tri = sb("tri", [P, P], F16)
        ones = sb("ones", [P, P], F16)
        key1 = sb("key1", [P, SELF_W])
        key2 = sb("key2", [P, SK])
        iota_e = sb("iota_e", [P, E])
        slot_off = sb("slot_off", [P, QT, 2])
        neg_half = sb("neg_half", [P, QT])
        eps = sb("eps", [P, QT])
        token = sb("token", [P, QT])
        taken = sb("taken", [P, 2 * E], F16)
        vec = {n: sb(n + "_bc", [P, D]) for n in ("g1", "o1", "g2", "o2", "g3", "o3", "fc2_b")}
        wr_sb = sb("wr_sb", [P, DC, E])
        a1 = pair("a1", [P, DC, D])
        a2 = pair("a2", [P, DC, D])
        wv1_p, wv2_p = pair("wv1", [P, DC, D]), pair("wv2", [P, DC, D])
        fc1_p, fc2_p = pair("fc1", [P, DC, D]), pair("fc2", [P, DC, D])
        b1_raw = sb("b1_raw", [E * FC + DC, P])
        gates_in = sb("gates_in", [P, 2])

        x_sb = sb("x_sb", [P, QT, D])
        xn = sb("xn", [P, QT, D])
        xn_p = pair("xn", [P, QT, D])
        xnT = pair("xnT", [P, DC, S])
        q1T = pair("q1T", [P, DC, S])
        mask1 = sb("mask1", [P, SELF_W])
        sm1 = sb("sm1", [P, SELF_W])
        p1T = pair("p1T", [P, SELF_W])
        c1T = pair("c1T", [P, DC, S])
        y1 = sb("y1", [P, QT, D])
        x2 = sb("x2", [P, QT, D])
        x2T = pair("x2T", [P, DC, S])
        c_sb = sb("c_sb", [P, KT, D])
        c_p = pair("c", [P, KT, D])
        ctxT = pair("ctxT", [P, DC, SK])
        q2T = pair("q2T", [P, DC, S])
        mask2 = sb("mask2", [P, SK])
        sm2 = sb("sm2", [P, QT, SK])
        p2T = pair("p2T", [P, KT, S])
        c2T = pair("c2T", [P, DC, S])
        x3 = sb("x3", [P, QT, D])
        xr = sb("xr", [P, QT, D])
        x3b = sb("x3b", [P, QT, D])
        x3T = pair("x3T", [P, DC, S])
        fh = sb("fh", [P, DC, S])
        fh_p = pair("fh", [P, DC, S])
        x4 = sb("x4", [P, QT, D])
        x4T = sb("x4T", [P, DC, S])
        rows = sb("rows", [P, QT, ROW])
        stat = [sb(f"stat{n}", [P, QT, 6]) for n in range(5)]
        mv = [sb(f"mv{n}", [P, QT, 2]) for n in range(5)]
        ve = [sb(f"ve{n}", [P, QT]) for n in range(5)]
        rstd = [sb(f"rstd{n}", [P, QT]) for n in range(5)]
        nz_k = [sb("nz_k1", [P, QT], F16), sb("nz_k2", [P, KT], F16)]
        length = [sb(f"length{n}", [P, 1]) for n in range(2)]
        top = [sb(f"top{n}", [P, QT]) for n in range(2)]
        ntop = [sb(f"ntop{n}", [P, QT]) for n in range(2)]
        total = [sb(f"total{n}", [P, QT]) for n in range(2)]
        some = [sb(f"some{n}", [P, 1]) for n in range(2)]
        full = [sb(f"full{n}", [P, QT]) for n in range(2)]
        inv = [sb(f"inv{n}", [P, QT]) for n in range(2)]
        lg = sb("lg", [P, QT, E])
        best = sb("best", [P, QT, 8])
        besti = sb("besti", [P, QT, 8], U32)
        pick = sb("pick", [P, QT, 2])
        hot = sb("hot", [P, QT, 2, E], F16)
        rsel = sb("rsel", [P, QT, 2, E])
        rank = sb("rank", [P, QT, 2])
        gap = sb("gap", [P, QT])
        egap = sb("egap", [P, QT])
        den = sb("den", [P, QT])
        gate = sb("gate", [P, QT, 2])
        keep = sb("keep", [P, QT, 2])
        over = sb("over", [P, QT, 2])
        slotf = sb("slotf", [P, QT, 2])
        slot = sb("slot", [P, QT * 2], I32)
        newly = sb("newly", [P, 2 * E])

        raw_w = {n: sm2[:, i // 2, (i % 2) * DC * D:(i % 2 + 1) * DC * D].rearrange("p (c d) -> p c d", c=DC)
                 for i, n in enumerate(("wq1", "wk1", "wq2", "wk2", "wv1", "wv2", "fc1", "fc2"))}
        wT = {n: t[:, :, 0:D] for n, t in (("wq1", fh), ("wk1", x4T))}
        wT["wq2"], wT["wk2"] = fh[:, :, D:2 * D], x4T[:, :, D:2 * D]
        blank = x3[:, 0:2, :].rearrange("p t d -> p (t d)")[:, 0:ROW]

        pool_t = [psum(f"bank_t{n}", [P, 512]) for n in range(2)]
        pool_m = [psum(f"bank_m{n}", [P, 512]) for n in range(2)]
        pool_s = [psum(f"bank_s{n}", [P, 1024]) for n in range(2)]
        banks = {"T": pool_t, "M": pool_m, "S": pool_s}

        ev = {n: sem(n) for n in SIGNALS}
        setup_in, vec_in, const_p, const_v = sem("setup_in"), sem("vec_in"), sem("const_p"), sem("const_v")
        wT_p, wT_v, a_p, a_v, gates = sem("wT_p"), sem("wT_v"), sem("a_p"), sem("a_v"), sem("gates")
        blank_out, settled = sem("blank_out"), sem("settled")
        DMA_EVENTS = ("x_in", "ctx_in", "xr_in", "x4_out", "dispatched")

        def unit(name):
            return 16 if name in DMA_EVENTS else 1

        def done(name, ins):
            ins.then_inc(ev[name], unit(name))

        def need(eng, name, it, k=None):
            n, k = SIGNALS[name], SIGNALS[name] - 1 if k is None else k
            eng.wait_ge(ev[name], it.times(n * unit(name), 1 + (k + 1) * unit(name)))

        def before(eng, name, it):
            eng.wait_ge(ev[name], it.times(SIGNALS[name] * unit(name), 1))

        def live(i, step):
            return 0 <= i - LAG[step[0]] < B

        def fills_in(pool, i):
            return [(s, k) for s in ORDER if live(i, s) for k in range(FILLS[pool].get(s, 0))]

        def fill(pool, step, k, i):
            index = fills_in(pool, i).index((step, k))
            assert len(fills_in(pool, i)) % 2 == 0
            return index

        def bank_of(pool, step, k, at):
            return banks[pool][fill(pool, step, k, at[0]) % 2]

        def open_fill(pe, pool, step, k, at):
            i, j = at
            index = fill(pool, step, k, i)
            if index >= 2:
                was, back = fills_in(pool, i)[index - 2], 0
            elif i > 0:
                was, back = fills_in(pool, i - 1)[index - 2], 1
                assert j is None or was == fills_in(pool, i)[index - 2]
            else:
                return banks[pool][index % 2]
            event, numbers = EMPTIED[was[0]]
            if was[0] == "b_len" or was[0] == "a_len":
                event, number = event[was[1]], 0
            else:
                number = numbers[was[1]]
            need(pe, event, Iteration(j, i - back - LAG[was[0][0]]), number)
            return banks[pool][index % 2]

        def walk(eng, body):
            def one(i, j):
                for s in ORDER:
                    if live(i, s):
                        body(s, Iteration(j, i - LAG[s[0]]), (i, j))
            for i in (0, 1):
                one(i, None)
            with eng.Fori(0, B - 2) as j:
                one(2, j)
            for i in (B, B + 1):
                one(i, None)

        def credit(eng, names):
            for n in names:
                if n != "dispatched":
                    eng.sem_inc(ev[n], 1)

        def settle(eng):
            eng.sem_inc(settled, 1)

        def batch(dram, it):
            view = dram.rearrange("b (t p) d -> b p t d", p=P)
            return view[it.offset] if it.j is None else view[it.j + it.offset]

        def out_rows(it):
            view = out[0:T, :].rearrange("(b t p) d -> b p t d", p=P, t=QT)
            return view[it.offset] if it.j is None else view[it.j + it.offset]

        names = list(SIGNALS)
        block = ctx.enter_context(nc.Block())

        @block.sync
        def _(sp):
            for n in ("wq1", "wk1", "wq2", "wk2", "wv1", "wv2", "fc1", "fc2"):
                dram = {"wq1": wq1, "wk1": wk1, "wq2": wq2, "wk2": wk2, "wv1": wv1, "wv2": wv2, "fc1": fc1_w,
                        "fc2": fc2_w}[n]
                sp.dma_start(raw_w[n], dram.rearrange("(c p) d -> p c d", p=P)).then_inc(setup_in, 16)
            credit(sp, names[0:4])
            sp.dma_start(b1_raw[0:E * FC, :], b1.rearrange("e (c p) -> (e c) p", p=P)).then_inc(vec_in, 16)
            sp.dma_start(b1_raw[E * FC:, :], fc1_b.rearrange("(c p) -> c p", p=P)).then_inc(vec_in, 16)
            sp.dma_start(wr_sb[:], wr.rearrange("(c p) e -> p c e", p=P)).then_inc(vec_in, 16)
            for v, n in ((ln1_g, "g1"), (ln1_b, "o1"), (ln2_g, "g2"), (ln2_b, "o2"), (ln3_g, "g3"), (ln3_b, "o3"),
                         (fc2_b, "fc2_b")):
                sp.dma_start(vec[n][:], v.partition_broadcast(P)).then_inc(vec_in, 16)
            sp.dma_start(gates_in[:, 0:1], g_x.partition_broadcast(P)).then_inc(vec_in, 16)
            sp.dma_start(gates_in[:, 1:2], g_f.partition_broadcast(P)).then_inc(vec_in, 16)

            def step(s, it, at):
                if s == "a_ln0":
                    before(sp, "xn", it)
                    done("x_in", sp.dma_start(x_sb[:], batch(x, it)))
                if s == "b_ctx":
                    before(sp, "ctx_l", it)
                    before(sp, "ctxT_p", it)
                    done("ctx_in", sp.dma_start(c_sb[:], batch(ctx_in, it)))
                if s == "c_x3T":
                    before(sp, "x4", it)
                    done("xr_in", sp.dma_start(xr[:], batch(x, it)))
                if s == "c_ln3":
                    need(sp, "x4", it)
                    done("x4_out", sp.dma_start(out_rows(it), x4[:]))

            walk(sp, step)
            sp.wait_ge(ev["x4_out"], 1 + 16 * B)
            g["load_expert"](sp, 0)

        @block.gpsimd
        def _(pool):
            credit(pool, names[4:20])
            pool.memset(ident[:], 0.0).then_inc(const_p, 1)
            pool.memset(tri[:], 1.0).then_inc(const_p, 1)
            pool.memset(ones[:], 1.0).then_inc(const_p, 1)
            pool.memset(blank, 0.0).then_inc(const_p, 1)
            pool.memset(neg_half[:], -0.5).then_inc(const_p, 1)
            pool.memset(eps[:], EPS).then_inc(const_p, 1)
            pool.memset(taken[:], 0.0).then_inc(const_p, 1)
            pool.memset(rows[:], 0.0).then_inc(const_p, 1)
            for t in range(QT):
                pool.iota(key1[:, q_seg[t]:q_seg[t] + P * (t + 1)], [[1, P * (t + 1)]], base=0, channel_multiplier=0,
                          allow_small_or_imprecise_dtypes=True).then_inc(const_p, 1)
            pool.iota(key2[:], [[1, SK]], base=0, channel_multiplier=0,
                      allow_small_or_imprecise_dtypes=True).then_inc(const_p, 1)
            pool.iota(iota_e[:], [[1, E]], base=0, channel_multiplier=0,
                      allow_small_or_imprecise_dtypes=True).then_inc(const_p, 1)
            pool.iota(slot_off[:], [[0, QT], [CAP, 2]], base=-1, channel_multiplier=0,
                      allow_small_or_imprecise_dtypes=True).then_inc(const_p, 1)
            pool.iota(token[:], [[P, QT]], base=0, channel_multiplier=1,
                      allow_small_or_imprecise_dtypes=True).then_inc(const_p, 1)
            pool.wait_ge(const_p, 12 + QT)
            pool.affine_select(out=ident[:], in_=ident[:], compare_op=ALU.not_equal, fill=1.0, base=0,
                               pattern=[[-1, P]], channel_multiplier=1).then_inc(const_p, 1)
            pool.affine_select(out=tri[:], in_=tri[:], compare_op=ALU.is_ge, fill=0.0, base=0,
                               pattern=[[1, P]], channel_multiplier=-1).then_inc(const_p, 1)
            for t in range(QT):
                d = key1[:, q_seg[t] + P * t:q_seg[t] + P * (t + 1)]
                pool.affine_select(out=d, in_=d, compare_op=ALU.is_ge, fill=NEVER, base=0, pattern=[[-1, P]],
                                   channel_multiplier=1).then_inc(const_p, 1)
            pool.iota(blank[:, TOKEN:TOKEN + 1].bitcast(I32), [[0, 1]], base=T, channel_multiplier=1).then_inc(const_p, 1)
            pool.wait_ge(const_p, 15 + 2 * QT)
            pool.dma_start(xs.rearrange("(c p) d -> p c d", p=P),
                           blank.unsqueeze(1).to_broadcast([P, E * SLOTS // P, ROW])).then_inc(blank_out, 16)
            pool.dma_start(out[T:T + P, :], blank[:, 0:D]).then_inc(blank_out, 16)
            pool.wait_ge(gates, 1)
            pool.wait_ge(vec_in, 16 * 12)
            for n in ("g3", "o3"):
                pool.tensor_scalar(vec[n][:], vec[n][:], tanh_g[:, 0:1], None, ALU.mult).then_inc(const_p, 1)
            pool.wait_ge(const_p, 17 + 2 * QT)
            pool.wait_ge(blank_out, 32)

            def norm_rstd(n, it):
                need(pool, f"mv{n}", it)
                done(f"ve{n}", pool.tensor_tensor(ve[n][:], mv[n][:, :, 1], eps[:], ALU.add))
                need(pool, f"ve{n}", it)
                done(f"rstd{n}", pool.tensor_tensor(rstd[n][:], ve[n][:], neg_half[:], ALU.pow))

            def affine(n, it, src, dst, scale, offset, scaled, ready):
                need(pool, f"yn{n}", it)
                sc = vec[scale][:].unsqueeze(1).to_broadcast([P, QT, D])
                of = vec[offset][:].unsqueeze(1).to_broadcast([P, QT, D])
                done(scaled, pool.tensor_tensor(src[:], src[:], sc, ALU.mult))
                need(pool, scaled, it)
                done(ready, pool.tensor_tensor(dst[:], src[:], of, ALU.add))

            def step(s, it, at):
                if s == "b_ctx":
                    need(pool, "ctx_in", it)
                    need(pool, "ctx_h", it)
                    before(pool, "c2T_p", it)
                    done("ctx_l", pool.tensor_tensor(c_p[1][:], c_sb[:], c_p[0][:], ALU.subtract))
                if s == "c_x3T":
                    need(pool, "x3", it)
                    before(pool, "y3", it)
                    fb = vec["fc2_b"][:].unsqueeze(1).to_broadcast([P, QT, D])
                    done("x3b", pool.tensor_tensor(x3b[:], x3[:], fb, ALU.add))
                if s == "a_ln0":
                    norm_rstd(0, it)
                    need(pool, "xn_h", it)
                    before(pool, "c1T_p", it)
                    done("xn_l", pool.tensor_tensor(xn_p[1][:], xn[:], xn_p[0][:], ALU.subtract))
                if s == "c_fc1":
                    for c in range(DC):
                        need(pool, "fh_h", it, c)
                        if c == 0:
                            before(pool, "fc2_p", it)
                        done("fh_l", pool.tensor_tensor(fh_p[1][:, c, :], fh[:, c, :], fh_p[0][:, c, :],
                                                        ALU.subtract))
                if s == "c_ln3":
                    norm_rstd(3, it)
                    affine(3, it, x4, x4, "g3", "o3", "yg3", "yb3")
                    norm_rstd(4, it)
                if s == "b_ln2":
                    norm_rstd(2, it)
                    affine(2, it, x3, x3, "g2", "o2", "yg2", "x3")
                if s == "a_ln1":
                    norm_rstd(1, it)
                    before(pool, "y2", Iteration(it.j, it.offset))
                    affine(1, it, y1, x2, "g1", "o1", "yg1", "x2")
                if s == "c_slots":
                    need(pool, "slots", it)
                    need(pool, "rowx", it)
                    settle(pool)
                    for t in range(QT):
                        for k in range(2):
                            n = 2 * t + k
                            done("dispatched", pool.indirect_dma_start(
                                xs, bass.IndirectOffsetOnAxis(ap=slot[:, n:n + 1].bitcast(U32), axis=0),
                                rows[:, t, :], None, bounds_check=E * SLOTS - 1, oob_is_err=False))

                if s == "c_gone":
                    pool.wait_ge(ev["dispatched"], it.times(16 * 2 * QT, 16 * 2 * QT))
                    pool.sem_inc(ev["rows_gone"], 1)

            walk(pool, step)

        @block.tensor
        def _(pe):
            credit(pe, names[20:40])
            pe.wait_ge(const_p, 13 + QT)
            pe.wait_ge(setup_in, 16 * 8)
            for i, n in enumerate(("wq1", "wk1", "wq2", "wk2")):
                if i >= 2:
                    pe.wait_ge(wT_v, i - 1)
                for eb in range(DC):
                    for db in range(DC):
                        m = pe.transpose(pool_t[i % 2][:, eb * D + db * P:eb * D + (db + 1) * P],
                                         raw_w[n][:, db, eb * P:(eb + 1) * P], ident[:])
                m.then_inc(wT_p, 1)
            pe.wait_ge(vec_in, 16 * 12)
            nb = E * FC + DC
            pe.transpose(pool_m[0][:, 0:nb], b1_raw[:], ident[0:nb, 0:nb]).then_inc(wT_p, 1)
            for i, (q, k) in enumerate((("wq1", "wk1"), ("wq2", "wk2"))):
                pe.wait_ge(wT_v, 2 * i + 2)
                for db in range(DC):
                    for eb in range(DC):
                        m = pe.matmul(pool_s[i][:, db * D:(db + 1) * D], wT[q][:, eb, db * P:(db + 1) * P],
                                      wT[k][:, eb, :], start=eb == 0, stop=eb == DC - 1)
                m.then_inc(a_p, 1)
            pe.wait_ge(a_v, 2)
            pe.wait_ge(wT_v, 5)
            pe.wait_ge(const_v, 2)

            def part(p, *i):
                return p[0][i], p[1][i]

            def turn(src, c, tiles, pool, step, k, at):
                bank = open_fill(pe, pool, step, k, at)
                for n, t in enumerate(tiles):
                    m = pe.transpose(bank[:, n * P:(n + 1) * P], src[:, t, c * P:(c + 1) * P], ident[:])
                return m

            def project(w, xT, dst, at, s, ready, srcs, it):
                for c in range(DC):
                    for n in srcs:
                        need(pe, n, it)
                    bank = open_fill(pe, "M", s, c, at)
                    for d in range(DC):
                        m = mm3(pe, bank[:], part(w, slice(None), d, slice(c * P, (c + 1) * P)),
                                part(xT, slice(None), d, slice(None)), d == 0, d == DC - 1)
                    done(ready, m)

            def back(xT, w, at, s, ready, it):
                for h in range(QT // 2):
                    bank = open_fill(pe, "M", s, h, at)
                    for n in range(2):
                        t = 2 * h + n
                        for d in range(DC):
                            m = mm3(pe, bank[:, n * D:(n + 1) * D], part(xT, slice(None), d, slice(t * P, (t + 1) * P)),
                                    part(w, slice(None), d, slice(None)), d == 0, d == DC - 1)
                    done(ready, m)

            def row0(kT, qT, tiles, s, at, ready, n, ones_ready, len_ready, it):
                bank = open_fill(pe, "M", s, 0, at)
                for t in range(tiles):
                    for d in range(DC):
                        m = mm3(pe, bank[:, t:t + 1], part(kT, slice(None), d, slice(t * P, (t + 1) * P)),
                                part(qT, slice(None), d, slice(0, 1)), d == 0, d == DC - 1)
                done(ready, m)
                need(pe, ones_ready, it)
                bank = open_fill(pe, "M", s, 1, at)
                done(len_ready, pe.matmul(bank[:, 0:tiles], ones[:], nz_k[n][:], start=True, stop=True))

            def step(s, it, at):
                if s == "b_ctx":
                    need(pe, "ctx_in", it)
                    for c in range(DC):
                        for h in range(2):
                            k = 2 * c + h
                            done("ctxT_p", turn(c_sb, c, range(4 * h, 4 * h + 4), "T", s, k, at))
                if s == "c_x3T":
                    need(pe, "x3", it)
                    for c in range(DC):
                        done("x3T_p", turn(x3, c, range(QT), "T", s, c, at))
                if s == "b_q2T":
                    project(a2, x2T, q2T, at, s, "q2T_p", ["x2T_l"], it)
                if s == "c_fc1":
                    project(fc1_p, x3T, fh, at, s, "fc1_p", ["x3T_l"], it)
                if s == "b_len":
                    need(pe, "q2T_l", it)
                    need(pe, "ctxT_l", it)
                    row0(ctxT, q2T, KT, s, at, "e2_p", 1, "nz2", "len2_p", it)
                if s == "a_xnT":
                    need(pe, "xn", it)
                    for c in range(DC):
                        done("xnT_p", turn(xn, c, range(QT), "T", s, c, at))
                if s in ("b_s2a", "b_s2b"):
                    for n in range(2):
                        t = (0 if s == "b_s2a" else 2) + n
                        bank = open_fill(pe, "S", s, n, at)
                        for h in range(2):
                            for d in range(DC):
                                m = mm3(pe, bank[:, h * 512:(h + 1) * 512],
                                        part(q2T, slice(None), d, slice(t * P, (t + 1) * P)),
                                        part(ctxT, slice(None), d, slice(h * 512, (h + 1) * 512)), d == 0, d == DC - 1)
                        done("s2_p", m)
                if s == "c_fc2":
                    need(pe, "fh_l", it)
                    back(fh_p, fc2_p, at, s, "fc2_p", it)
                if s == "a_q1T":
                    project(a1, xnT, q1T, at, s, "q1T_p", ["xnT_l"], it)
                if s == "a_len":
                    need(pe, "q1T_l", it)
                    row0(xnT, q1T, QT, s, at, "e1_p", 0, "nz1", "len1_p", it)
                if s == "a_s1":
                    for n, tiles in enumerate(((0, 1, 2), (3,))):
                        bank = open_fill(pe, "S", s, n, at)
                        for t in tiles:
                            w = P * (t + 1)
                            o = q_seg[t] + (P if t == 2 else 0) - (q_seg[3] if t == 3 else 0)
                            for d in range(DC):
                                m = mm3(pe, bank[:, o:o + w], part(q1T, slice(None), d, slice(t * P, (t + 1) * P)),
                                        part(xnT, slice(None), d, slice(0, w)), d == 0, d == DC - 1)
                        done("s1_p", m)
                if s == "b_p2T":
                    need(pe, "p2", it)
                    for k in range(KT):
                        bank = open_fill(pe, "T", s, k, at)
                        for t in range(QT):
                            m = pe.transpose(bank[:, t * P:(t + 1) * P], sm2[:, t, k * P:(k + 1) * P], ident[:])
                        done("p2T_p", m)
                if s == "c_x4T":
                    need(pe, "rowx", it)
                    for c in range(DC):
                        done("x4T_p", turn(rows, c, range(QT), "T", s, c, at))
                if s == "b_c2T":
                    need(pe, "ctx_l", it)
                    for c in range(DC):
                        bank = open_fill(pe, "M", s, c, at)
                        for k in range(KT):
                            if c == 0:
                                need(pe, "p2T_l", it, k)
                            m = mm3(pe, bank[:], part(c_p, slice(None), k, slice(c * P, (c + 1) * P)),
                                    part(p2T, slice(None), k, slice(None)), k == 0, k == KT - 1)
                        done("c2T_p", m)
                if s == "c_logits":
                    need(pe, "x4T", it)
                    bank = open_fill(pe, "M", s, 0, at)
                    for t in range(QT):
                        for d in range(DC):
                            m = pe.matmul(bank[:, t * E:(t + 1) * E], x4T[:, d, t * P:(t + 1) * P], wr_sb[:, d, :],
                                          start=d == 0, stop=d == DC - 1)
                    done("logits_p", m)
                if s == "a_p1T":
                    need(pe, "p1", it)
                    for k in range(QT):
                        bank = open_fill(pe, "T", s, k, at)
                        for n, t in enumerate(range(k, QT)):
                            o = q_seg[t] + k * P
                            m = pe.transpose(bank[:, n * P:(n + 1) * P], sm1[:, o:o + P], ident[:])
                        done("p1T_p", m)
                if s == "c_rank":
                    need(pe, "route", it, 5)
                    bank = open_fill(pe, "M", s, 0, at)
                    w = 2 * E
                    hot2 = hot[:].rearrange("p t k e -> p t (k e)")
                    out_ = bank[:, 0:QT * w].rearrange("p (t w) -> p t w", t=QT)
                    pe.matmul(out_, tri[:], hot2, start=True, stop=False)
                    for t in range(QT - 1):
                        pe.matmul(out_[:, t + 1:, :], ones[:], hot2[:, t:t + 1, :].to_broadcast([P, QT - 1 - t, w]),
                                  start=False, stop=False)
                    done("rank_p", pe.matmul(out_, ones[:], taken[:].unsqueeze(1).to_broadcast([P, QT, w]),
                                             start=False, stop=True))
                if s == "a_c1T":
                    need(pe, "xn_l", it)
                    for c in range(DC):
                        bank = open_fill(pe, "M", s, c, at)
                        for k in range(QT):
                            if c == 0:
                                need(pe, "p1T_l", it, k)
                            w = P * (QT - k)
                            m = mm3(pe, bank[:, k * P:512], part(xn_p, slice(None), k, slice(c * P, (c + 1) * P)),
                                    part(p1T, slice(None), slice(k_seg[k], k_seg[k] + w)), k == 0, k == QT - 1)
                        done("c1T_p", m)
                if s == "b_z2":
                    need(pe, "c2T_l", it)
                    back(c2T, wv2_p, at, s, "z2_p", it)
                if s == "a_z1":
                    need(pe, "c1T_l", it)
                    back(c1T, wv1_p, at, s, "z1_p", it)
                if s == "a_x2T":
                    need(pe, "x2", it)
                    for c in range(DC):
                        done("x2T_p", turn(x2, c, range(QT), "T", s, c, at))

            walk(pe, step)

        EVACUATE = {
            "b_ctx": ("T", "ctxT_p", ctxT, "ctxT_h", "ctxT_l", "s2_p"),
            "c_x3T": ("T", "x3T_p", x3T, "x3T_h", "x3T_l", "fc1_p"),
            "b_q2T": ("M", "q2T_p", q2T, "q2T_h", "q2T_l", "s2_p"),
            "a_xnT": ("T", "xnT_p", xnT, "xnT_h", "xnT_l", "s1_p"),
            "a_q1T": ("M", "q1T_p", q1T, "q1T_h", "q1T_l", "s1_p"),
            "b_p2T": ("T", "p2T_p", p2T, "p2T_h", "p2T_l", "c2T_p"),
            "b_c2T": ("M", "c2T_p", c2T, "c2T_h", "c2T_l", "z2_p"),
            "a_p1T": ("T", "p1T_p", p1T, "p1T_h", "p1T_l", "c1T_p"),
            "a_c1T": ("M", "c1T_p", c1T, "c1T_h", "c1T_l", "z1_p"),
            "a_x2T": ("T", "x2T_p", x2T, "x2T_h", "x2T_l", "q2T_p"),
        }

        def where(s, k, t):
            if s == "b_ctx":
                return t[:, k // 2, (k % 2) * 512:(k % 2 + 1) * 512], 512
            if s == "a_p1T":
                w = P * (QT - k)
                return t[:, k_seg[k]:k_seg[k] + w], w
            return t[:, k, :], 512

        @block.scalar
        def _(act):
            credit(act, names[40:70])
            act.wait_ge(vec_in, 16 * 12)
            act.activation(tanh_g[:], gates_in[:], ACT.Tanh).then_inc(gates, 1)

            def step(s, it, at):
                if s in EVACUATE:
                    pool, filled, t, high, _, reader = EVACUATE[s]
                    for k in range(FILLS[pool][s]):
                        need(act, filled, it, k)
                        if k == 0:
                            before(act, reader, it)
                        dst, w = where(s, k, t[0])
                        done(high, act.activation(dst, bank_of(pool, s, k, at)[:, 0:w], ACT.Copy))
                if s == "b_ctx":
                    need(act, "ctx_in", it)
                    before(act, "c2T_p", it)
                    done("ctx_h", act.activation(c_p[0][:], c_sb[:], ACT.Copy))
                if s == "a_xnT":
                    need(act, "xn", it)
                    before(act, "c1T_p", it)
                    done("xn_h", act.activation(xn_p[0][:], xn[:], ACT.Copy))
                if s == "c_fc1":
                    for c in range(DC):
                        need(act, "fc1_p", it, c)
                        before(act, "fh_l", it)
                        done("fh", act.activation(fh[:, c, :], bank_of("M", s, c, at)[:], ACT.Relu,
                                                  bias=b1T[:, E * FC + c:E * FC + c + 1]))
                if s in ("b_s2a", "b_s2b"):
                    b0 = 0 if s == "b_s2a" else 2
                    need(act, "nmax2", it, b0 // 2)
                    for t in (b0, b0 + 1):
                        done("p2", act.activation(sm2[:, t, :], sm2[:, t, :], ACT.Exp, bias=ntop[1][:, t:t + 1],
                                                  scale=SCALE, accum_out=total[1][:, t:t + 1]))
                if s == "a_s1":
                    need(act, "nmax1", it)
                    for t in range(QT):
                        o, w = q_seg[t], P * (t + 1)
                        done("p1", act.activation(sm1[:, o:o + w], sm1[:, o:o + w], ACT.Exp,
                                                  bias=ntop[0][:, t:t + 1], scale=SCALE,
                                                  accum_out=total[0][:, t:t + 1]))
                if s == "c_x4T":
                    before(act, "logits_p", it)
                    for c in range(DC):
                        need(act, "x4T_p", it, c)
                        done("x4T", act.activation(x4T[:, c, :], bank_of("T", s, c, at)[:], ACT.Copy))
                if s == "c_rank":
                    need(act, "gap", it)
                    done("gate", act.activation(egap[:], gap[:], ACT.Exp))

            walk(act, step)

        @block.vector
        def _(dve):
            credit(dve, names[70:])
            for i, n in enumerate(("wq1", "wk1", "wq2", "wk2")):
                dve.wait_ge(wT_p, i + 1)
                dve.tensor_copy(wT[n], pool_t[i % 2][:].rearrange("p (c d) -> p c d", c=DC)).then_inc(wT_v, 1)
            dve.wait_ge(wT_p, 5)
            dve.tensor_copy(b1T[:], pool_m[0][:, 0:E * FC + DC]).then_inc(wT_v, 1)
            for n, p in (("wv1", wv1_p), ("wv2", wv2_p), ("fc1", fc1_p), ("fc2", fc2_p)):
                ins = dve.tensor_copy(p[0][:], raw_w[n])
            ins.then_inc(const_v, 1)
            dve.wait_ge(const_v, 1)
            for n, p in (("wv1", wv1_p), ("wv2", wv2_p), ("fc1", fc1_p), ("fc2", fc2_p)):
                ins = dve.tensor_tensor(p[1][:], raw_w[n], p[0][:], ALU.subtract)
            ins.then_inc(const_v, 1)
            for i, p in enumerate((a1, a2)):
                dve.wait_ge(a_p, i + 1)
                src = pool_s[i][:, 0:DC * D].rearrange("p (c d) -> p c d", c=DC)
                dve.tensor_copy(p[0][:], src).then_inc(const_v, 1)
                dve.wait_ge(const_v, 3 + i)
                dve.tensor_tensor(p[1][:], src, p[0][:], ALU.subtract).then_inc(a_v, 1)
            dve.wait_ge(const_p, 17 + 2 * QT)

            def norm_stats(n, it, src, width):
                for t in range(QT):
                    done(f"bn{n}", dve.bn_stats(stat[n][:, t, :], src[:, t, 0:width]))
                need(dve, f"bn{n}", it)
                settle(dve)
                for t in range(QT):
                    ins = dve.bn_aggr(mv[n][:, t, :], stat[n][:, t, :])
                done(f"mv{n}", ins)

            def normalise(n, it, src, dst, ready):
                need(dve, f"rstd{n}", it)
                for t in range(QT):
                    ins = dve.tensor_scalar(dst[:, t, 0:D], src[:, t, :], mv[n][:, t, 0:1], rstd[n][:, t:t + 1],
                                            ALU.subtract, ALU.mult)
                done(ready, ins)

            def count(n, tiles, s, at, it, width, key, mask):
                e, nz, lp, ln, mk = ("e1_p", "nz1", "len1_p", "len1", "mask1") if n == 0 else \
                    ("e2_p", "nz2", "len2_p", "len2", "mask2")
                need(dve, e, it)
                ins = dve.tensor_scalar(nz_k[n][:], bank_of("M", s, 0, at)[:, 0:tiles], 0.0, None, ALU.not_equal)
                done(nz, ins)
                need(dve, lp, it)
                ins = dve.tensor_reduce(length[n][:], bank_of("M", s, 1, at)[:, 0:tiles], AX.X, ALU.add)
                done(ln, ins)
                need(dve, ln, it)
                done(mk, dve.tensor_scalar(mask[:], key[:], length[n][:], MASKED, ALU.is_ge, ALU.mult))

            def invert(n, it, last_total):
                name = f"inv{n + 1}"
                need(dve, last_total, it)
                done(name, dve.tensor_scalar(some[n][:], length[n][:], 1.0, None, ALU.min))
                need(dve, name, it, 0)
                done(name, dve.tensor_scalar(full[n][:], total[n][:], some[n][:], None, ALU.mult))
                need(dve, name, it, 1)
                done(name, dve.reciprocal(inv[n][:], full[n][:]))
                need(dve, name, it, 2)

            def step(s, it, at):
                if s in EVACUATE:
                    pool, _, t, high, low, _ = EVACUATE[s]
                    for k in range(FILLS[pool][s]):
                        need(dve, high, it, k)
                        dst, w = where(s, k, t[1])
                        hi, _ = where(s, k, t[0])
                        ins = dve.tensor_tensor(dst, bank_of(pool, s, k, at)[:, 0:w], hi, ALU.subtract)
                        done(low, ins)
                if s == "a_ln0":
                    need(dve, "x_in", it)
                    norm_stats(0, it, x_sb, D)
                    before(dve, "y1", it)
                    before(dve, "xn_l", it)
                    normalise(0, it, x_sb, xn, "xn")
                if s == "c_fc1":
                    for c in range(DC):
                        need(dve, "fh", it, c)
                        done("fh_h", dve.tensor_copy(fh_p[0][:, c, :], fh[:, c, :]))
                if s == "b_len":
                    count(1, KT, s, at, it, SK, key2, mask2)
                if s == "a_len":
                    count(0, QT, s, at, it, SELF_W, key1, mask1)
                if s in ("b_s2a", "b_s2b"):
                    b0 = 0 if s == "b_s2a" else 2
                    if b0 == 0:
                        need(dve, "mask2", it)
                        before(dve, "p2T_p", it)
                    for n in range(2):
                        t = b0 + n
                        need(dve, "s2_p", it, t)
                        settle(dve)
                        ins = dve.tensor_tensor_reduce(sm2[:, t, :], bank_of("S", s, n, at)[:], mask2[:], 1.0,
                                                       -3.4e38, ALU.add, ALU.max, top[1][:, t:t + 1])
                        done("sm2", ins)
                    need(dve, "sm2", it, b0 + 1)
                    done("nmax2", dve.tensor_scalar(ntop[1][:, b0:b0 + 2], top[1][:, b0:b0 + 2], -SCALE, None,
                                                    ALU.mult))
                if s == "a_s1":
                    need(dve, "mask1", it)
                    for t in range(QT):
                        if t in (0, 3):
                            need(dve, "s1_p", it, t // 3)
                            settle(dve)
                        bank = bank_of("S", s, t // 3, at)
                        w = P * (t + 1)
                        o = q_seg[t] + (P if t == 2 else 0) - (q_seg[3] if t == 3 else 0)
                        done("sm1", dve.tensor_tensor_reduce(
                            sm1[:, q_seg[t]:q_seg[t] + w], bank[:, o:o + w], mask1[:, q_seg[t]:q_seg[t] + w], 1.0,
                            -3.4e38, ALU.add, ALU.max, top[0][:, t:t + 1]))
                    need(dve, "sm1", it)
                    done("nmax1", dve.tensor_scalar(ntop[0][:], top[0][:], -SCALE, None, ALU.mult))
                if s == "c_fc2":
                    need(dve, "x3b", it)
                    before(dve, "x4_out", it)
                    for h in range(2):
                        need(dve, "fc2_p", it, h)
                        src = bank_of("M", s, h, at)[:].rearrange("p (t d) -> p t d", t=2)
                        ins = dve.tensor_tensor(x4[:, 2 * h:2 * h + 2, :], src, x3b[:, 2 * h:2 * h + 2, :], ALU.add)
                        done("y3", ins)
                if s == "c_ln3":
                    need(dve, "y3", it)
                    norm_stats(3, it, x4, D)
                    normalise(3, it, x4, x4, "yn3")
                    need(dve, "yb3", it)
                    need(dve, "xr_in", it)
                    done("x4", dve.tensor_tensor(x4[:], x4[:], xr[:], ALU.add))
                    need(dve, "x4", it)
                    norm_stats(4, it, x4, D)
                    before(dve, "rows_gone", it)
                    normalise(4, it, x4, rows, "rowx")
                if s in ("b_z2", "a_z1"):
                    n, z, y, res, dst = (1, "z2_p", "y2", x2, x3) if s == "b_z2" else (0, "z1_p", "y1", xn, y1)
                    invert(n, it, "p2" if n else "p1")
                    if n:
                        before(dve, "x3T_p", Iteration(it.j, it.offset))
                        before(dve, "x3b", Iteration(it.j, it.offset))
                    for t in range(QT):
                        if t % 2 == 0:
                            need(dve, z, it, t // 2)
                        o = (t % 2) * D
                        ins = dve.scalar_tensor_tensor(dst[:, t, :], bank_of("M", s, t // 2, at)[:, o:o + D],
                                                       inv[n][:, t:t + 1], res[:, t, :], ALU.mult, ALU.add)
                        done(y, ins)
                if s == "b_ln2":
                    need(dve, "y2", it)
                    norm_stats(2, it, x3, D)
                    normalise(2, it, x3, x3, "yn2")
                if s == "a_ln1":
                    need(dve, "y1", it)
                    norm_stats(1, it, y1, D)
                    normalise(1, it, y1, y1, "yn1")
                r = [0]

                def link(ins):
                    done("route", ins)
                    need(dve, "route", it, r[0])
                    r[0] += 1

                if s == "c_logits":
                    need(dve, "logits_p", it)
                    ins = dve.tensor_copy(lg[:], bank_of("M", s, 0, at)[:, 0:QT * E].rearrange(
                        "p (t e) -> p t e", t=QT))
                    done("logits", ins)
                    need(dve, "logits", it)
                    settle(dve)
                    for t in range(QT):
                        ins = dve.max(best[:, t, :], lg[:, t, :])
                    link(ins)
                    settle(dve)
                    for t in range(QT):
                        ins = dve.max_index(besti[:, t, :], best[:, t, :], lg[:, t, :])
                    link(ins)
                    link(dve.tensor_copy(pick[:], besti[:, :, 0:2]))
                    before(dve, "rank_p", it)
                    for k in range(2):
                        ins = dve.tensor_tensor(hot[:, :, k, :], iota_e[:].unsqueeze(1).to_broadcast([P, QT, E]),
                                                pick[:, :, k:k + 1].to_broadcast([P, QT, E]), ALU.is_equal)
                    link(ins)
                    done("gap", dve.tensor_tensor(gap[:], best[:, :, 1], best[:, :, 0], ALU.subtract))
                    link(dve.tensor_reduce(newly[:], hot[:].rearrange("p t k e -> p (k e) t"), AX.X, ALU.add))
                    link(dve.tensor_copy(rows[:, :, TOKEN].bitcast(I32), token[:]))
                if s == "c_rank":
                    need(dve, "rank_p", it)
                    r[0] = 6
                    bank = bank_of("M", s, 0, at)
                    link(dve.tensor_tensor(rsel[:], bank[:, 0:QT * 2 * E].rearrange(
                        "p (t k e) -> p t k e", t=QT, k=2), hot[:], ALU.mult))
                    ins = dve.tensor_reduce(rank[:], rsel[:], AX.X, ALU.add)
                    ins = dve.tensor_tensor(taken[:], taken[:], newly[:], ALU.add)
                    ins = dve.tensor_scalar(token[:], token[:], float(S), None, ALU.add)
                    link(ins)
                if s == "c_slots":
                    r[0] = 8
                    need(dve, "gate", it)
                    ins = dve.tensor_scalar(den[:], egap[:], 1.0, None, ALU.add)
                    dve.tensor_scalar(keep[:], rank[:], float(CAP), None, ALU.is_le)
                    dve.tensor_scalar(over[:], rank[:], float(CAP), SKIP, ALU.is_gt, ALU.mult)
                    link(dve.scalar_tensor_tensor(slotf[:], pick[:], float(SLOTS), rank[:], ALU.mult, ALU.add))
                    dve.reciprocal(gate[:, :, 0], den[:])
                    link(dve.tensor_tensor(slotf[:], slotf[:], slot_off[:], ALU.add))
                    dve.tensor_tensor(gate[:, :, 1], gate[:, :, 0], egap[:], ALU.mult)
                    link(dve.tensor_tensor(slotf[:], slotf[:], over[:], ALU.add))
                    link(dve.scalar_tensor_tensor(rows[:, :, WEIGHT:WEIGHT + 2], gate[:], tanh_g[:, 1:2], keep[:],
                                                  ALU.mult, ALU.mult))
                    done("slots", dve.tensor_scalar(slot[:], slotf[:].rearrange("p t k -> p (t k)"), 0.0, 2 * SKIP,
                                                    ALU.max, ALU.min))

            walk(dve, step)


def experts(nc, g):
    (w1, w2, b2, out, xs, ident, b1T, w_in, w1_raw, w2_raw) = (g[n] for n in (
        "w1", "w2", "b2", "out", "xs", "ident", "b1T", "w_in", "w1_raw", "w2_raw"))
    D, E, F, DC, FC, T, SLOTS, ROW, TOKEN, WEIGHT, CAP, W_IN = (g[n] for n in (
        "D", "E", "F", "DC", "FC", "T", "SLOTS", "ROW", "TOKEN", "WEIGHT", "CAP", "W_IN"))
    CH = 2 * P
    NCH = SLOTS // CH
    PAIR = 2 * NCH
    HF = FC // 2
    assert SLOTS % CH == 0 and E % 2 == 0

    with ExitStack() as ctx:
        def sb(name, shape, dt=F32):
            return ctx.enter_context(nc.sbuf_tensor(name, shape, dt))

        def psum(name, shape):
            return ctx.enter_context(nc.psum_tensor(name, shape, F32))

        def sem(name):
            return ctx.enter_context(nc.semaphore(name))

        w1_p = [[sb(f"w1_{n}{h}", [P, DC, F], F16) for h in "hl"] for n in range(2)]
        w2_p = [[sb(f"w2_{n}{h}", [P, FC, D], F16) for h in "hl"] for n in range(2)]
        b2_bc = [sb(f"b2_bc{n}", [P, D]) for n in range(2)]
        slot_x = [sb(f"slot_x{n}", [P, 2, ROW]) for n in range(2)]
        xT_p = [[sb(f"sxT_{n}{h}", [P, DC, CH], F16) for h in "hl"] for n in range(2)]
        hid = [sb(f"hid{n}", [P, 2, CH]) for n in range(2)]
        hid_p = [[sb(f"hid_{n}{h}", [P, FC, CH], F16) for h in "hl"] for n in range(2)]
        yb = [sb(f"yb{n}", [P, D]) for n in range(2)]
        ys = [sb(f"ys{n}", [P, D]) for n in range(2)]
        dest = [sb(f"dest{n}", [P, 1], I32) for n in range(2)]
        bias = [sb(f"bias{n}", [P, FC]) for n in range(2)]
        zero1 = sb("zero1", [P, 1], I32)
        bank_x = [psum(f"bank_x{n}", [P, DC, CH]) for n in range(2)]
        bank_h = [psum(f"bank_h{n}", [P, 2, CH]) for n in range(4)]
        bank_y = [psum(f"bank_y{n}", [P, 2, D]) for n in range(2)]

        N = {"w_h": 4, "w_l": 4, "b2_in0": 1, "b2_in1": 1, "slot_in0": NCH, "slot_in1": NCH, "xT_f": PAIR, "xT_h": PAIR, "xT_l": PAIR,
             "h_f": PAIR * HF, "gelu": PAIR * HF, "hid_h": PAIR * HF, "hid_l": PAIR * HF, "y_f": PAIR,
             "y_b": 2 * PAIR, "y_w": 2 * PAIR, "dest": 2 * PAIR, "added": 2 * PAIR, "bias": 2, "ys_free": 2 * PAIR}
        DMAS = ("b2_in0", "b2_in1", "slot_in0", "slot_in1", "added")
        ev = {n: sem("e_" + n) for n in N}
        zeroed = sem("zeroed")

        def unit(n):
            return 16 if n in DMAS else 1

        def done(n, ins):
            ins.then_inc(ev[n], unit(n))

        CREDIT = 64

        def upto(eng, n, j, k):
            eng.wait_ge(ev[n], j * (N[n] * unit(n)) + (CREDIT + k * unit(n)))

        def credit(eng, names):
            for n in names:
                if n != "added":
                    eng.sem_inc(ev[n], CREDIT)

        names = list(N)
        block = ctx.enter_context(nc.Block())

        @block.sync
        def _(sp):
            credit(sp, names[0:4])

            xs_v = xs.rearrange("(n t p) d -> n p t d", p=P, t=2)

            def two_experts(j, last):
                for h in range(2):
                    upto(sp, "y_b", j, 2 * NCH * (h - 1))
                    done(f"b2_in{h}", sp.dma_start(b2_bc[h][:], b2[j * 2 + h].partition_broadcast(P)))
                    for c in range(NCH):
                        n = h * NCH + c
                        upto(sp, "y_w", j, 2 * n - 2)
                        upto(sp, "dest", j, 2 * n - 2)
                        done(f"slot_in{n % 2}", sp.dma_start(slot_x[n % 2][:], xs_v[j * PAIR + n]))
                        if c == 1 and not (last and h == 1):
                            upto(sp, "w_l", j, 2 * h + 2)
                            g["load_expert"](sp, j * 2 + (h + 1))

            with sp.Fori(0, E // 2 - 1) as j:
                two_experts(j, False)
            two_experts(E // 2 - 1, True)

        @block.gpsimd
        def _(pool):
            credit(pool, names[4:8])
            pool.memset(zero1[:], 0).then_inc(zeroed, 1)
            pool.wait_ge(zeroed, 1)
            def split_low(j, h):
                upto(pool, "w_h", j, 2 * h + 1)
                upto(pool, "y_f", j, NCH * (h - 1))
                done("w_l", pool.tensor_tensor(w1_p[h % 2][1][:], w1_raw, w1_p[h % 2][0][:], ALU.subtract))
                upto(pool, "w_h", j, 2 * h + 2)
                done("w_l", pool.tensor_tensor(w2_p[h % 2][1][:], w2_raw, w2_p[h % 2][0][:], ALU.subtract))

            def two_experts(j, last):
                for n in range(PAIR):
                    for t in range(2):
                        k = 2 * n + t
                        upto(pool, f"slot_in{n % 2}", j, n // 2 + 1)
                        upto(pool, "y_w", j, k + 1)
                        done("dest", pool.tensor_tensor(
                            dest[t][:], slot_x[n % 2][:, t, TOKEN:TOKEN + 1].bitcast(I32), zero1[:], ALU.add))
                        upto(pool, "dest", j, k + 1)
                        pool.sem_inc(zeroed, 1)
                        done("added", pool.indirect_dma_start(
                            out, bass.IndirectOffsetOnAxis(ap=dest[t][:].bitcast(U32), axis=0), ys[t][:], None,
                            compute_op=ALU.add, oob_is_err=True))
                        if n % NCH == 2 and t == 0 and not (last and n > NCH):
                            split_low(j, n // NCH + 1)
                        pool.wait_ge(ev["added"], j * (16 * 2 * PAIR) + 16 * (k + 1))
                        pool.sem_inc(ev["ys_free"], 1)

            split_low(0, 0)
            with pool.Fori(0, E // 2 - 1) as j:
                two_experts(j, False)
            two_experts(E // 2 - 1, True)

        @block.tensor
        def _(pe):
            credit(pe, names[8:12])

            def turn(j, n):
                upto(pe, f"slot_in{n % 2}", j, n // 2 + 1)
                upto(pe, "xT_l", j, n - 1)
                for d in range(DC):
                    for t in range(2):
                        m = pe.transpose(bank_x[n % 2][:, d, t * P:(t + 1) * P],
                                         slot_x[n % 2][:, t, d * P:(d + 1) * P], ident[:])
                done("xT_f", m)

            with pe.Fori(0, E // 2) as j:
                for n in range(PAIR):
                    h = n // NCH
                    turn(j, n)
                    if n % NCH == 0:
                        upto(pe, "w_l", j, 2 * h + 2)
                    upto(pe, "xT_l", j, n + 1)
                    for b in range(HF):
                        k = n * HF + b
                        upto(pe, "hid_l", j, k - 3)
                        bank = bank_h[k % 4]
                        for f2 in range(2):
                            f = 2 * b + f2
                            for d in range(DC):
                                fs = slice(f * P, (f + 1) * P)
                                m = mm3(pe, bank[:, f2, :], (w1_p[h][0][:, d, fs], w1_p[h][1][:, d, fs]),
                                        (xT_p[n % 2][0][:, d, :], xT_p[n % 2][1][:, d, :]), d == 0, d == DC - 1)
                        done("h_f", m)
                    upto(pe, "y_b", j, 2 * n - 2)
                    for t in range(2):
                        for f in range(FC):
                            if t == 0 and f % 2 == 0:
                                upto(pe, "hid_l", j, n * HF + f // 2 + 1)
                            ts = slice(t * P, (t + 1) * P)
                            m = mm3(pe, bank_y[n % 2][:, t, :],
                                    (hid_p[n % 2][0][:, f, ts], hid_p[n % 2][1][:, f, ts]),
                                    (w2_p[h][0][:, f, :], w2_p[h][1][:, f, :]), f == 0, f == FC - 1)
                    done("y_f", m)

        @block.scalar
        def _(act):
            credit(act, names[12:14])

            def split_high(j, h):
                act.wait_ge(w_in, j * (2 * W_IN) + W_IN * (h + 1))
                upto(act, "y_f", j, NCH * (h - 1))
                done("w_h", act.activation(w1_p[h % 2][0][:], w1_raw, ACT.Copy))
                done("w_h", act.activation(w2_p[h % 2][0][:], w2_raw, ACT.Copy))
                done("bias", act.activation(bias[h % 2][:], b1T[:, bass.ds((j * 2 + h) * FC, FC)], ACT.Copy))

            def two_experts(j, last):
                for n in range(PAIR):
                    h = n // NCH
                    if n % NCH == 0:
                        upto(act, "bias", j, h + 1)
                    upto(act, "xT_f", j, n + 1)
                    upto(act, "h_f", j, HF * (n - 1))
                    done("xT_h", act.activation(xT_p[n % 2][0][:], bank_x[n % 2][:], ACT.Copy))
                    for b in range(HF):
                        k = n * HF + b
                        upto(act, "h_f", j, k + 1)
                        upto(act, "hid_l", j, k - 1)
                        for f2 in range(2):
                            f = 2 * b + f2
                            m = act.activation(hid[b % 2][:, f2, :], bank_h[k % 4][:, f2, :], ACT.Gelu,
                                               bias=bias[h][:, f:f + 1])
                        done("gelu", m)
                    if n % NCH == 2 and not (last and h == 1):
                        split_high(j, h + 1)

            split_high(0, 0)
            with act.Fori(0, E // 2 - 1) as j:
                two_experts(j, False)
            two_experts(E // 2 - 1, True)

        @block.vector
        def _(dve):
            credit(dve, names[14:])
            with dve.Fori(0, E // 2) as j:
                for n in range(PAIR):
                    h = n // NCH
                    upto(dve, "xT_h", j, n + 1)
                    done("xT_l", dve.tensor_tensor(xT_p[n % 2][1][:], bank_x[n % 2][:], xT_p[n % 2][0][:],
                                                   ALU.subtract))
                    for b in range(HF):
                        k = n * HF + b
                        upto(dve, "gelu", j, k + 1)
                        if b == 0:
                            upto(dve, "y_f", j, n - 1)
                        fs = slice(2 * b, 2 * b + 2)
                        done("hid_h", dve.tensor_copy(hid_p[n % 2][0][:, fs, :], hid[b % 2][:]))
                        upto(dve, "hid_h", j, k + 1)
                        done("hid_l", dve.tensor_tensor(hid_p[n % 2][1][:, fs, :], hid[b % 2][:],
                                                        hid_p[n % 2][0][:, fs, :], ALU.subtract))
                    upto(dve, "y_f", j, n + 1)
                    if n % NCH == 0:
                        upto(dve, f"b2_in{h}", j, 1)
                    for t in range(2):
                        k = 2 * n + t
                        done("y_b", dve.tensor_tensor(yb[t][:], bank_y[n % 2][:, t, :], b2_bc[h][:], ALU.add))
                        upto(dve, "y_b", j, k + 1)
                        upto(dve, "ys_free", j, k - 1)
                        choice = (n % NCH * 2 + t) // (CAP // P)
                        done("y_w", dve.tensor_scalar(ys[t][:], yb[t][:],
                                                      slot_x[n % 2][:, t, WEIGHT + choice:WEIGHT + choice + 1], None,
                                                      ALU.mult))


_INS = ['x', 'ctx_1024', 'g_xattn', 'g_ffn', 'L0_xattn_Wq1', 'L0_xattn_Wk1', 'L0_xattn_Wv1', 'L0_xattn_Wq2',
        'L0_xattn_Wk2', 'L0_xattn_Wv2', 'L0_xattn_fc1_w', 'L0_xattn_fc1_b', 'L0_xattn_fc2_w', 'L0_xattn_fc2_b',
        'L0_xattn_ln1_g', 'L0_xattn_ln1_b', 'L0_xattn_ln2_g', 'L0_xattn_ln2_b', 'L0_xattn_ln3_g', 'L0_xattn_ln3_b',
        'L0_ffn_Wr', 'L0_ffn_W1', 'L0_ffn_b1', 'L0_ffn_W2', 'L0_ffn_b2']


def kernel(**inputs):
    import numpy as _np
    import concourse.bacc as _bacc
    from concourse import mybir as _mybir
    from concourse.bass_utils import run_bass_kernel_spmd as _run

    nc = _bacc.Bacc("TRN2", target_bir_lowering=False, num_devices=1)
    arrays, args = {}, []
    for name in _INS:
        a = _np.ascontiguousarray(inputs[name])
        arrays[f"in_{name}_dram"] = a
        args.append(nc.dram_tensor(f"in_{name}_dram", a.shape, _mybir.dt.from_np(a.dtype), kind="ExternalInput").ap())
    b, s, d = inputs["x"].shape
    tokens, experts_ = b * s, inputs["L0_ffn_Wr"].shape[1]
    out = nc.dram_tensor("out_0_dram", (tokens + 128, d), _mybir.dt.float32, kind="ExternalOutput").ap()
    slots = experts_ * 2 * int(tokens * 1.25 / experts_)
    xs = nc.dram_tensor("slot_rows", (slots, d + 4), _mybir.dt.float32, kind="Internal").ap()
    flamingo_moe_kernel(nc, *args, out, xs)
    r = _run(nc, [arrays], core_ids=[0])
    return r.results[0]["out_0_dram"][:tokens].reshape(b, s, d)
```

```python
from contextlib import ExitStack

import concourse.bass as bass
from concourse import mybir

F32 = mybir.dt.float32
F16 = mybir.dt.float16
I32 = mybir.dt.int32
U32 = mybir.dt.uint32
ALU = mybir.AluOpType
ACT = mybir.ActivationFunctionType
AX = mybir.AxisListType

P = 128
EPS = 1e-5
MASKED = -3.0e38
NEVER = 1.0e9
SKIP = 30000.0

ORDER = [
    ("b_s2a", 2), ("z_ln0", 0), ("c_fc1", 3), ("b_s2b", 2), ("c_fc2", 3), ("a_c1T", 1), ("b_p2T", 2),
    ("c_n3", 3), ("a_z1", 1), ("c_x4", 3), ("z_n0", 0), ("b_c2T0", 2), ("b_c2T1", 2), ("a_xnT", 0),
    ("c_n4", 3), ("a_n1", 1), ("b_z2", 2), ("c_x4T", 3), ("a_q1T", 0), ("b_ctx", 1), ("a_len", 0),
    ("c_logits", 3), ("a_x2T", 1), ("b_n2", 2), ("d_send", 3), ("a_s1", 0), ("c_rank", 3), ("c_slots", 3),
    ("b_q2T", 1), ("a_p1T", 0), ("b_len", 1), ("c_x3T", 2),
]
LAG = dict(ORDER)
DEPTH = max(LAG.values())
START = DEPTH + 1

FILLS = {
    "T": {"b_ctx": 4, "c_x3T": 2, "a_xnT": 2, "b_p2T": 8, "c_x4T": 2, "a_p1T": 4, "a_x2T": 2},
    "M": {"b_q2T": 2, "c_fc1": 2, "b_len": 2, "c_fc2": 2, "a_q1T": 2, "a_len": 2, "b_c2T0": 1, "b_c2T1": 1,
          "c_logits": 1, "a_c1T": 2, "c_rank": 1, "b_z2": 2, "a_z1": 2},
    "S": {"b_s2a": 2, "b_s2b": 2, "a_s1": 2},
}

EMPTIED = {
    "b_ctx": ("ctxT_l", range(4)), "c_x3T": ("x3T_l", range(2)), "a_xnT": ("xnT_l", range(2)),
    "b_p2T": ("p2T_l", range(8)), "c_x4T": ("x4T", range(2)), "a_p1T": ("p1T_l", range(4)),
    "a_x2T": ("x2T_l", range(2)), "b_q2T": ("q2T_l", range(2)), "c_fc1": ("fh", range(2)),
    "c_fc2": ("y3", range(2)), "a_q1T": ("q1T_l", range(2)), "b_c2T0": ("c2T_l", [0]),
    "b_c2T1": ("c2T_l", [1]),
    "c_logits": ("logits", [0]), "a_c1T": ("c1T_l", range(2)), "c_rank": ("route", [6]),
    "b_z2": ("y2", [1, 3]), "a_z1": ("y1", [1, 3]), "b_s2a": ("sm2", [0, 1]), "b_s2b": ("sm2", [2, 3]),
    "a_s1": ("sm1", [2, 3]), "b_len": (("nz2", "len2"), None), "a_len": (("nz1", "len1"), None),
}

SIGNALS = {
    "x_in": 1, "ctx_in": 1, "xr_in": 1, "x4_out": 1, "dispatched": 8,
    "bn0": 4, "mv0": 1, "ve0": 1, "rstd0": 1, "nm0": 1, "nb0": 1, "xn": 1, "xn_h": 1, "xn_l": 1,
    "xnT_p": 2, "xnT_h": 2, "xnT_l": 2, "q1T_p": 2, "q1T_h": 2, "q1T_l": 2,
    "e1_p": 1, "nz1": 1, "len1_p": 1, "len1": 1, "mask1": 1, "inv1": 3,
    "s1_p": 2, "sm1": 4, "nmax1": 1, "p1": 4, "p1T_p": 4, "p1T_h": 4, "p1T_l": 4,
    "c1T_p": 2, "c1T_h": 2, "c1T_l": 2, "z1_p": 2, "y1": 4,
    "bn1": 4, "mv1": 1, "ve1": 1, "rstd1": 1, "nm1": 1, "nb1": 1, "yn1": 1, "yg1": 1, "x2": 1,
    "x2T_p": 2, "x2T_h": 2, "x2T_l": 2,
    "ctx_h": 1, "ctx_l": 1, "ctxT_p": 4, "ctxT_h": 4, "ctxT_l": 4,
    "q2T_p": 2, "q2T_h": 2, "q2T_l": 2, "e2_p": 1, "nz2": 1, "len2_p": 1, "len2": 1, "mask2": 1,
    "inv2": 3, "s2_p": 4, "sm2": 4, "nmax2": 2, "p2": 4, "p2T_p": 8, "p2T_h": 8, "p2T_l": 8,
    "c2T_p": 2, "c2T_h": 2, "c2T_l": 2, "z2_p": 2, "y2": 4,
    "bn2": 4, "mv2": 1, "ve2": 1, "rstd2": 1, "nm2": 1, "nb2": 1, "yn2": 1, "yg2": 1, "x3": 1,
    "x3b": 1, "x3T_p": 2, "x3T_h": 2, "x3T_l": 2, "fc1_p": 2, "fh": 2, "fh_h": 2, "fh_l": 2,
    "fc2_p": 2, "y3": 2, "bn3": 4, "mv3": 1, "ve3": 1, "rstd3": 1, "nm3": 1, "nb3": 1, "yn3": 1, "yg3": 1, "xro": 1, "x4": 1,
    "bn4": 4, "mv4": 1, "ve4": 1, "rstd4": 1, "nm4": 1, "nb4": 1, "rowx": 1, "x4T_p": 2, "x4T": 2,
    "logits_p": 1, "logits": 1, "route": 12, "gap": 1, "gate": 1, "rank_p": 1, "slots": 1, "rows_gone": 1,
}


class Iteration:

    def __init__(self, j, offset):
        self.j, self.offset = j, offset

    def times(self, n, plus):
        at = n * self.offset + plus
        return at if self.j is None else self.j * n + at


def flamingo_moe_kernel(nc, x, ctx_in, g_x, g_f, wq1, wk1, wv1, wq2, wk2, wv2, fc1_w, fc1_b, fc2_w, fc2_b,
                        ln1_g, ln1_b, ln2_g, ln2_b, ln3_g, ln3_b, wr, w1, b1, w2, b2, out, xs):
    B, S, D = x.shape
    SK = ctx_in.shape[1]
    E, _, F = w1.shape
    DC, QT, KT = D // P, S // P, SK // P
    FC = F // P
    T = B * S
    CAP = int(T * 1.25 / E)
    SLOTS = 2 * CAP
    ROW = xs.shape[1]
    TOKEN, WEIGHT = D, D + 1
    SCALE = 1.0 / 4.0
    SELF_W = P * QT * (QT + 1) // 2
    assert D == 256 and S == 512 and SK == 1024 and E == 8 and CAP % P == 0 and B > START

    q_seg = [P * t * (t + 1) // 2 for t in range(QT)]
    k_seg = [P * (t * QT - t * (t - 1) // 2) for t in range(QT)]

    ctx = ExitStack()
    with ctx:
        def sb(name, shape, dt=F32):
            return ctx.enter_context(nc.sbuf_tensor(name, shape, dt))

        def sem(name):
            return ctx.enter_context(nc.semaphore(name))

        ident = sb("ident", [P, P])
        b1T = sb("b1T", [P, E * FC + DC])
        tanh_g = sb("tanh_g", [P, 2])
        w_raw = sb("w_raw", [P, DC * F + FC * D])

        w1_raw = w_raw[:, 0:DC * F].rearrange("p (c f) -> p c f", c=DC)
        w2_raw = w_raw[:, DC * F:].rearrange("p (c d) -> p c d", c=FC)
        w_in = sem("w_in")
        W_IN = 32

        def load_expert(eng, e):
            eng.dma_start(w1_raw, w1[e].rearrange("(c p) f -> p c f", p=P)).then_inc(w_in, 16)
            eng.dma_start(w2_raw, w2[e].rearrange("(c p) d -> p c d", p=P)).then_inc(w_in, 16)

        attention(nc, locals())
        experts(nc, locals())


def mm3(pe, out, left, right, first=True, last=True):
    (lh, ll), (rh, rl) = left, right
    pe.matmul(out, lh, rh, start=first, stop=False)
    pe.matmul(out, lh, rl, start=False, stop=False)
    return pe.matmul(out, ll, rh, start=False, stop=last)


def attention(nc, g):
    (x, ctx_in, g_x, g_f, wq1, wk1, wv1, wq2, wk2, wv2, fc1_w, fc1_b, fc2_w, fc2_b, ln1_g, ln1_b, ln2_g, ln2_b,
     ln3_g, ln3_b, wr, b1, out, xs) = (g[n] for n in (
         "x", "ctx_in", "g_x", "g_f", "wq1", "wk1", "wv1", "wq2", "wk2", "wv2", "fc1_w", "fc1_b", "fc2_w", "fc2_b",
         "ln1_g", "ln1_b", "ln2_g", "ln2_b", "ln3_g", "ln3_b", "wr", "b1", "out", "xs"))
    B, S, D, SK, E, F, DC, QT, KT, FC, T, CAP, SLOTS, ROW, TOKEN, WEIGHT, SCALE, SELF_W = (g[n] for n in (
        "B", "S", "D", "SK", "E", "F", "DC", "QT", "KT", "FC", "T", "CAP", "SLOTS", "ROW", "TOKEN", "WEIGHT",
        "SCALE", "SELF_W"))
    q_seg, k_seg, ident, b1T, tanh_g = (g[n] for n in ("q_seg", "k_seg", "ident", "b1T", "tanh_g"))

    with ExitStack() as ctx:
        def sb(name, shape, dt=F32):
            return ctx.enter_context(nc.sbuf_tensor(name, shape, dt))

        def pair(name, shape):
            return sb(name + "_h", shape, F16), sb(name + "_l", shape, F16)

        def psum(name, shape):
            return ctx.enter_context(nc.psum_tensor(name, shape, F32))

        def sem(name):
            return ctx.enter_context(nc.semaphore(name))

        tri = sb("tri", [P, P], F16)
        ones = sb("ones", [P, P], F16)
        key1 = sb("key1", [P, SELF_W])
        key2 = sb("key2", [P, SK])
        iota_e = sb("iota_e", [P, E])
        slot_off = sb("slot_off", [P, QT, 2])
        neg_half = sb("neg_half", [P, QT])
        eps = sb("eps", [P, QT])
        neg_one = sb("neg_one", [P, QT])
        token = sb("token", [P, QT])
        taken = sb("taken", [P, 2 * E], F16)
        vec = {n: sb(n + "_bc", [P, D]) for n in ("g1", "o1", "g2", "o2", "g3", "o3", "fc2_b")}
        wr_sb = sb("wr_sb", [P, DC, E])
        a1 = pair("a1", [P, DC, D])
        a2 = pair("a2", [P, DC, D])
        wv1_p, wv2_p = pair("wv1", [P, DC, D]), pair("wv2", [P, DC, D])
        fc1_p, fc2_p = pair("fc1", [P, DC, D]), pair("fc2", [P, DC, D])
        b1_raw = sb("b1_raw", [E * FC + DC, P])
        gates_in = sb("gates_in", [P, 2])

        x_sb = sb("x_sb", [P, QT, D])
        xn = sb("xn", [P, QT, D])
        xn_p = pair("xn", [P, QT, D])
        xnT = pair("xnT", [P, DC, S])
        q1T = pair("q1T", [P, DC, S])
        mask1 = sb("mask1", [P, SELF_W])
        sm1 = sb("sm1", [P, SELF_W])
        p1T = pair("p1T", [P, SELF_W])
        c1T = pair("c1T", [P, DC, S])
        y1 = sb("y1", [P, QT, D])
        x2 = sb("x2", [P, QT, D])
        x2T = pair("x2T", [P, DC, S])
        c_sb = sb("c_sb", [P, KT, D])
        c_p = pair("c", [P, KT, D])
        ctxT = pair("ctxT", [P, DC, SK])
        q2T = pair("q2T", [P, DC, S])
        mask2 = sb("mask2", [P, SK])
        sm2 = sb("sm2", [P, QT, SK])
        p2T = pair("p2T", [P, KT, S])
        c2T = pair("c2T", [P, DC, S])
        x3 = sb("x3", [P, QT, D])
        xr = sb("xr", [P, QT, D])
        x3b = sb("x3b", [P, QT, D])
        x3T = pair("x3T", [P, DC, S])
        fh = sb("fh", [P, DC, S])
        fh_p = pair("fh", [P, DC, S])
        x4 = sb("x4", [P, QT, D])
        x4T = sb("x4T", [P, DC, S])
        rows = sb("rows", [P, QT, ROW])
        stat = [sb(f"stat{n}", [P, QT, 6]) for n in range(5)]
        mv = [sb(f"mv{n}", [P, QT, 2]) for n in range(5)]
        ve = [sb(f"ve{n}", [P, QT]) for n in range(5)]
        nm = [sb(f"nm{n}", [P, QT]) for n in range(5)]
        nb = [sb(f"nb{n}", [P, QT]) for n in range(5)]
        rstd = [sb(f"rstd{n}", [P, QT]) for n in range(5)]
        nz_k = [sb("nz_k1", [P, QT], F16), sb("nz_k2", [P, KT], F16)]
        length = [sb(f"length{n}", [P, 1]) for n in range(2)]
        top = [sb(f"top{n}", [P, QT]) for n in range(2)]
        ntop = [sb(f"ntop{n}", [P, QT]) for n in range(2)]
        total = [sb(f"total{n}", [P, QT]) for n in range(2)]
        some = [sb(f"some{n}", [P, 1]) for n in range(2)]
        full = [sb(f"full{n}", [P, QT]) for n in range(2)]
        inv = [sb(f"inv{n}", [P, QT]) for n in range(2)]
        lg = sb("lg", [P, QT, E])
        best = sb("best", [P, QT, 8])
        besti = sb("besti", [P, QT, 8], U32)
        pick = sb("pick", [P, QT, 2])
        hot = sb("hot", [P, QT, 2, E], F16)
        rsel = sb("rsel", [P, QT, 2, E])
        rank = sb("rank", [P, QT, 2])
        gap = sb("gap", [P, QT])
        egap = sb("egap", [P, QT])
        den = sb("den", [P, QT])
        gate = sb("gate", [P, QT, 2])
        keep = sb("keep", [P, QT, 2])
        over = sb("over", [P, QT, 2])
        slotf = sb("slotf", [P, QT, 2])
        slot = sb("slot", [P, QT * 2], I32)
        newly = sb("newly", [P, 2 * E])

        raw_w = {n: sm2[:, i // 2, (i % 2) * DC * D:(i % 2 + 1) * DC * D].rearrange("p (c d) -> p c d", c=DC)
                 for i, n in enumerate(("wq1", "wk1", "wq2", "wk2", "wv1", "wv2", "fc1", "fc2"))}
        wT = {n: t[:, :, 0:D] for n, t in (("wq1", fh), ("wk1", x4T))}
        wT["wq2"], wT["wk2"] = fh[:, :, D:2 * D], x4T[:, :, D:2 * D]
        blank = rows[:, 0, :]

        pool_t = [psum(f"bank_t{n}", [P, 512]) for n in range(2)]
        pool_m = [psum(f"bank_m{n}", [P, 512]) for n in range(2)]
        pool_s = [psum(f"bank_s{n}", [P, 1024]) for n in range(2)]
        banks = {"T": pool_t, "M": pool_m, "S": pool_s}

        ev = {n: sem(n) for n in SIGNALS}
        setup_in, vec_in, const_p, const_v = sem("setup_in"), sem("vec_in"), sem("const_p"), sem("const_v")
        wT_p, wT_v, a_p, a_v, gates = sem("wT_p"), sem("wT_v"), sem("a_p"), sem("a_v"), sem("gates")
        blank_out, settled = sem("blank_out"), sem("settled")
        DMA_EVENTS = ("x_in", "ctx_in", "xr_in", "x4_out", "dispatched")

        def unit(name):
            return 16 if name in DMA_EVENTS else 1

        def done(name, ins):
            ins.then_inc(ev[name], unit(name))

        def need(eng, name, it, k=None):
            n, k = SIGNALS[name], SIGNALS[name] - 1 if k is None else k
            eng.wait_ge(ev[name], it.times(n * unit(name), 1 + (k + 1) * unit(name)))

        def before(eng, name, it):
            eng.wait_ge(ev[name], it.times(SIGNALS[name] * unit(name), 1))

        def live(i, step):
            return 0 <= i - LAG[step] < B

        def fills_in(pool, i):
            return [(s, k) for s in LAG if live(i, s) for k in range(FILLS[pool].get(s, 0))]

        def fill(pool, step, k, i):
            index = fills_in(pool, i).index((step, k))
            assert len(fills_in(pool, i)) % 2 == 0
            return index

        def bank_of(pool, step, k, at):
            return banks[pool][fill(pool, step, k, at[0]) % 2]

        def open_fill(pe, pool, step, k, at):
            i, j = at
            index = fill(pool, step, k, i)
            if index >= 2:
                was, back = fills_in(pool, i)[index - 2], 0
            else:
                back = next((n for n in range(1, i + 1) if fills_in(pool, i - n)), None)
                if back is None:
                    return banks[pool][index % 2]
                was = fills_in(pool, i - back)[index - 2]
                assert j is None or (back == 1 and was == fills_in(pool, i)[index - 2])
            event, numbers = EMPTIED[was[0]]
            if was[0] == "b_len" or was[0] == "a_len":
                event, number = event[was[1]], 0
            else:
                number = numbers[was[1]]
            need(pe, event, Iteration(j, i - back - LAG[was[0]]), number)
            return banks[pool][index % 2]

        def walk(eng, body):
            def one(i, j):
                for s in LAG:
                    if live(i, s):
                        body(s, Iteration(j, i - LAG[s]), (i, j))
            for i in range(START):
                one(i, None)
            with eng.Fori(0, B - START) as j:
                one(START, j)
            for i in range(B, B + DEPTH):
                one(i, None)

        def credit(eng, names):
            for n in names:
                if n != "dispatched":
                    eng.sem_inc(ev[n], 1)

        def settle(eng):
            eng.sem_inc(settled, 1)

        def batch(dram, it):
            view = dram.rearrange("b (t p) d -> b p t d", p=P)
            return view[it.offset] if it.j is None else view[it.j + it.offset]

        def out_rows(it):
            view = out[0:T, :].rearrange("(b t p) d -> b p t d", p=P, t=QT)
            return view[it.offset] if it.j is None else view[it.j + it.offset]

        names = list(SIGNALS)
        block = ctx.enter_context(nc.Block())

        @block.sync
        def _(sp):
            for n in ("wq1", "wk1", "wq2", "wk2", "wv1", "wv2", "fc1", "fc2"):
                dram = {"wq1": wq1, "wk1": wk1, "wq2": wq2, "wk2": wk2, "wv1": wv1, "wv2": wv2, "fc1": fc1_w,
                        "fc2": fc2_w}[n]
                sp.dma_start(raw_w[n], dram.rearrange("(c p) d -> p c d", p=P)).then_inc(setup_in, 16)
            credit(sp, names[0:4])
            sp.dma_start(b1_raw[0:E * FC, :], b1.rearrange("e (c p) -> (e c) p", p=P)).then_inc(vec_in, 16)
            sp.dma_start(b1_raw[E * FC:, :], fc1_b.rearrange("(c p) -> c p", p=P)).then_inc(vec_in, 16)
            sp.dma_start(wr_sb[:], wr.rearrange("(c p) e -> p c e", p=P)).then_inc(vec_in, 16)
            for v, n in ((ln1_g, "g1"), (ln1_b, "o1"), (ln2_g, "g2"), (ln2_b, "o2"), (ln3_g, "g3"), (ln3_b, "o3"),
                         (fc2_b, "fc2_b")):
                sp.dma_start(vec[n][:], v.partition_broadcast(P)).then_inc(vec_in, 16)
            sp.dma_start(gates_in[:, 0:1], g_x.partition_broadcast(P)).then_inc(vec_in, 16)
            sp.dma_start(gates_in[:, 1:2], g_f.partition_broadcast(P)).then_inc(vec_in, 16)

            def step(s, it, at):
                if s == "z_ln0":
                    before(sp, "xn", it)
                    done("x_in", sp.dma_start(x_sb[:], batch(x, it)))
                if s == "b_ctx":
                    before(sp, "ctx_l", it)
                    before(sp, "ctxT_p", it)
                    done("ctx_in", sp.dma_start(c_sb[:], batch(ctx_in, it)))
                if s == "c_x3T":
                    before(sp, "x4", it)
                    done("xr_in", sp.dma_start(xr[:], batch(x, it)))
                if s == "c_x4":
                    need(sp, "x4", it)
                    done("x4_out", sp.dma_start(out_rows(it), x4[:]))

            walk(sp, step)
            sp.wait_ge(ev["x4_out"], 1 + 16 * B)
            g["load_expert"](sp, 0)

        @block.gpsimd
        def _(pool):
            credit(pool, names[4:20])
            pool.memset(ident[:], 0.0).then_inc(const_p, 1)
            pool.memset(tri[:], 1.0).then_inc(const_p, 1)
            pool.memset(ones[:], 1.0).then_inc(const_p, 1)
            pool.memset(neg_half[:], -0.5).then_inc(const_p, 1)
            pool.memset(eps[:], EPS).then_inc(const_p, 1)
            pool.memset(neg_one[:], -1.0).then_inc(const_p, 1)
            pool.memset(taken[:], 0.0).then_inc(const_p, 1)
            pool.memset(rows[:], 0.0).then_inc(const_p, 1)
            for t in range(QT):
                pool.iota(key1[:, q_seg[t]:q_seg[t] + P * (t + 1)], [[1, P * (t + 1)]], base=0, channel_multiplier=0,
                          allow_small_or_imprecise_dtypes=True).then_inc(const_p, 1)
            pool.iota(key2[:], [[1, SK]], base=0, channel_multiplier=0,
                      allow_small_or_imprecise_dtypes=True).then_inc(const_p, 1)
            pool.iota(iota_e[:], [[1, E]], base=0, channel_multiplier=0,
                      allow_small_or_imprecise_dtypes=True).then_inc(const_p, 1)
            pool.iota(slot_off[:], [[0, QT], [CAP, 2]], base=-1, channel_multiplier=0,
                      allow_small_or_imprecise_dtypes=True).then_inc(const_p, 1)
            pool.iota(token[:], [[P, QT]], base=0, channel_multiplier=1,
                      allow_small_or_imprecise_dtypes=True).then_inc(const_p, 1)
            pool.wait_ge(const_p, 12 + QT)
            pool.affine_select(out=ident[:], in_=ident[:], compare_op=ALU.not_equal, fill=1.0, base=0,
                               pattern=[[-1, P]], channel_multiplier=1).then_inc(const_p, 1)
            pool.affine_select(out=tri[:], in_=tri[:], compare_op=ALU.is_ge, fill=0.0, base=0,
                               pattern=[[1, P]], channel_multiplier=-1).then_inc(const_p, 1)
            for t in range(QT):
                d = key1[:, q_seg[t] + P * t:q_seg[t] + P * (t + 1)]
                pool.affine_select(out=d, in_=d, compare_op=ALU.is_ge, fill=NEVER, base=0, pattern=[[-1, P]],
                                   channel_multiplier=1).then_inc(const_p, 1)
            pool.iota(blank[:, TOKEN:TOKEN + 1].bitcast(I32), [[0, 1]], base=T, channel_multiplier=1).then_inc(const_p, 1)
            pool.wait_ge(const_p, 15 + 2 * QT)
            pool.dma_start(xs.rearrange("(c p) d -> p c d", p=P),
                           blank.unsqueeze(1).to_broadcast([P, E * SLOTS // P, ROW])).then_inc(blank_out, 16)
            pool.dma_start(out[T:T + P, :], blank[:, 0:D]).then_inc(blank_out, 16)
            pool.wait_ge(gates, 1)
            pool.wait_ge(vec_in, 16 * 12)
            for n in ("g3", "o3"):
                pool.tensor_scalar(vec[n][:], vec[n][:], tanh_g[:, 0:1], None, ALU.mult).then_inc(const_p, 1)
            pool.wait_ge(const_p, 17 + 2 * QT)

            def norm_rstd(n, it):
                need(pool, f"mv{n}", it)
                done(f"ve{n}", pool.tensor_tensor(ve[n][:], mv[n][:, :, 1], eps[:], ALU.add))
                done(f"nm{n}", pool.tensor_tensor(nm[n][:], mv[n][:, :, 0], neg_one[:], ALU.mult))
                need(pool, f"ve{n}", it)
                done(f"rstd{n}", pool.tensor_tensor(rstd[n][:], ve[n][:], neg_half[:], ALU.pow))
                need(pool, f"nm{n}", it)
                need(pool, f"rstd{n}", it)
                done(f"nb{n}", pool.tensor_tensor(nb[n][:], nm[n][:], rstd[n][:], ALU.mult))

            def affine(n, it, src, dst, scale, offset, scaled, ready):
                need(pool, f"yn{n}", it)
                sc = vec[scale][:].unsqueeze(1).to_broadcast([P, QT, D])
                of = vec[offset][:].unsqueeze(1).to_broadcast([P, QT, D])
                done(scaled, pool.tensor_tensor(src[:], src[:], sc, ALU.mult))
                need(pool, scaled, it)
                done(ready, pool.tensor_tensor(dst[:], src[:], of, ALU.add))

            def step(s, it, at):
                if s == "b_ctx":
                    need(pool, "ctx_in", it)
                    need(pool, "ctx_h", it)
                    before(pool, "c2T_p", it)
                    done("ctx_l", pool.tensor_tensor(c_p[1][:], c_sb[:], c_p[0][:], ALU.subtract))
                if s == "c_x3T":
                    need(pool, "x3", it)
                    before(pool, "y3", it)
                    fb = vec["fc2_b"][:].unsqueeze(1).to_broadcast([P, QT, D])
                    done("x3b", pool.tensor_tensor(x3b[:], x3[:], fb, ALU.add))
                if s == "z_ln0":
                    norm_rstd(0, it)
                if s == "z_n0":
                    need(pool, "xn_h", it)
                    before(pool, "c1T_p", it)
                    done("xn_l", pool.tensor_tensor(xn_p[1][:], xn[:], xn_p[0][:], ALU.subtract))
                if s == "c_fc1":
                    for c in range(DC):
                        need(pool, "fh_h", it, c)
                        if c == 0:
                            before(pool, "fc2_p", it)
                        done("fh_l", pool.tensor_tensor(fh_p[1][:, c, :], fh[:, c, :], fh_p[0][:, c, :],
                                                        ALU.subtract))
                    need(pool, "xr_in", it)
                    before(pool, "x4", it)
                    ob = vec["o3"][:].unsqueeze(1).to_broadcast([P, QT, D])
                    done("xro", pool.tensor_tensor(xr[:], xr[:], ob, ALU.add))
                if s == "c_fc2":
                    norm_rstd(3, it)
                if s == "c_n3":
                    need(pool, "yn3", it)
                    sc = vec["g3"][:].unsqueeze(1).to_broadcast([P, QT, D])
                    done("yg3", pool.tensor_tensor(x4[:], x4[:], sc, ALU.mult))
                if s == "c_x4":
                    norm_rstd(4, it)
                if s == "a_z1":
                    norm_rstd(1, it)
                if s == "a_n1":
                    before(pool, "y2", it)
                    affine(1, it, y1, x2, "g1", "o1", "yg1", "x2")
                if s == "b_z2":
                    norm_rstd(2, it)
                if s == "b_n2":
                    if it.j is None and it.offset == 0:
                        pool.wait_ge(blank_out, 32)
                    affine(2, it, x3, x3, "g2", "o2", "yg2", "x3")
                if s == "d_send":
                    need(pool, "slots", it)
                    need(pool, "rowx", it)
                    settle(pool)
                    for t in range(QT):
                        for k in range(2):
                            n = 2 * t + k
                            done("dispatched", pool.indirect_dma_start(
                                xs, bass.IndirectOffsetOnAxis(ap=slot[:, n:n + 1].bitcast(U32), axis=0),
                                rows[:, t, :], None, bounds_check=E * SLOTS - 1, oob_is_err=False))
                if s == "c_n4":
                    SENT = 16 * 2 * QT
                    if it.j is not None or it.offset > 0:
                        pool.wait_ge(ev["dispatched"], it.times(SENT, 0))
                    pool.sem_inc(ev["rows_gone"], 1)

            walk(pool, step)
            pool.wait_ge(ev["dispatched"], 16 * 2 * QT * B)

        @block.tensor
        def _(pe):
            credit(pe, names[20:40])
            pe.wait_ge(const_p, 13 + QT)
            pe.wait_ge(setup_in, 16 * 8)
            for i, n in enumerate(("wq1", "wk1", "wq2", "wk2")):
                if i >= 2:
                    pe.wait_ge(wT_v, i - 1)
                for eb in range(DC):
                    for db in range(DC):
                        m = pe.transpose(pool_t[i % 2][:, eb * D + db * P:eb * D + (db + 1) * P],
                                         raw_w[n][:, db, eb * P:(eb + 1) * P], ident[:])
                m.then_inc(wT_p, 1)
            pe.wait_ge(vec_in, 16 * 12)
            nb = E * FC + DC
            pe.transpose(pool_m[0][:, 0:nb], b1_raw[:], ident[0:nb, 0:nb]).then_inc(wT_p, 1)
            for i, (q, k) in enumerate((("wq1", "wk1"), ("wq2", "wk2"))):
                pe.wait_ge(wT_v, 2 * i + 2)
                for db in range(DC):
                    for eb in range(DC):
                        m = pe.matmul(pool_s[i][:, db * D:(db + 1) * D], wT[q][:, eb, db * P:(db + 1) * P],
                                      wT[k][:, eb, :], start=eb == 0, stop=eb == DC - 1)
                m.then_inc(a_p, 1)
            pe.wait_ge(a_v, 2)
            pe.wait_ge(wT_v, 5)
            pe.wait_ge(const_v, 2)

            def part(p, *i):
                return p[0][i], p[1][i]

            def turn(src, c, tiles, pool, step, k, at):
                bank = open_fill(pe, pool, step, k, at)
                for n, t in enumerate(tiles):
                    m = pe.transpose(bank[:, n * P:(n + 1) * P], src[:, t, c * P:(c + 1) * P], ident[:])
                return m

            def project(w, xT, dst, at, s, ready, srcs, it):
                for c in range(DC):
                    for n in srcs:
                        need(pe, n, it)
                    bank = open_fill(pe, "M", s, c, at)
                    for d in range(DC):
                        m = mm3(pe, bank[:], part(w, slice(None), d, slice(c * P, (c + 1) * P)),
                                part(xT, slice(None), d, slice(None)), d == 0, d == DC - 1)
                    done(ready, m)

            def back(xT, w, at, s, ready, it):
                for h in range(QT // 2):
                    bank = open_fill(pe, "M", s, h, at)
                    for n in range(2):
                        t = 2 * h + n
                        for d in range(DC):
                            m = mm3(pe, bank[:, n * D:(n + 1) * D], part(xT, slice(None), d, slice(t * P, (t + 1) * P)),
                                    part(w, slice(None), d, slice(None)), d == 0, d == DC - 1)
                    done(ready, m)

            def row0(kT, qT, tiles, s, at, ready, n, ones_ready, len_ready, it):
                bank = open_fill(pe, "M", s, 0, at)
                for t in range(tiles):
                    for d in range(DC):
                        m = mm3(pe, bank[:, t:t + 1], part(kT, slice(None), d, slice(t * P, (t + 1) * P)),
                                part(qT, slice(None), d, slice(0, 1)), d == 0, d == DC - 1)
                done(ready, m)
                need(pe, ones_ready, it)
                bank = open_fill(pe, "M", s, 1, at)
                done(len_ready, pe.matmul(bank[:, 0:tiles], ones[:], nz_k[n][:], start=True, stop=True))

            def step(s, it, at):
                if s == "b_ctx":
                    need(pe, "ctx_in", it)
                    for c in range(DC):
                        for h in range(2):
                            k = 2 * c + h
                            done("ctxT_p", turn(c_sb, c, range(4 * h, 4 * h + 4), "T", s, k, at))
                if s == "c_x3T":
                    need(pe, "x3", it)
                    for c in range(DC):
                        done("x3T_p", turn(x3, c, range(QT), "T", s, c, at))
                if s == "b_q2T":
                    project(a2, x2T, q2T, at, s, "q2T_p", ["x2T_l"], it)
                if s == "c_fc1":
                    project(fc1_p, x3T, fh, at, s, "fc1_p", ["x3T_l"], it)
                if s == "b_len":
                    need(pe, "q2T_l", it)
                    need(pe, "ctxT_l", it)
                    row0(ctxT, q2T, KT, s, at, "e2_p", 1, "nz2", "len2_p", it)
                if s == "a_xnT":
                    need(pe, "xn", it)
                    for c in range(DC):
                        done("xnT_p", turn(xn, c, range(QT), "T", s, c, at))
                if s in ("b_s2a", "b_s2b"):
                    for n in range(2):
                        t = (0 if s == "b_s2a" else 2) + n
                        bank = open_fill(pe, "S", s, n, at)
                        for h in range(2):
                            for d in range(DC):
                                m = mm3(pe, bank[:, h * 512:(h + 1) * 512],
                                        part(q2T, slice(None), d, slice(t * P, (t + 1) * P)),
                                        part(ctxT, slice(None), d, slice(h * 512, (h + 1) * 512)), d == 0, d == DC - 1)
                        done("s2_p", m)
                if s == "c_fc2":
                    need(pe, "fh_l", it)
                    back(fh_p, fc2_p, at, s, "fc2_p", it)
                if s == "a_q1T":
                    project(a1, xnT, q1T, at, s, "q1T_p", ["xnT_l"], it)
                if s == "a_len":
                    need(pe, "q1T_l", it)
                    row0(xnT, q1T, QT, s, at, "e1_p", 0, "nz1", "len1_p", it)
                if s == "a_s1":
                    for n, tiles in enumerate(((0, 1, 2), (3,))):
                        bank = open_fill(pe, "S", s, n, at)
                        for t in tiles:
                            w = P * (t + 1)
                            o = q_seg[t] + (P if t == 2 else 0) - (q_seg[3] if t == 3 else 0)
                            for d in range(DC):
                                m = mm3(pe, bank[:, o:o + w], part(q1T, slice(None), d, slice(t * P, (t + 1) * P)),
                                        part(xnT, slice(None), d, slice(0, w)), d == 0, d == DC - 1)
                        done("s1_p", m)
                if s == "b_p2T":
                    need(pe, "p2", it)
                    for k in range(KT):
                        bank = open_fill(pe, "T", s, k, at)
                        for t in range(QT):
                            m = pe.transpose(bank[:, t * P:(t + 1) * P], sm2[:, t, k * P:(k + 1) * P], ident[:])
                        done("p2T_p", m)
                if s == "c_x4T":
                    need(pe, "rowx", it)
                    for c in range(DC):
                        done("x4T_p", turn(rows, c, range(QT), "T", s, c, at))
                if s in ("b_c2T0", "b_c2T1"):
                    c = int(s[-1])
                    need(pe, "ctx_l", it)
                    bank = open_fill(pe, "M", s, 0, at)
                    for k in range(KT):
                        if c == 0:
                            need(pe, "p2T_l", it, k)
                        m = mm3(pe, bank[:], part(c_p, slice(None), k, slice(c * P, (c + 1) * P)),
                                part(p2T, slice(None), k, slice(None)), k == 0, k == KT - 1)
                    done("c2T_p", m)
                if s == "c_logits":
                    need(pe, "x4T", it)
                    bank = open_fill(pe, "M", s, 0, at)
                    for t in range(QT):
                        for d in range(DC):
                            m = pe.matmul(bank[:, t * E:(t + 1) * E], x4T[:, d, t * P:(t + 1) * P], wr_sb[:, d, :],
                                          start=d == 0, stop=d == DC - 1)
                    done("logits_p", m)
                if s == "a_p1T":
                    need(pe, "p1", it)
                    for k in range(QT):
                        bank = open_fill(pe, "T", s, k, at)
                        for n, t in enumerate(range(k, QT)):
                            o = q_seg[t] + k * P
                            m = pe.transpose(bank[:, n * P:(n + 1) * P], sm1[:, o:o + P], ident[:])
                        done("p1T_p", m)
                if s == "c_rank":
                    need(pe, "route", it, 5)
                    bank = open_fill(pe, "M", s, 0, at)
                    w = 2 * E
                    hot2 = hot[:].rearrange("p t k e -> p t (k e)")
                    out_ = bank[:, 0:QT * w].rearrange("p (t w) -> p t w", t=QT)
                    pe.matmul(out_, tri[:], hot2, start=True, stop=False)
                    for t in range(QT - 1):
                        pe.matmul(out_[:, t + 1:, :], ones[:], hot2[:, t:t + 1, :].to_broadcast([P, QT - 1 - t, w]),
                                  start=False, stop=False)
                    done("rank_p", pe.matmul(out_, ones[:], taken[:].unsqueeze(1).to_broadcast([P, QT, w]),
                                             start=False, stop=True))
                if s == "a_c1T":
                    need(pe, "xn_l", it)
                    for c in range(DC):
                        bank = open_fill(pe, "M", s, c, at)
                        for k in range(QT):
                            if c == 0:
                                need(pe, "p1T_l", it, k)
                            w = P * (QT - k)
                            m = mm3(pe, bank[:, k * P:512], part(xn_p, slice(None), k, slice(c * P, (c + 1) * P)),
                                    part(p1T, slice(None), slice(k_seg[k], k_seg[k] + w)), k == 0, k == QT - 1)
                        done("c1T_p", m)
                if s == "b_z2":
                    need(pe, "c2T_l", it)
                    back(c2T, wv2_p, at, s, "z2_p", it)
                if s == "a_z1":
                    need(pe, "c1T_l", it)
                    back(c1T, wv1_p, at, s, "z1_p", it)
                if s == "a_x2T":
                    need(pe, "x2", it)
                    for c in range(DC):
                        done("x2T_p", turn(x2, c, range(QT), "T", s, c, at))

            walk(pe, step)

        EVACUATE = {
            "b_ctx": ("T", "ctxT_p", ctxT, "ctxT_h", "ctxT_l", "s2_p"),
            "c_x3T": ("T", "x3T_p", x3T, "x3T_h", "x3T_l", "fc1_p"),
            "b_q2T": ("M", "q2T_p", q2T, "q2T_h", "q2T_l", "s2_p"),
            "a_xnT": ("T", "xnT_p", xnT, "xnT_h", "xnT_l", "s1_p"),
            "a_q1T": ("M", "q1T_p", q1T, "q1T_h", "q1T_l", "s1_p"),
            "b_p2T": ("T", "p2T_p", p2T, "p2T_h", "p2T_l", "c2T_p"),
            "b_c2T0": ("M", "c2T_p", c2T, "c2T_h", "c2T_l", "z2_p"),
            "b_c2T1": ("M", "c2T_p", c2T, "c2T_h", "c2T_l", "z2_p"),
            "a_p1T": ("T", "p1T_p", p1T, "p1T_h", "p1T_l", "c1T_p"),
            "a_c1T": ("M", "c1T_p", c1T, "c1T_h", "c1T_l", "z1_p"),
            "a_x2T": ("T", "x2T_p", x2T, "x2T_h", "x2T_l", "q2T_p"),
        }

        def number(s, k):
            return 1 if s == "b_c2T1" else k

        def where(s, k, t):
            if s == "b_ctx":
                return t[:, k // 2, (k % 2) * 512:(k % 2 + 1) * 512], 512
            if s == "a_p1T":
                w = P * (QT - k)
                return t[:, k_seg[k]:k_seg[k] + w], w
            return t[:, number(s, k), :], 512

        @block.scalar
        def _(act):
            credit(act, names[40:70])
            act.wait_ge(vec_in, 16 * 12)
            act.activation(tanh_g[:], gates_in[:], ACT.Tanh).then_inc(gates, 1)

            NORMS = {"z_n0": (0, x_sb, xn, "xn"), "a_n1": (1, y1, y1, "yn1"), "b_n2": (2, x3, x3, "yn2"),
                     "c_n3": (3, x4, x4, "yn3"), "c_n4": (4, x4, rows, "rowx")}

            def step(s, it, at):
                if s in EVACUATE:
                    pool, filled, t, high, _, reader = EVACUATE[s]
                    for k in range(FILLS[pool][s]):
                        need(act, filled, it, number(s, k))
                        if k == 0:
                            before(act, reader, it)
                        dst, w = where(s, k, t[0])
                        done(high, act.activation(dst, bank_of(pool, s, k, at)[:, 0:w], ACT.Copy))
                if s == "b_ctx":
                    need(act, "ctx_in", it)
                    before(act, "c2T_p", it)
                    done("ctx_h", act.activation(c_p[0][:], c_sb[:], ACT.Copy))
                for ln, (n, src, dst, ready) in NORMS.items():
                    if s == ln:
                        need(act, f"nb{n}", it)
                        if n == 0:
                            before(act, "y1", it)
                            before(act, "xn_l", it)
                            before(act, "xnT_p", it)
                        if n == 4:
                            need(act, "rows_gone", it)
                        for t in range(QT):
                            m = act.activation(dst[:, t, 0:D], src[:, t, :], ACT.Identity, bias=nb[n][:, t:t + 1],
                                               scale=rstd[n][:, t:t + 1])
                        done(ready, m)
                if s == "z_n0":
                    need(act, "xn", it)
                    before(act, "c1T_p", it)
                    done("xn_h", act.activation(xn_p[0][:], xn[:], ACT.Copy))
                if s == "c_fc1":
                    for c in range(DC):
                        need(act, "fc1_p", it, c)
                        before(act, "fh_l", it)
                        done("fh", act.activation(fh[:, c, :], bank_of("M", s, c, at)[:], ACT.Relu,
                                                  bias=b1T[:, E * FC + c:E * FC + c + 1]))
                        need(act, "fh", it, c)
                        before(act, "fc2_p", it)
                        done("fh_h", act.activation(fh_p[0][:, c, :], fh[:, c, :], ACT.Copy))
                if s in ("b_s2a", "b_s2b"):
                    b0 = 0 if s == "b_s2a" else 2
                    need(act, "nmax2", it, b0 // 2)
                    for t in (b0, b0 + 1):
                        done("p2", act.activation(sm2[:, t, :], sm2[:, t, :], ACT.Exp, bias=ntop[1][:, t:t + 1],
                                                  scale=SCALE, accum_out=total[1][:, t:t + 1]))
                if s == "a_s1":
                    need(act, "nmax1", it)
                    for t in range(QT):
                        o, w = q_seg[t], P * (t + 1)
                        done("p1", act.activation(sm1[:, o:o + w], sm1[:, o:o + w], ACT.Exp,
                                                  bias=ntop[0][:, t:t + 1], scale=SCALE,
                                                  accum_out=total[0][:, t:t + 1]))
                if s == "c_x4T":
                    before(act, "logits_p", it)
                    for c in range(DC):
                        need(act, "x4T_p", it, c)
                        done("x4T", act.activation(x4T[:, c, :], bank_of("T", s, c, at)[:], ACT.Copy))
                if s == "c_rank":
                    need(act, "gap", it)
                    done("gate", act.activation(egap[:], gap[:], ACT.Exp))

            walk(act, step)

        @block.vector
        def _(dve):
            credit(dve, names[70:])
            for i, n in enumerate(("wq1", "wk1", "wq2", "wk2")):
                dve.wait_ge(wT_p, i + 1)
                dve.tensor_copy(wT[n], pool_t[i % 2][:].rearrange("p (c d) -> p c d", c=DC)).then_inc(wT_v, 1)
            dve.wait_ge(wT_p, 5)
            dve.tensor_copy(b1T[:], pool_m[0][:, 0:E * FC + DC]).then_inc(wT_v, 1)
            for n, p in (("wv1", wv1_p), ("wv2", wv2_p), ("fc1", fc1_p), ("fc2", fc2_p)):
                ins = dve.tensor_copy(p[0][:], raw_w[n])
            ins.then_inc(const_v, 1)
            dve.wait_ge(const_v, 1)
            for n, p in (("wv1", wv1_p), ("wv2", wv2_p), ("fc1", fc1_p), ("fc2", fc2_p)):
                ins = dve.tensor_tensor(p[1][:], raw_w[n], p[0][:], ALU.subtract)
            ins.then_inc(const_v, 1)
            for i, p in enumerate((a1, a2)):
                dve.wait_ge(a_p, i + 1)
                src = pool_s[i][:, 0:DC * D].rearrange("p (c d) -> p c d", c=DC)
                dve.tensor_copy(p[0][:], src).then_inc(const_v, 1)
                dve.wait_ge(const_v, 3 + i)
                dve.tensor_tensor(p[1][:], src, p[0][:], ALU.subtract).then_inc(a_v, 1)
            dve.wait_ge(const_p, 17 + 2 * QT)

            def norm_stats(n, it, src, width):
                for t in range(QT):
                    done(f"bn{n}", dve.bn_stats(stat[n][:, t, :], src[:, t, 0:width]))
                need(dve, f"bn{n}", it)
                settle(dve)
                for t in range(QT):
                    ins = dve.bn_aggr(mv[n][:, t, :], stat[n][:, t, :])
                done(f"mv{n}", ins)

            def count(n, tiles, s, at, it, width, key, mask):
                e, nz, lp, ln, mk = ("e1_p", "nz1", "len1_p", "len1", "mask1") if n == 0 else \
                    ("e2_p", "nz2", "len2_p", "len2", "mask2")
                need(dve, e, it)
                ins = dve.tensor_scalar(nz_k[n][:], bank_of("M", s, 0, at)[:, 0:tiles], 0.0, None, ALU.not_equal)
                done(nz, ins)
                need(dve, lp, it)
                ins = dve.tensor_reduce(length[n][:], bank_of("M", s, 1, at)[:, 0:tiles], AX.X, ALU.add)
                done(ln, ins)
                need(dve, ln, it)
                done(mk, dve.tensor_scalar(mask[:], key[:], length[n][:], MASKED, ALU.is_ge, ALU.mult))

            def invert(n, it, last_total):
                name = f"inv{n + 1}"
                need(dve, last_total, it)
                done(name, dve.tensor_scalar(some[n][:], length[n][:], 1.0, None, ALU.min))
                need(dve, name, it, 0)
                done(name, dve.tensor_scalar(full[n][:], total[n][:], some[n][:], None, ALU.mult))
                need(dve, name, it, 1)
                done(name, dve.reciprocal(inv[n][:], full[n][:]))
                need(dve, name, it, 2)

            def step(s, it, at):
                if s in EVACUATE:
                    pool, _, t, high, low, _ = EVACUATE[s]
                    for k in range(FILLS[pool][s]):
                        need(dve, high, it, number(s, k))
                        dst, w = where(s, k, t[1])
                        hi, _ = where(s, k, t[0])
                        ins = dve.tensor_tensor(dst, bank_of(pool, s, k, at)[:, 0:w], hi, ALU.subtract)
                        done(low, ins)
                if s == "z_ln0":
                    need(dve, "x_in", it)
                    norm_stats(0, it, x_sb, D)
                if s == "b_len":
                    count(1, KT, s, at, it, SK, key2, mask2)
                if s == "a_len":
                    count(0, QT, s, at, it, SELF_W, key1, mask1)
                if s in ("b_s2a", "b_s2b"):
                    b0 = 0 if s == "b_s2a" else 2
                    if b0 == 0:
                        need(dve, "mask2", it)
                        before(dve, "p2T_p", it)
                    for n in range(2):
                        t = b0 + n
                        need(dve, "s2_p", it, t)
                        settle(dve)
                        ins = dve.tensor_tensor_reduce(sm2[:, t, :], bank_of("S", s, n, at)[:], mask2[:], 1.0,
                                                       -3.4e38, ALU.add, ALU.max, top[1][:, t:t + 1])
                        done("sm2", ins)
                    need(dve, "sm2", it, b0 + 1)
                    done("nmax2", dve.tensor_scalar(ntop[1][:, b0:b0 + 2], top[1][:, b0:b0 + 2], -SCALE, None,
                                                    ALU.mult))
                if s == "a_s1":
                    need(dve, "mask1", it)
                    for t in range(QT):
                        if t in (0, 3):
                            need(dve, "s1_p", it, t // 3)
                            settle(dve)
                        bank = bank_of("S", s, t // 3, at)
                        w = P * (t + 1)
                        o = q_seg[t] + (P if t == 2 else 0) - (q_seg[3] if t == 3 else 0)
                        done("sm1", dve.tensor_tensor_reduce(
                            sm1[:, q_seg[t]:q_seg[t] + w], bank[:, o:o + w], mask1[:, q_seg[t]:q_seg[t] + w], 1.0,
                            -3.4e38, ALU.add, ALU.max, top[0][:, t:t + 1]))
                    need(dve, "sm1", it)
                    done("nmax1", dve.tensor_scalar(ntop[0][:], top[0][:], -SCALE, None, ALU.mult))
                if s == "c_fc2":
                    need(dve, "x3b", it)
                    before(dve, "x4_out", it)
                    for h in range(2):
                        need(dve, "fc2_p", it, h)
                        src = bank_of("M", s, h, at)[:].rearrange("p (t d) -> p t d", t=2)
                        ins = dve.tensor_tensor(x4[:, 2 * h:2 * h + 2, :], src, x3b[:, 2 * h:2 * h + 2, :], ALU.add)
                        done("y3", ins)
                    need(dve, "y3", it)
                    norm_stats(3, it, x4, D)
                if s == "c_x4":
                    need(dve, "yg3", it)
                    need(dve, "xro", it)
                    done("x4", dve.tensor_tensor(x4[:], x4[:], xr[:], ALU.add))
                    need(dve, "x4", it)
                    norm_stats(4, it, x4, D)
                if s in ("b_z2", "a_z1"):
                    n, z, y, res, dst = (1, "z2_p", "y2", x2, x3) if s == "b_z2" else (0, "z1_p", "y1", xn, y1)
                    invert(n, it, "p2" if n else "p1")
                    if n:
                        before(dve, "x3T_p", it)
                        before(dve, "x3b", it)
                    for t in range(QT):
                        if t % 2 == 0:
                            need(dve, z, it, t // 2)
                        o = (t % 2) * D
                        ins = dve.scalar_tensor_tensor(dst[:, t, :], bank_of("M", s, t // 2, at)[:, o:o + D],
                                                       inv[n][:, t:t + 1], res[:, t, :], ALU.mult, ALU.add)
                        done(y, ins)
                    need(dve, y, it)
                    norm_stats(2 if n else 1, it, dst, D)
                r = [0]

                def link(ins):
                    done("route", ins)
                    need(dve, "route", it, r[0])
                    r[0] += 1

                if s == "c_logits":
                    need(dve, "logits_p", it)
                    ins = dve.tensor_copy(lg[:], bank_of("M", s, 0, at)[:, 0:QT * E].rearrange(
                        "p (t e) -> p t e", t=QT))
                    done("logits", ins)
                    need(dve, "logits", it)
                    settle(dve)
                    for t in range(QT):
                        ins = dve.max(best[:, t, :], lg[:, t, :])
                    link(ins)
                    settle(dve)
                    for t in range(QT):
                        ins = dve.max_index(besti[:, t, :], best[:, t, :], lg[:, t, :])
                    link(ins)
                    link(dve.tensor_copy(pick[:], besti[:, :, 0:2]))
                    before(dve, "rank_p", it)
                    for k in range(2):
                        ins = dve.tensor_tensor(hot[:, :, k, :], iota_e[:].unsqueeze(1).to_broadcast([P, QT, E]),
                                                pick[:, :, k:k + 1].to_broadcast([P, QT, E]), ALU.is_equal)
                    link(ins)
                    done("gap", dve.tensor_tensor(gap[:], best[:, :, 1], best[:, :, 0], ALU.subtract))
                    link(dve.tensor_reduce(newly[:], hot[:].rearrange("p t k e -> p (k e) t"), AX.X, ALU.add))
                    link(dve.tensor_copy(rows[:, :, TOKEN].bitcast(I32), token[:]))
                if s == "c_rank":
                    need(dve, "rank_p", it)
                    r[0] = 6
                    bank = bank_of("M", s, 0, at)
                    link(dve.tensor_tensor(rsel[:], bank[:, 0:QT * 2 * E].rearrange(
                        "p (t k e) -> p t k e", t=QT, k=2), hot[:], ALU.mult))
                    ins = dve.tensor_reduce(rank[:], rsel[:], AX.X, ALU.add)
                    ins = dve.tensor_tensor(taken[:], taken[:], newly[:], ALU.add)
                    ins = dve.tensor_scalar(token[:], token[:], float(S), None, ALU.add)
                    link(ins)
                if s == "c_slots":
                    r[0] = 8
                    need(dve, "gate", it)
                    ins = dve.tensor_scalar(den[:], egap[:], 1.0, None, ALU.add)
                    dve.tensor_scalar(keep[:], rank[:], float(CAP), None, ALU.is_le)
                    dve.tensor_scalar(over[:], rank[:], float(CAP), SKIP, ALU.is_gt, ALU.mult)
                    link(dve.scalar_tensor_tensor(slotf[:], pick[:], float(SLOTS), rank[:], ALU.mult, ALU.add))
                    dve.reciprocal(gate[:, :, 0], den[:])
                    link(dve.tensor_tensor(slotf[:], slotf[:], slot_off[:], ALU.add))
                    dve.tensor_tensor(gate[:, :, 1], gate[:, :, 0], egap[:], ALU.mult)
                    link(dve.tensor_tensor(slotf[:], slotf[:], over[:], ALU.add))
                    link(dve.scalar_tensor_tensor(rows[:, :, WEIGHT:WEIGHT + 2], gate[:], tanh_g[:, 1:2], keep[:],
                                                  ALU.mult, ALU.mult))
                    done("slots", dve.tensor_scalar(slot[:], slotf[:].rearrange("p t k -> p (t k)"), 0.0, 2 * SKIP,
                                                    ALU.max, ALU.min))

            walk(dve, step)


def experts(nc, g):
    (w1, w2, b2, out, xs, ident, b1T, w_in, w1_raw, w2_raw) = (g[n] for n in (
        "w1", "w2", "b2", "out", "xs", "ident", "b1T", "w_in", "w1_raw", "w2_raw"))
    D, E, F, DC, FC, T, SLOTS, ROW, TOKEN, WEIGHT, CAP, W_IN = (g[n] for n in (
        "D", "E", "F", "DC", "FC", "T", "SLOTS", "ROW", "TOKEN", "WEIGHT", "CAP", "W_IN"))
    CH = 2 * P
    NCH = SLOTS // CH
    PAIR = 2 * NCH
    TILES = SLOTS // P
    YS = 4
    HF = FC // 2
    assert SLOTS % CH == 0 and E % 2 == 0

    with ExitStack() as ctx:
        def sb(name, shape, dt=F32):
            return ctx.enter_context(nc.sbuf_tensor(name, shape, dt))

        def psum(name, shape):
            return ctx.enter_context(nc.psum_tensor(name, shape, F32))

        def sem(name):
            return ctx.enter_context(nc.semaphore(name))

        w1_p = [[sb(f"w1_{n}{h}", [P, DC, F], F16) for h in "hl"] for n in range(2)]
        w2_p = [[sb(f"w2_{n}{h}", [P, FC, D], F16) for h in "hl"] for n in range(2)]
        b2_bc = [sb(f"b2_bc{n}", [P, D]) for n in range(2)]
        slot_x = [sb(f"slot_x{n}", [P, TILES, ROW]) for n in range(2)]
        xT_p = [[sb(f"sxT_{n}{h}", [P, DC, CH], F16) for h in "hl"] for n in range(2)]
        hid = [sb(f"hid{n}", [P, 2, CH]) for n in range(2)]
        hid_p = [[sb(f"hid_{n}{h}", [P, FC, CH], F16) for h in "hl"] for n in range(2)]
        yb = [sb(f"yb{n}", [P, D]) for n in range(2)]
        ys = [sb(f"ys{n}", [P, D]) for n in range(YS)]
        bias = [sb(f"bias{n}", [P, FC]) for n in range(2)]
        bank_x = [psum(f"bank_x{n}", [P, DC, CH]) for n in range(2)]
        bank_h = [psum(f"bank_h{n}", [P, 2, CH]) for n in range(4)]
        bank_y = [psum(f"bank_y{n}", [P, 2, D]) for n in range(2)]

        N = {"w_h": 4, "w_l": 4, "b2_in0": 1, "b2_in1": 1, "head_in0": 1, "head_in1": 1, "tail_in0": 1, "tail_in1": 1, "xT_f": PAIR, "xT_h": PAIR, "xT_l": PAIR,
             "h_f": PAIR * HF, "gelu": PAIR * HF, "hid_h": PAIR * HF, "hid_l": PAIR * HF, "y_f": PAIR,
             "y_b": 2 * PAIR, "y_w": 2 * PAIR, "added": 2 * PAIR, "bias": 2, "ys_free": 2 * PAIR}
        DMAS = ("b2_in0", "b2_in1", "head_in0", "head_in1", "tail_in0", "tail_in1", "added")
        ev = {n: sem("e_" + n) for n in N}
        settled = sem("e_settled")

        def unit(n):
            return 16 if n in DMAS else 1

        def done(n, ins):
            ins.then_inc(ev[n], unit(n))

        CREDIT = 64

        def upto(eng, n, j, k):
            eng.wait_ge(ev[n], j * (N[n] * unit(n)) + (CREDIT + k * unit(n)))

        def credit(eng, names):
            for n in names:
                if n != "added":
                    eng.sem_inc(ev[n], CREDIT)

        names = list(N)
        block = ctx.enter_context(nc.Block())

        @block.sync
        def _(sp):
            credit(sp, names[0:4])

            xs_v = xs.rearrange("(e t p) d -> e p t d", p=P, t=TILES)

            def load_slots(j, h):
                upto(sp, "ys_free", j, 2 * NCH * (h - 1))
                done(f"head_in{h % 2}", sp.dma_start(slot_x[h % 2][:, 0:2, :], xs_v[j * 2 + h][:, 0:2, :]))
                done(f"tail_in{h % 2}", sp.dma_start(slot_x[h % 2][:, 2:, :], xs_v[j * 2 + h][:, 2:, :]))

            def two_experts(j, last):
                for h in range(2):
                    if not (last and h == 1):
                        load_slots(j, h + 1)
                    upto(sp, "y_b", j, 2 * NCH * (h - 1))
                    done(f"b2_in{h}", sp.dma_start(b2_bc[h][:], b2[j * 2 + h].partition_broadcast(P)))
                    if not (last and h == 1):
                        upto(sp, "w_l", j, 2 * h + 2)
                        g["load_expert"](sp, j * 2 + (h + 1))

            load_slots(0, 0)
            with sp.Fori(0, E // 2 - 1) as j:
                two_experts(j, False)
            two_experts(E // 2 - 1, True)

        @block.gpsimd
        def _(pool):
            credit(pool, names[4:8])

            def two_experts(j, last):
                for n in range(PAIR):
                    h = n // NCH
                    for t in range(2):
                        k = 2 * n + t
                        upto(pool, "y_w", j, k + 1)
                        pool.sem_inc(settled, 1)
                        tile = n % NCH * 2 + t
                        done("added", pool.indirect_dma_start(
                            out, bass.IndirectOffsetOnAxis(ap=slot_x[h][:, tile, TOKEN:TOKEN + 1].bitcast(U32), axis=0),
                            ys[k % YS][:], None, compute_op=ALU.add, oob_is_err=True))
                        pool.wait_ge(ev["added"], j * (16 * 2 * PAIR) + 16 * (k + 1))
                        pool.sem_inc(ev["ys_free"], 1)

            with pool.Fori(0, E // 2 - 1) as j:
                two_experts(j, False)
            two_experts(E // 2 - 1, True)

        @block.tensor
        def _(pe):
            credit(pe, names[8:12])

            def turn(j, n):
                h, c = n // NCH, n % NCH
                if c < 2:
                    upto(pe, f"{'tail' if c else 'head'}_in{h % 2}", j, h // 2 + 1)
                upto(pe, "xT_l", j, n - 1)
                for d in range(DC):
                    for t in range(2):
                        m = pe.transpose(bank_x[n % 2][:, d, t * P:(t + 1) * P],
                                         slot_x[h % 2][:, 2 * c + t, d * P:(d + 1) * P], ident[:])
                done("xT_f", m)

            def two_experts(j, last):
                for n in range(PAIR):
                    h = n // NCH
                    if n % NCH == 0:
                        upto(pe, "w_l", j, 2 * h + 2)
                    upto(pe, "xT_l", j, n + 1)
                    for b in range(HF):
                        k = n * HF + b
                        upto(pe, "hid_l", j, k - 3)
                        bank = bank_h[k % 4]
                        for f2 in range(2):
                            f = 2 * b + f2
                            for d in range(DC):
                                fs = slice(f * P, (f + 1) * P)
                                m = mm3(pe, bank[:, f2, :], (w1_p[h][0][:, d, fs], w1_p[h][1][:, d, fs]),
                                        (xT_p[n % 2][0][:, d, :], xT_p[n % 2][1][:, d, :]), d == 0, d == DC - 1)
                        done("h_f", m)
                    if not (last and n == PAIR - 1):
                        turn(j, n + 1)
                    upto(pe, "y_b", j, 2 * n - 2)
                    for t in range(2):
                        for f in range(FC):
                            if t == 0 and f % 2 == 0:
                                upto(pe, "hid_l", j, n * HF + f // 2 + 1)
                            ts = slice(t * P, (t + 1) * P)
                            m = mm3(pe, bank_y[n % 2][:, t, :],
                                    (hid_p[n % 2][0][:, f, ts], hid_p[n % 2][1][:, f, ts]),
                                    (w2_p[h][0][:, f, :], w2_p[h][1][:, f, :]), f == 0, f == FC - 1)
                    done("y_f", m)

            turn(0, 0)
            with pe.Fori(0, E // 2 - 1) as j:
                two_experts(j, False)
            two_experts(E // 2 - 1, True)

        @block.scalar
        def _(act):
            credit(act, names[12:14])

            def split_high(j, h):
                act.wait_ge(w_in, j * (2 * W_IN) + W_IN * (h + 1))
                upto(act, "y_f", j, NCH * (h - 1))
                done("bias", act.activation(bias[h % 2][:], b1T[:, bass.ds((j * 2 + h) * FC, FC)], ACT.Copy))
                done("w_h", act.activation(w1_p[h % 2][0][:], w1_raw, ACT.Copy))

            def split_high2(j, h):
                done("w_h", act.activation(w2_p[h % 2][0][:], w2_raw, ACT.Copy))

            def two_experts(j, last):
                for n in range(PAIR):
                    h = n // NCH
                    if n % NCH == 0:
                        upto(act, "bias", j, h + 1)
                    for b in range(HF):
                        k = n * HF + b
                        upto(act, "h_f", j, k + 1)
                        upto(act, "hid_l", j, k - 1)
                        for f2 in range(2):
                            f = 2 * b + f2
                            m = act.activation(hid[b % 2][:, f2, :], bank_h[k % 4][:, f2, :], ACT.Gelu,
                                               bias=bias[h][:, f:f + 1])
                        done("gelu", m)
                    if not (last and n == PAIR - 1):
                        slots_high(j, n + 1)
                    if n % NCH == 1 and not (last and h == 1):
                        split_high(j, h + 1)
                    if n % NCH == 2 and not (last and h == 1):
                        split_high2(j, h + 1)

            def slots_high(j, n):
                upto(act, "xT_f", j, n + 1)
                upto(act, "h_f", j, HF * (n - 1))
                done("xT_h", act.activation(xT_p[n % 2][0][:], bank_x[n % 2][:], ACT.Copy))

            split_high(0, 0)
            split_high2(0, 0)
            slots_high(0, 0)
            with act.Fori(0, E // 2 - 1) as j:
                two_experts(j, False)
            two_experts(E // 2 - 1, True)

        @block.vector
        def _(dve):
            credit(dve, names[14:])

            def split_low(j, h, n):
                upto(dve, "w_h", j, 2 * h + n + 1)
                part, raw = ((w1_p, w1_raw), (w2_p, w2_raw))[n]
                done("w_l", dve.tensor_tensor(part[h % 2][1][:], raw, part[h % 2][0][:], ALU.subtract))

            def slots_low(j, n):
                upto(dve, "xT_h", j, n + 1)
                done("xT_l", dve.tensor_tensor(xT_p[n % 2][1][:], bank_x[n % 2][:], xT_p[n % 2][0][:],
                                               ALU.subtract))

            def two_experts(j, last):
                for n in range(PAIR):
                    h = n // NCH
                    for b in range(HF):
                        k = n * HF + b
                        upto(dve, "gelu", j, k + 1)
                        if b == 0:
                            upto(dve, "y_f", j, n - 1)
                        fs = slice(2 * b, 2 * b + 2)
                        done("hid_h", dve.tensor_copy(hid_p[n % 2][0][:, fs, :], hid[b % 2][:]))
                        upto(dve, "hid_h", j, k + 1)
                        done("hid_l", dve.tensor_tensor(hid_p[n % 2][1][:, fs, :], hid[b % 2][:],
                                                        hid_p[n % 2][0][:, fs, :], ALU.subtract))
                    if not (last and n == PAIR - 1):
                        slots_low(j, n + 1)
                    upto(dve, "y_f", j, n + 1)
                    if n % NCH == 0:
                        upto(dve, f"b2_in{h}", j, 1)
                    for t in range(2):
                        k = 2 * n + t
                        done("y_b", dve.tensor_tensor(yb[t][:], bank_y[n % 2][:, t, :], b2_bc[h][:], ALU.add))
                        upto(dve, "y_b", j, k + 1)
                        upto(dve, "ys_free", j, k - YS + 1)
                        choice = (n % NCH * 2 + t) // (CAP // P)
                        weight = slot_x[h][:, n % NCH * 2 + t, WEIGHT + choice:WEIGHT + choice + 1]
                        done("y_w", dve.tensor_scalar(ys[k % YS][:], yb[t][:], weight, None, ALU.mult))
                    if n % NCH in (1, 2) and not (last and h == 1):
                        split_low(j, h + 1, n % NCH - 1)

            split_low(0, 0, 0)
            split_low(0, 0, 1)
            slots_low(0, 0)
            with dve.Fori(0, E // 2 - 1) as j:
                two_experts(j, False)
            two_experts(E // 2 - 1, True)


_INS = ['x', 'ctx_1024', 'g_xattn', 'g_ffn', 'L0_xattn_Wq1', 'L0_xattn_Wk1', 'L0_xattn_Wv1', 'L0_xattn_Wq2',
        'L0_xattn_Wk2', 'L0_xattn_Wv2', 'L0_xattn_fc1_w', 'L0_xattn_fc1_b', 'L0_xattn_fc2_w', 'L0_xattn_fc2_b',
        'L0_xattn_ln1_g', 'L0_xattn_ln1_b', 'L0_xattn_ln2_g', 'L0_xattn_ln2_b', 'L0_xattn_ln3_g', 'L0_xattn_ln3_b',
        'L0_ffn_Wr', 'L0_ffn_W1', 'L0_ffn_b1', 'L0_ffn_W2', 'L0_ffn_b2']


def kernel(**inputs):
    import numpy as _np
    import concourse.bacc as _bacc
    from concourse import mybir as _mybir
    from concourse.bass_utils import run_bass_kernel_spmd as _run

    nc = _bacc.Bacc("TRN2", target_bir_lowering=False, num_devices=1)
    arrays, args = {}, []
    for name in _INS:
        a = _np.ascontiguousarray(inputs[name])
        arrays[f"in_{name}_dram"] = a
        args.append(nc.dram_tensor(f"in_{name}_dram", a.shape, _mybir.dt.from_np(a.dtype), kind="ExternalInput").ap())
    b, s, d = inputs["x"].shape
    tokens, experts_ = b * s, inputs["L0_ffn_Wr"].shape[1]
    out = nc.dram_tensor("out_0_dram", (tokens + 128, d), _mybir.dt.float32, kind="ExternalOutput").ap()
    slots = experts_ * 2 * int(tokens * 1.25 / experts_)
    xs = nc.dram_tensor("slot_rows", (slots, d + 4), _mybir.dt.float32, kind="Internal").ap()
    flamingo_moe_kernel(nc, *args, out, xs)
    r = _run(nc, [arrays], core_ids=[0])
    return r.results[0]["out_0_dram"][:tokens].reshape(b, s, d)
```

```python
from contextlib import ExitStack

import concourse.bass as bass
from concourse import mybir

F32 = mybir.dt.float32
F16 = mybir.dt.float16
I32 = mybir.dt.int32
U32 = mybir.dt.uint32
ALU = mybir.AluOpType
ACT = mybir.ActivationFunctionType
AX = mybir.AxisListType

P = 128
EPS = 1e-5
MASKED = -3.0e38
NEVER = 1.0e9
SKIP = 30000.0

ORDER = [
    ("z_ln0", 0), ("d_send0", 4), ("d_send1", 4), ("b_s2a", 2), ("d_send2", 4), ("c_slots", 4), ("c_fc2", 3),
    ("c_ln3", 3), ("b_split", 2), ("b_s2b", 2), ("d_send3", 4), ("c_x4", 3), ("a_c1T", 1), ("b_p2T0", 2),
    ("a_z1", 1), ("b_p2T1", 2), ("a_ln1", 1), ("b_c2T0", 2), ("c_ln4", 3), ("z_n0", 0), ("b_c2T1", 2),
    ("a_xnT", 0), ("b_z2", 2), ("c_n4", 3), ("a_n1", 1), ("b_ln2", 2), ("a_q1T", 0), ("c_x4T", 3),
    ("a_len", 0), ("b_n2", 2), ("a_x2T", 1), ("a_s1", 0), ("c_logits", 3), ("c_x3T", 2), ("b_q2T", 1),
    ("b_ctx0", 1), ("c_xr", 2), ("b_ctx1", 1), ("c_fc1", 2), ("b_len", 1), ("a_p1T", 0), ("c_rank", 3),
]
BEGIN = ("z_ln0", "z_n0", "a_xnT")
LAG = dict(ORDER)
DEPTH = max(LAG.values())

FILLS = {
    "T": {"c_x3T": 2, "a_xnT": 2, "c_x4T": 2, "a_p1T": 4, "a_x2T": 2},
    "M": {"b_q2T": 2, "c_fc1": 2, "b_len": 2, "c_fc2": 2, "a_q1T": 2, "a_len": 2, "b_c2T0": 1, "b_c2T1": 1,
          "c_logits": 1, "a_c1T": 2, "c_rank": 1, "b_z2": 2, "a_z1": 2},
    "S": {"b_ctx0": 1, "b_ctx1": 1, "b_p2T0": 2, "b_p2T1": 2, "b_s2a": 2, "b_s2b": 2, "a_s1": 2},
}

EMPTIED = {
    "b_ctx0": ("ctxT_l", [0]), "b_ctx1": ("ctxT_l", [1]), "c_x3T": ("x3T_l", range(2)), "a_xnT": ("xnT_l", range(2)),
    "b_p2T0": ("p2T_l", range(2)), "b_p2T1": ("p2T_l", range(2, 4)), "c_x4T": ("x4T", range(2)),
    "a_p1T": ("p1T_l", range(4)), "a_x2T": ("x2T_l", range(2)), "b_q2T": ("q2T_l", range(2)),
    "c_fc1": ("fh", range(2)), "c_fc2": ("y3", range(2)), "a_q1T": ("q1T_l", range(2)),
    "b_c2T0": ("c2T_l", [0]), "b_c2T1": ("c2T_l", [1]),
    "c_logits": ("logits", [0]), "a_c1T": ("c1T_l", range(2)), "c_rank": ("route", [6]),
    "b_z2": ("y2", [1, 3]), "a_z1": ("y1", [1, 3]), "b_s2a": ("sm2", [0, 1]), "b_s2b": ("sm2", [2, 3]),
    "a_s1": ("sm1", [2, 3]), "b_len": (("nz2", "len2"), None), "a_len": (("nz1", "len1"), None),
}

SIGNALS = {
    "x_in": 1, "ctx_in": 1, "xr_in": 1, "x4_out": 1, "dispatched": 8,
    "bn0": 4, "mv0": 1, "ve0": 1, "rstd0": 1, "nb0": 1, "xn": 1, "xn_h": 1, "xn_l": 1,
    "xnT_p": 2, "xnT_h": 2, "xnT_l": 2, "q1T_p": 2, "q1T_h": 2, "q1T_l": 2,
    "e1_p": 1, "nz1": 1, "len1_p": 1, "len1": 1, "mask1": 1, "inv1": 3,
    "s1_p": 2, "sm1": 4, "nmax1": 1, "p1": 4, "p1T_p": 4, "p1T_h": 4, "p1T_l": 4,
    "c1T_p": 2, "c1T_h": 2, "c1T_l": 2, "z1_p": 2, "y1": 4,
    "bn1": 4, "mv1": 1, "ve1": 1, "rstd1": 1, "nb1": 1, "yn1": 1, "yg1": 1, "x2": 1,
    "x2T_p": 2, "x2T_h": 2, "x2T_l": 2,
    "ctx_h": 1, "ctx_l": 1, "ctxT_p": 2, "ctxT_h": 2, "ctxT_l": 2,
    "q2T_p": 2, "q2T_h": 2, "q2T_l": 2, "e2_p": 1, "nz2": 1, "len2_p": 1, "len2": 1, "mask2": 1,
    "inv2": 3, "s2_p": 4, "sm2": 4, "nmax2": 2, "p2": 4, "p2T_p": 4, "p2T_h": 4, "p2T_l": 4,
    "c2T_p": 2, "c2T_h": 2, "c2T_l": 2, "z2_p": 2, "y2": 4,
    "bn2": 4, "mv2": 1, "ve2": 1, "rstd2": 1, "yg2": 1, "x3": 1,
    "x3b": 1, "x3T_p": 2, "x3T_h": 2, "x3T_l": 2, "fc1_p": 2, "fh": 2, "fh_h": 2, "fh_l": 2,
    "fc2_p": 2, "y3": 2, "bn3": 4, "mv3": 1, "ve3": 1, "rstd3": 1, "yg3": 1, "xro": 1, "x4": 1,
    "bn4": 4, "mv4": 1, "ve4": 1, "rstd4": 1, "nb4": 1, "rowx": 1, "x4T_p": 2, "x4T": 2,
    "logits_p": 1, "logits": 1, "route": 12, "gap": 1, "gate": 1, "rank_p": 1, "slots": 1, "rows_gone": 1,
}


class Iteration:

    def __init__(self, j, offset):
        self.j, self.offset = j, offset

    def times(self, n, plus):
        at = n * self.offset + plus
        return at if self.j is None else self.j * n + at


def flamingo_moe_kernel(nc, x, ctx_in, g_x, g_f, wq1, wk1, wv1, wq2, wk2, wv2, fc1_w, fc1_b, fc2_w, fc2_b,
                        ln1_g, ln1_b, ln2_g, ln2_b, ln3_g, ln3_b, wr, w1, b1, w2, b2, out, xs):
    B, S, D = x.shape
    SK = ctx_in.shape[1]
    E, _, F = w1.shape
    DC, QT, KT = D // P, S // P, SK // P
    FC = F // P
    T = B * S
    CAP = int(T * 1.25 / E)
    SLOTS = 2 * CAP
    ROW = xs.shape[1]
    TOKEN, WEIGHT = D, D + 1
    SCALE = 1.0 / 4.0
    SELF_W = P * QT * (QT + 1) // 2
    assert D == 256 and S == 512 and SK == 1024 and E == 8 and CAP % P == 0 and B > DEPTH
    assert LAG["c_n4"] < DEPTH

    q_seg = [P * t * (t + 1) // 2 for t in range(QT)]
    k_seg = [P * (t * QT - t * (t - 1) // 2) for t in range(QT)]

    ctx = ExitStack()
    with ctx:
        def sb(name, shape, dt=F32):
            return ctx.enter_context(nc.sbuf_tensor(name, shape, dt))

        def sem(name):
            return ctx.enter_context(nc.semaphore(name))

        ident = sb("ident", [P, P])
        b1T = sb("b1T", [P, E * FC + DC])
        tanh_g = sb("tanh_g", [P, 2])
        w1_first = [sb(f"w1_0{h}", [P, DC, F], F16) for h in "hl"]
        w2_first = [sb(f"w2_0{h}", [P, FC, D], F16) for h in "hl"]
        w_in, w_split = sem("w_in"), sem("w_split")
        W_IN = 32

        def raw_weights(buffer):
            return (buffer[:, 0:DC * F].rearrange("p (c f) -> p c f", c=DC),
                    buffer[:, DC * F:].rearrange("p (c d) -> p c d", c=FC))

        def load_expert(eng, e, raw):
            eng.dma_start(raw[0], w1[e].rearrange("(c p) f -> p c f", p=P)).then_inc(w_in, 16)
            eng.dma_start(raw[1], w2[e].rearrange("(c p) d -> p c d", p=P)).then_inc(w_in, 16)

        attention(nc, locals())
        experts(nc, locals())


def mm3(pe, out, left, right, first=True, last=True):
    (lh, ll), (rh, rl) = left, right
    pe.matmul(out, lh, rh, start=first, stop=False)
    pe.matmul(out, lh, rl, start=False, stop=False)
    return pe.matmul(out, ll, rh, start=False, stop=last)


def attention(nc, g):
    (x, ctx_in, g_x, g_f, wq1, wk1, wv1, wq2, wk2, wv2, fc1_w, fc1_b, fc2_w, fc2_b, ln1_g, ln1_b, ln2_g, ln2_b,
     ln3_g, ln3_b, wr, b1, out, xs) = (g[n] for n in (
         "x", "ctx_in", "g_x", "g_f", "wq1", "wk1", "wv1", "wq2", "wk2", "wv2", "fc1_w", "fc1_b", "fc2_w", "fc2_b",
         "ln1_g", "ln1_b", "ln2_g", "ln2_b", "ln3_g", "ln3_b", "wr", "b1", "out", "xs"))
    B, S, D, SK, E, F, DC, QT, KT, FC, T, CAP, SLOTS, ROW, TOKEN, WEIGHT, SCALE, SELF_W = (g[n] for n in (
        "B", "S", "D", "SK", "E", "F", "DC", "QT", "KT", "FC", "T", "CAP", "SLOTS", "ROW", "TOKEN", "WEIGHT",
        "SCALE", "SELF_W"))
    q_seg, k_seg, ident, b1T, tanh_g = (g[n] for n in ("q_seg", "k_seg", "ident", "b1T", "tanh_g"))

    with ExitStack() as ctx:
        def sb(name, shape, dt=F32):
            return ctx.enter_context(nc.sbuf_tensor(name, shape, dt))

        def pair(name, shape):
            return sb(name + "_h", shape, F16), sb(name + "_l", shape, F16)

        def psum(name, shape):
            return ctx.enter_context(nc.psum_tensor(name, shape, F32))

        def sem(name):
            return ctx.enter_context(nc.semaphore(name))

        tri = sb("tri", [P, P], F16)
        ones = sb("ones", [P, P], F16)
        key1 = sb("key1", [P, SELF_W])
        key2 = sb("key2", [P, SK])
        iota_e = sb("iota_e", [P, E])
        slot_off = sb("slot_off", [P, QT, 2])
        neg_half = sb("neg_half", [P, QT])
        eps = sb("eps", [P, QT])
        token = sb("token", [P, QT])
        taken = sb("taken", [P, 2 * E], F16)
        vec = {n: sb(n + "_bc", [P, D]) for n in ("g1", "o1", "g2", "o2", "g3", "o3", "fc2_b")}
        wr_sb = sb("wr_sb", [P, DC, E])
        a1 = pair("a1", [P, DC, D])
        a2 = pair("a2", [P, DC, D])
        wv1_p, wv2_p = pair("wv1", [P, DC, D]), pair("wv2", [P, DC, D])
        fc1_p, fc2_p = pair("fc1", [P, DC, D]), pair("fc2", [P, DC, D])
        b1_raw = sb("b1_raw", [E * FC + DC, P])
        gates_in = sb("gates_in", [P, 2])

        x_sb = sb("x_sb", [P, QT, D])
        xn = sb("xn", [P, QT, D])
        xn_p = pair("xn", [P, QT, D])
        xnT = pair("xnT", [P, DC, S])
        q1T = pair("q1T", [P, DC, S])
        mask1 = sb("mask1", [P, SELF_W])
        sm1 = sb("sm1", [P, SELF_W])
        p1T = pair("p1T", [P, SELF_W])
        c1T = pair("c1T", [P, DC, S])
        y1 = sb("y1", [P, QT, D])
        x2 = sb("x2", [P, QT, D])
        x2T = pair("x2T", [P, DC, S])
        c_sb = sb("c_sb", [P, KT, D])
        c_p = pair("c", [P, KT, D])
        ctxT = pair("ctxT", [P, DC, SK])
        q2T = pair("q2T", [P, DC, S])
        mask2 = sb("mask2", [P, SK])
        sm2 = sb("sm2", [P, QT, SK])
        p2T = pair("p2T", [P, KT, S])
        c2T = pair("c2T", [P, DC, S])
        x3 = sb("x3", [P, QT, D])
        xr = sb("xr", [P, QT, D])
        x3b = sb("x3b", [P, QT, D])
        x3T = pair("x3T", [P, DC, S])
        fh = sb("fh", [P, DC, S])
        fh_p = pair("fh", [P, DC, S])
        x4 = sb("x4", [P, QT, D])
        x4T = sb("x4T", [P, DC, S])
        rows = sb("rows", [P, QT, ROW])
        stat = [sb(f"stat{n}", [P, QT, 6]) for n in range(5)]
        mv = [sb(f"mv{n}", [P, QT, 2]) for n in range(5)]
        nb = [sb(f"nb{n}", [P, QT]) for n in range(5)]
        ve = [sb(f"ve{n}", [P, QT]) for n in range(5)]
        rstd = [sb(f"rstd{n}", [P, QT]) for n in range(5)]
        nz_k = [sb("nz_k1", [P, QT], F16), sb("nz_k2", [P, KT], F16)]
        length = [sb(f"length{n}", [P, 1]) for n in range(2)]
        top = [sb(f"top{n}", [P, QT]) for n in range(2)]
        ntop = [sb(f"ntop{n}", [P, QT]) for n in range(2)]
        total = [sb(f"total{n}", [P, QT]) for n in range(2)]
        some = [sb(f"some{n}", [P, 1]) for n in range(2)]
        full = [sb(f"full{n}", [P, QT]) for n in range(2)]
        inv = [sb(f"inv{n}", [P, QT]) for n in range(2)]
        lg = sb("lg", [P, QT, E])
        best = sb("best", [P, QT, 8])
        besti = sb("besti", [P, QT, 8], U32)
        pick = sb("pick", [P, QT, 2])
        hot = sb("hot", [P, QT, 2, E], F16)
        rsel = sb("rsel", [P, QT, 2, E])
        rank = sb("rank", [P, QT, 2])
        gap = sb("gap", [P, QT])
        egap = sb("egap", [P, QT])
        den = sb("den", [P, QT])
        gate = sb("gate", [P, QT, 2])
        keep = sb("keep", [P, QT, 2])
        over = sb("over", [P, QT, 2])
        slotf = sb("slotf", [P, QT, 2])
        slot = sb("slot", [P, QT * 2], I32)
        newly = sb("newly", [P, 2 * E])

        raw_w = {n: sm2[:, i // 2, (i % 2) * DC * D:(i % 2 + 1) * DC * D].rearrange("p (c d) -> p c d", c=DC)
                 for i, n in enumerate(("wq1", "wk1", "wq2", "wk2", "wv1", "wv2", "fc1", "fc2"))}
        wT = {n: t[:, :, 0:D] for n, t in (("wq1", fh), ("wk1", x4T))}
        wT["wq2"], wT["wk2"] = fh[:, :, D:2 * D], x4T[:, :, D:2 * D]
        blank = rows[:, 0, :]

        first_raw = g["raw_weights"](sm2[:].rearrange("p t k -> p (t k)"))

        pool_t = [psum(f"bank_t{n}", [P, 512]) for n in range(2)]
        pool_m = [psum(f"bank_m{n}", [P, 512]) for n in range(2)]
        pool_s = [psum(f"bank_s{n}", [P, 1024]) for n in range(2)]
        banks = {"T": pool_t, "M": pool_m, "S": pool_s}

        ev = {n: sem(n) for n in SIGNALS}
        qk1_in, setup_in, vec_in = sem("qk1_in"), sem("setup_in"), sem("vec_in")
        const_p, const_v = sem("const_p"), sem("const_v")
        wT_p, wT_v, a_p, a_v, gates = sem("wT_p"), sem("wT_v"), sem("a_p"), sem("a_v"), sem("gates")
        blank_out, settled = sem("blank_out"), sem("settled")
        DMA_EVENTS = ("x_in", "ctx_in", "xr_in", "x4_out", "dispatched")

        def unit(name):
            return 16 if name in DMA_EVENTS else 1

        def done(name, ins):
            ins.then_inc(ev[name], unit(name))

        def need(eng, name, it, k=None):
            n, k = SIGNALS[name], SIGNALS[name] - 1 if k is None else k
            eng.wait_ge(ev[name], it.times(n * unit(name), 1 + (k + 1) * unit(name)))

        def before(eng, name, it):
            eng.wait_ge(ev[name], it.times(SIGNALS[name] * unit(name), 1))

        def live(i, step):
            return 0 <= i - LAG[step] < B

        def fills_in(pool, i):
            return [(s, k) for s in LAG if live(i, s) for k in range(FILLS[pool].get(s, 0))]

        def fill(pool, step, k, i):
            index = fills_in(pool, i).index((step, k))
            assert len(fills_in(pool, i)) % 2 == 0
            return index

        def bank_of(pool, step, k, at):
            return banks[pool][fill(pool, step, k, at[0]) % 2]

        def open_fill(pe, pool, step, k, at):
            i, j = at
            index = fill(pool, step, k, i)
            if index >= 2:
                was, back = fills_in(pool, i)[index - 2], 0
            else:
                back = next((n for n in range(1, i + 1) if fills_in(pool, i - n)), None)
                if back is None:
                    return banks[pool][index % 2]
                was = fills_in(pool, i - back)[index - 2]
                assert j is None or (back == 1 and was == fills_in(pool, i)[index - 2])
            event, numbers = EMPTIED[was[0]]
            if was[0] == "b_len" or was[0] == "a_len":
                event, number = event[was[1]], 0
            else:
                number = numbers[was[1]]
            need(pe, event, Iteration(j, i - back - LAG[was[0]]), number)
            return banks[pool][index % 2]

        def one(eng, body, i, j, steps):
            for s in steps:
                if live(i, s):
                    body(s, Iteration(j, i - LAG[s]), (i, j))

        def begin(eng, body, *steps):
            one(eng, body, 0, None, steps)

        def walk(eng, body):
            for i in range(DEPTH):
                one(eng, body, i, None, [s for s in LAG if i > 0 or s not in BEGIN])
            with eng.Fori(0, B - DEPTH) as j:
                one(eng, body, DEPTH, j, LAG)
            for i in range(B, B + DEPTH):
                one(eng, body, i, None, LAG)

        def credit(eng, names):
            for n in names:
                if n != "dispatched":
                    eng.sem_inc(ev[n], 1)

        def settle(eng):
            eng.sem_inc(settled, 1)

        def batch(dram, it):
            view = dram.rearrange("b (t p) d -> b p t d", p=P)
            return view[it.offset] if it.j is None else view[it.j + it.offset]

        def out_rows(it):
            view = out[0:T, :].rearrange("(b t p) d -> b p t d", p=P, t=QT)
            return view[it.offset] if it.j is None else view[it.j + it.offset]

        names = list(SIGNALS)
        block = ctx.enter_context(nc.Block())

        @block.sync
        def _(sp):
            def step(s, it, at):
                if s == "z_ln0":
                    before(sp, "xn", it)
                    done("x_in", sp.dma_start(x_sb[:], batch(x, it)))
                if s == "b_c2T0" and it.j is None and it.offset == B - 1:
                    need(sp, "p2T_p", it)
                    g["load_expert"](sp, 0, first_raw)
                if s == "b_ctx0":
                    before(sp, "ctx_l", it)
                    before(sp, "ctxT_p", it)
                    done("ctx_in", sp.dma_start(c_sb[:], batch(ctx_in, it)))
                if s == "c_x3T":
                    before(sp, "x4", it)
                    done("xr_in", sp.dma_start(xr[:], batch(x, it)))
                if s == "c_x4":
                    need(sp, "x4", it)
                    done("x4_out", sp.dma_start(out_rows(it), x4[:]))

            credit(sp, names[0:4])
            begin(sp, step, "z_ln0", "z_n0", "a_xnT")
            for n in ("wq1", "wk1", "wq2", "wk2", "wv1", "wv2", "fc1", "fc2"):
                dram = {"wq1": wq1, "wk1": wk1, "wq2": wq2, "wk2": wk2, "wv1": wv1, "wv2": wv2, "fc1": fc1_w,
                        "fc2": fc2_w}[n]
                sp.dma_start(raw_w[n], dram.rearrange("(c p) d -> p c d", p=P)).then_inc(
                    qk1_in if n in ("wq1", "wk1") else setup_in, 16)
            sp.dma_start(b1_raw[0:E * FC, :], b1.rearrange("e (c p) -> (e c) p", p=P)).then_inc(vec_in, 16)
            sp.dma_start(b1_raw[E * FC:, :], fc1_b.rearrange("(c p) -> c p", p=P)).then_inc(vec_in, 16)
            sp.dma_start(wr_sb[:], wr.rearrange("(c p) e -> p c e", p=P)).then_inc(vec_in, 16)
            for v, n in ((ln1_g, "g1"), (ln1_b, "o1"), (ln2_g, "g2"), (ln2_b, "o2"), (ln3_g, "g3"), (ln3_b, "o3"),
                         (fc2_b, "fc2_b")):
                sp.dma_start(vec[n][:], v.partition_broadcast(P)).then_inc(vec_in, 16)
            sp.dma_start(gates_in[:, 0:1], g_x.partition_broadcast(P)).then_inc(vec_in, 16)
            sp.dma_start(gates_in[:, 1:2], g_f.partition_broadcast(P)).then_inc(vec_in, 16)

            walk(sp, step)
            sp.wait_ge(ev["x4_out"], 1 + 16 * B)

        @block.gpsimd
        def _(pool):
            NORM_OF = {"z_ln0": 0, "a_ln1": 1, "b_ln2": 2, "c_ln3": 3, "c_ln4": 4}

            def step(s, it, at):
                if s == "b_split":
                    need(pool, "ctx_in", it)
                    need(pool, "ctx_h", it)
                    before(pool, "c2T_p", it)
                    done("ctx_l", pool.tensor_tensor(c_p[1][:], c_sb[:], c_p[0][:], ALU.subtract))
                if s == "c_x3T":
                    need(pool, "x3", it)
                    before(pool, "y3", it)
                    fb = vec["fc2_b"][:].unsqueeze(1).to_broadcast([P, QT, D])
                    done("x3b", pool.tensor_tensor(x3b[:], x3[:], fb, ALU.add))
                if s == "z_n0":
                    need(pool, "xn_h", it)
                    before(pool, "c1T_p", it)
                    done("xn_l", pool.tensor_tensor(xn_p[1][:], xn[:], xn_p[0][:], ALU.subtract))
                if s == "c_fc1":
                    for c in range(DC):
                        need(pool, "fh_h", it, c)
                        if c == 0:
                            before(pool, "fc2_p", it)
                        done("fh_l", pool.tensor_tensor(fh_p[1][:, c, :], fh[:, c, :], fh_p[0][:, c, :],
                                                        ALU.subtract))
                if s == "c_xr":
                    need(pool, "xr_in", it)
                    before(pool, "x4", it)
                    ob = vec["o3"][:].unsqueeze(1).to_broadcast([P, QT, D])
                    done("xro", pool.tensor_tensor(xr[:], xr[:], ob, ALU.add))
                if s in NORM_OF:
                    n = NORM_OF[s]
                    need(pool, f"mv{n}", it)
                    done(f"ve{n}", pool.tensor_tensor(ve[n][:], mv[n][:, :, 1], eps[:], ALU.add))
                    need(pool, f"ve{n}", it)
                    done(f"rstd{n}", pool.tensor_tensor(rstd[n][:], ve[n][:], neg_half[:], ALU.pow))
                if s == "a_n1":
                    need(pool, "yn1", it)
                    sc = vec["g1"][:].unsqueeze(1).to_broadcast([P, QT, D])
                    of = vec["o1"][:].unsqueeze(1).to_broadcast([P, QT, D])
                    done("yg1", pool.tensor_tensor(y1[:], y1[:], sc, ALU.mult))
                    need(pool, "yg1", it)
                    before(pool, "y2", it)
                    done("x2", pool.tensor_tensor(x2[:], y1[:], of, ALU.add))
                if s == "b_n2" and it.j is None and it.offset == 0:
                    pool.wait_ge(blank_out, 32)
                if s.startswith("d_send"):
                    t = int(s[-1])
                    need(pool, "slots", it)
                    need(pool, "rowx", it)
                    settle(pool)
                    for n in (2 * t, 2 * t + 1):
                        done("dispatched", pool.indirect_dma_start(
                            xs, bass.IndirectOffsetOnAxis(ap=slot[:, n:n + 1].bitcast(U32), axis=0),
                            rows[:, t, :], None, bounds_check=E * SLOTS - 1, oob_is_err=False))
                if s == "c_n4":
                    SENT = 16 * 2 * QT
                    if it.j is not None or it.offset > 0:
                        pool.wait_ge(ev["dispatched"], it.times(SENT, 0))
                    pool.sem_inc(ev["rows_gone"], 1)

            credit(pool, names[4:20])
            pool.memset(ident[:], 0.0).then_inc(const_p, 1)
            pool.memset(tri[:], 1.0).then_inc(const_p, 1)
            pool.memset(ones[:], 1.0).then_inc(const_p, 1)
            pool.memset(neg_half[:], -0.5).then_inc(const_p, 1)
            pool.memset(eps[:], EPS).then_inc(const_p, 1)
            pool.memset(taken[:], 0.0).then_inc(const_p, 1)
            pool.memset(rows[:], 0.0).then_inc(const_p, 1)
            for t in range(QT):
                pool.iota(key1[:, q_seg[t]:q_seg[t] + P * (t + 1)], [[1, P * (t + 1)]], base=0, channel_multiplier=0,
                          allow_small_or_imprecise_dtypes=True).then_inc(const_p, 1)
            pool.iota(key2[:], [[1, SK]], base=0, channel_multiplier=0,
                      allow_small_or_imprecise_dtypes=True).then_inc(const_p, 1)
            pool.iota(iota_e[:], [[1, E]], base=0, channel_multiplier=0,
                      allow_small_or_imprecise_dtypes=True).then_inc(const_p, 1)
            pool.iota(slot_off[:], [[0, QT], [CAP, 2]], base=-1, channel_multiplier=0,
                      allow_small_or_imprecise_dtypes=True).then_inc(const_p, 1)
            pool.iota(token[:], [[P, QT]], base=0, channel_multiplier=1,
                      allow_small_or_imprecise_dtypes=True).then_inc(const_p, 1)
            pool.wait_ge(const_p, 11 + QT)
            pool.affine_select(out=ident[:], in_=ident[:], compare_op=ALU.not_equal, fill=1.0, base=0,
                               pattern=[[-1, P]], channel_multiplier=1).then_inc(const_p, 1)
            pool.affine_select(out=tri[:], in_=tri[:], compare_op=ALU.is_ge, fill=0.0, base=0,
                               pattern=[[1, P]], channel_multiplier=-1).then_inc(const_p, 1)
            for t in range(QT):
                d = key1[:, q_seg[t] + P * t:q_seg[t] + P * (t + 1)]
                pool.affine_select(out=d, in_=d, compare_op=ALU.is_ge, fill=NEVER, base=0, pattern=[[-1, P]],
                                   channel_multiplier=1).then_inc(const_p, 1)
            pool.iota(blank[:, TOKEN:TOKEN + 1].bitcast(I32), [[0, 1]], base=T,
                      channel_multiplier=1).then_inc(const_p, 1)
            begin(pool, step, "z_ln0", "z_n0", "a_xnT")
            pool.wait_ge(const_p, 14 + 2 * QT)
            pool.dma_start(xs.rearrange("(c p) d -> p c d", p=P),
                           blank.unsqueeze(1).to_broadcast([P, E * SLOTS // P, ROW])).then_inc(blank_out, 16)
            pool.dma_start(out[T:T + P, :], blank[:, 0:D]).then_inc(blank_out, 16)
            pool.wait_ge(gates, 1)
            pool.wait_ge(vec_in, 16 * 12)
            for n in ("g3", "o3"):
                pool.tensor_scalar(vec[n][:], vec[n][:], tanh_g[:, 0:1], None, ALU.mult).then_inc(const_p, 1)
            pool.wait_ge(const_p, 16 + 2 * QT)

            walk(pool, step)
            pool.wait_ge(ev["dispatched"], 16 * 2 * QT * B)

        @block.tensor
        def _(pe):
            credit(pe, names[20:40])

            def part(p, *i):
                return p[0][i], p[1][i]

            def turn(src, c, tiles, pool, step, k, at):
                bank = open_fill(pe, pool, step, k, at)
                for n, t in enumerate(tiles):
                    m = pe.transpose(bank[:, n * P:(n + 1) * P], src[:, t, c * P:(c + 1) * P], ident[:])
                return m

            def project(w, xT, dst, at, s, ready, srcs, it):
                for c in range(DC):
                    for n in srcs:
                        need(pe, n, it)
                    bank = open_fill(pe, "M", s, c, at)
                    for d in range(DC):
                        m = mm3(pe, bank[:], part(w, slice(None), d, slice(c * P, (c + 1) * P)),
                                part(xT, slice(None), d, slice(None)), d == 0, d == DC - 1)
                    done(ready, m)

            def back(xT, w, at, s, ready, it):
                for h in range(QT // 2):
                    bank = open_fill(pe, "M", s, h, at)
                    for n in range(2):
                        t = 2 * h + n
                        for d in range(DC):
                            m = mm3(pe, bank[:, n * D:(n + 1) * D], part(xT, slice(None), d, slice(t * P, (t + 1) * P)),
                                    part(w, slice(None), d, slice(None)), d == 0, d == DC - 1)
                    done(ready, m)

            def row0(kT, qT, tiles, s, at, ready, n, ones_ready, len_ready, it):
                bank = open_fill(pe, "M", s, 0, at)
                for t in range(tiles):
                    for d in range(DC):
                        m = mm3(pe, bank[:, t:t + 1], part(kT, slice(None), d, slice(t * P, (t + 1) * P)),
                                part(qT, slice(None), d, slice(0, 1)), d == 0, d == DC - 1)
                done(ready, m)
                need(pe, ones_ready, it)
                bank = open_fill(pe, "M", s, 1, at)
                done(len_ready, pe.matmul(bank[:, 0:tiles], ones[:], nz_k[n][:], start=True, stop=True))

            def step(s, it, at):
                if s in ("b_ctx0", "b_ctx1"):
                    need(pe, "ctx_in", it)
                    done("ctxT_p", turn(c_sb, int(s[-1]), range(KT), "S", s, 0, at))
                if s == "c_x3T":
                    need(pe, "x3", it)
                    for c in range(DC):
                        done("x3T_p", turn(x3, c, range(QT), "T", s, c, at))
                if s == "b_q2T":
                    project(a2, x2T, q2T, at, s, "q2T_p", ["x2T_l"], it)
                if s == "c_fc1":
                    project(fc1_p, x3T, fh, at, s, "fc1_p", ["x3T_l"], it)
                if s == "b_len":
                    need(pe, "q2T_l", it)
                    need(pe, "ctxT_l", it)
                    row0(ctxT, q2T, KT, s, at, "e2_p", 1, "nz2", "len2_p", it)
                if s == "a_xnT":
                    need(pe, "xn", it)
                    for c in range(DC):
                        done("xnT_p", turn(xn, c, range(QT), "T", s, c, at))
                if s in ("b_s2a", "b_s2b"):
                    for n in range(2):
                        t = (0 if s == "b_s2a" else 2) + n
                        bank = open_fill(pe, "S", s, n, at)
                        for h in range(2):
                            for d in range(DC):
                                m = mm3(pe, bank[:, h * 512:(h + 1) * 512],
                                        part(q2T, slice(None), d, slice(t * P, (t + 1) * P)),
                                        part(ctxT, slice(None), d, slice(h * 512, (h + 1) * 512)), d == 0, d == DC - 1)
                        done("s2_p", m)
                if s == "c_fc2":
                    need(pe, "fh_l", it)
                    back(fh_p, fc2_p, at, s, "fc2_p", it)
                if s == "a_q1T":
                    project(a1, xnT, q1T, at, s, "q1T_p", ["xnT_l"], it)
                if s == "a_len":
                    need(pe, "q1T_l", it)
                    row0(xnT, q1T, QT, s, at, "e1_p", 0, "nz1", "len1_p", it)
                if s == "a_s1":
                    for n, tiles in enumerate(((0, 1, 2), (3,))):
                        bank = open_fill(pe, "S", s, n, at)
                        for t in tiles:
                            w = P * (t + 1)
                            o = q_seg[t] + (P if t == 2 else 0) - (q_seg[3] if t == 3 else 0)
                            for d in range(DC):
                                m = mm3(pe, bank[:, o:o + w], part(q1T, slice(None), d, slice(t * P, (t + 1) * P)),
                                        part(xnT, slice(None), d, slice(0, w)), d == 0, d == DC - 1)
                        done("s1_p", m)
                if s in ("b_p2T0", "b_p2T1"):
                    need(pe, "p2", it)
                    for n in range(2):
                        k0 = KT // 2 * int(s[-1]) + 2 * n
                        bank = open_fill(pe, "S", s, n, at)
                        for k in (k0, k0 + 1):
                            for t in range(QT):
                                o = (k - k0) * S + t * P
                                m = pe.transpose(bank[:, o:o + P], sm2[:, t, k * P:(k + 1) * P], ident[:])
                        done("p2T_p", m)
                if s == "c_x4T":
                    need(pe, "rowx", it)
                    for c in range(DC):
                        done("x4T_p", turn(rows, c, range(QT), "T", s, c, at))
                if s in ("b_c2T0", "b_c2T1"):
                    c = int(s[-1])
                    need(pe, "ctx_l", it)
                    bank = open_fill(pe, "M", s, 0, at)
                    for k in range(KT):
                        if c == 0:
                            need(pe, "p2T_l", it, k // 2)
                        m = mm3(pe, bank[:], part(c_p, slice(None), k, slice(c * P, (c + 1) * P)),
                                part(p2T, slice(None), k, slice(None)), k == 0, k == KT - 1)
                    done("c2T_p", m)
                if s == "c_logits":
                    need(pe, "x4T", it)
                    bank = open_fill(pe, "M", s, 0, at)
                    for t in range(QT):
                        for d in range(DC):
                            m = pe.matmul(bank[:, t * E:(t + 1) * E], x4T[:, d, t * P:(t + 1) * P], wr_sb[:, d, :],
                                          start=d == 0, stop=d == DC - 1)
                    done("logits_p", m)
                if s == "a_p1T":
                    need(pe, "p1", it)
                    for k in range(QT):
                        bank = open_fill(pe, "T", s, k, at)
                        for n, t in enumerate(range(k, QT)):
                            o = q_seg[t] + k * P
                            m = pe.transpose(bank[:, n * P:(n + 1) * P], sm1[:, o:o + P], ident[:])
                        done("p1T_p", m)
                if s == "c_rank":
                    need(pe, "route", it, 5)
                    bank = open_fill(pe, "M", s, 0, at)
                    w = 2 * E
                    hot2 = hot[:].rearrange("p t k e -> p t (k e)")
                    out_ = bank[:, 0:QT * w].rearrange("p (t w) -> p t w", t=QT)
                    pe.matmul(out_, tri[:], hot2, start=True, stop=False)
                    for t in range(QT - 1):
                        pe.matmul(out_[:, t + 1:, :], ones[:], hot2[:, t:t + 1, :].to_broadcast([P, QT - 1 - t, w]),
                                  start=False, stop=False)
                    done("rank_p", pe.matmul(out_, ones[:], taken[:].unsqueeze(1).to_broadcast([P, QT, w]),
                                             start=False, stop=True))
                if s == "a_c1T":
                    need(pe, "xn_l", it)
                    for c in range(DC):
                        bank = open_fill(pe, "M", s, c, at)
                        for k in range(QT):
                            if c == 0:
                                need(pe, "p1T_l", it, k)
                            w = P * (QT - k)
                            m = mm3(pe, bank[:, k * P:512], part(xn_p, slice(None), k, slice(c * P, (c + 1) * P)),
                                    part(p1T, slice(None), slice(k_seg[k], k_seg[k] + w)), k == 0, k == QT - 1)
                        done("c1T_p", m)
                if s == "b_z2":
                    need(pe, "c2T_l", it)
                    back(c2T, wv2_p, at, s, "z2_p", it)
                if s == "a_z1":
                    if it.j is None and it.offset == 0:
                        pe.wait_ge(const_v, 4)
                    need(pe, "c1T_l", it)
                    back(c1T, wv1_p, at, s, "z1_p", it)
                if s == "a_x2T":
                    need(pe, "x2", it)
                    for c in range(DC):
                        done("x2T_p", turn(x2, c, range(QT), "T", s, c, at))

            pe.wait_ge(const_p, 12 + QT)
            pe.wait_ge(qk1_in, 16 * 2)
            for i, n in enumerate(("wq1", "wk1", "wq2", "wk2")):
                if i == 2:
                    pe.wait_ge(setup_in, 16 * 6)
                if i >= 2:
                    pe.wait_ge(wT_v, i - 1)
                for eb in range(DC):
                    for db in range(DC):
                        m = pe.transpose(pool_t[i % 2][:, eb * D + db * P:eb * D + (db + 1) * P],
                                         raw_w[n][:, db, eb * P:(eb + 1) * P], ident[:])
                m.then_inc(wT_p, 1)
            pe.wait_ge(vec_in, 16 * 12)
            nb = E * FC + DC
            pe.transpose(pool_m[0][:, 0:nb], b1_raw[:], ident[0:nb, 0:nb]).then_inc(wT_p, 1)
            pe.wait_ge(wT_v, 4)
            for i, (q, k) in enumerate((("wq1", "wk1"), ("wq2", "wk2"))):
                if i == 1:
                    begin(pe, step, "a_xnT")
                pe.wait_ge(wT_v, 2 * i + 2)
                for db in range(DC):
                    for eb in range(DC):
                        m = pe.matmul(pool_s[i][:, db * D:(db + 1) * D], wT[q][:, eb, db * P:(db + 1) * P],
                                      wT[k][:, eb, :], start=eb == 0, stop=eb == DC - 1)
                m.then_inc(a_p, 1)
            pe.wait_ge(a_v, 2)
            pe.wait_ge(wT_v, 5)

            walk(pe, step)

        EVACUATE = {
            "b_ctx0": ("S", "ctxT_p", ctxT, "ctxT_h", "ctxT_l", "s2_p"),
            "b_ctx1": ("S", "ctxT_p", ctxT, "ctxT_h", "ctxT_l", "s2_p"),
            "c_x3T": ("T", "x3T_p", x3T, "x3T_h", "x3T_l", "fc1_p"),
            "b_q2T": ("M", "q2T_p", q2T, "q2T_h", "q2T_l", "s2_p"),
            "a_xnT": ("T", "xnT_p", xnT, "xnT_h", "xnT_l", "s1_p"),
            "a_q1T": ("M", "q1T_p", q1T, "q1T_h", "q1T_l", "s1_p"),
            "b_p2T0": ("S", "p2T_p", p2T, "p2T_h", "p2T_l", "c2T_p"),
            "b_p2T1": ("S", "p2T_p", p2T, "p2T_h", "p2T_l", "c2T_p"),
            "b_c2T0": ("M", "c2T_p", c2T, "c2T_h", "c2T_l", "z2_p"),
            "b_c2T1": ("M", "c2T_p", c2T, "c2T_h", "c2T_l", "z2_p"),
            "a_p1T": ("T", "p1T_p", p1T, "p1T_h", "p1T_l", "c1T_p"),
            "a_c1T": ("M", "c1T_p", c1T, "c1T_h", "c1T_l", "z1_p"),
            "a_x2T": ("T", "x2T_p", x2T, "x2T_h", "x2T_l", "q2T_p"),
        }

        def number(s, k):
            return k + {"b_c2T1": 1, "b_ctx1": 1, "b_p2T1": 2}.get(s, 0)

        def where(s, k, t):
            if s in ("b_ctx0", "b_ctx1"):
                return t[:, int(s[-1]), :], SK
            if s in ("b_p2T0", "b_p2T1"):
                n = number(s, k)
                return t[:, 2 * n:2 * n + 2, :].rearrange("p k q -> p (k q)"), 2 * S
            if s == "a_p1T":
                w = P * (QT - k)
                return t[:, k_seg[k]:k_seg[k] + w], w
            return t[:, number(s, k), :], 512

        @block.scalar
        def _(act):
            credit(act, names[40:70])
            NORMS = {"z_n0": (0, x_sb, xn, "xn"), "a_n1": (1, y1, y1, "yn1"), "c_n4": (4, x4, rows, "rowx")}

            def step(s, it, at):
                if s in EVACUATE:
                    pool, filled, t, high, _, reader = EVACUATE[s]
                    for k in range(FILLS[pool][s]):
                        need(act, filled, it, number(s, k))
                        if k == 0:
                            before(act, reader, it)
                        dst, w = where(s, k, t[0])
                        done(high, act.activation(dst, bank_of(pool, s, k, at)[:, 0:w], ACT.Copy))
                if s == "b_split":
                    need(act, "ctx_in", it)
                    before(act, "c2T_p", it)
                    done("ctx_h", act.activation(c_p[0][:], c_sb[:], ACT.Copy))
                for ln, (n, src, dst, ready) in NORMS.items():
                    if s == ln:
                        need(act, f"nb{n}", it)
                        if n == 0:
                            before(act, "y1", it)
                            before(act, "xn_l", it)
                            before(act, "xnT_p", it)
                        if n == 4:
                            need(act, "rows_gone", it)
                        for t in range(QT):
                            m = act.activation(dst[:, t, 0:D], src[:, t, :], ACT.Identity, bias=nb[n][:, t:t + 1],
                                               scale=rstd[n][:, t:t + 1])
                        done(ready, m)
                if s == "z_n0":
                    need(act, "xn", it)
                    before(act, "c1T_p", it)
                    done("xn_h", act.activation(xn_p[0][:], xn[:], ACT.Copy))
                if s == "c_fc1":
                    for c in range(DC):
                        need(act, "fc1_p", it, c)
                        before(act, "fh_l", it)
                        done("fh", act.activation(fh[:, c, :], bank_of("M", s, c, at)[:], ACT.Relu,
                                                  bias=b1T[:, E * FC + c:E * FC + c + 1]))
                        need(act, "fh", it, c)
                        before(act, "fc2_p", it)
                        done("fh_h", act.activation(fh_p[0][:, c, :], fh[:, c, :], ACT.Copy))
                if s in ("b_s2a", "b_s2b"):
                    b0 = 0 if s == "b_s2a" else 2
                    need(act, "nmax2", it, b0 // 2)
                    for t in (b0, b0 + 1):
                        done("p2", act.activation(sm2[:, t, :], sm2[:, t, :], ACT.Exp, bias=ntop[1][:, t:t + 1],
                                                  scale=SCALE, accum_out=total[1][:, t:t + 1]))
                if s == "a_s1":
                    need(act, "nmax1", it)
                    for t in range(QT):
                        o, w = q_seg[t], P * (t + 1)
                        done("p1", act.activation(sm1[:, o:o + w], sm1[:, o:o + w], ACT.Exp,
                                                  bias=ntop[0][:, t:t + 1], scale=SCALE,
                                                  accum_out=total[0][:, t:t + 1]))
                if s == "c_ln3" and it.j is None and it.offset == B - 1:
                    act.wait_ge(g["w_in"], g["W_IN"])
                    act.activation(g["w1_first"][0][:], first_raw[0], ACT.Copy).then_inc(g["w_split"], 1)
                    act.activation(g["w2_first"][0][:], first_raw[1], ACT.Copy).then_inc(g["w_split"], 1)
                if s == "c_x4T":
                    before(act, "logits_p", it)
                    for c in range(DC):
                        need(act, "x4T_p", it, c)
                        done("x4T", act.activation(x4T[:, c, :], bank_of("T", s, c, at)[:], ACT.Copy))
                if s == "c_rank":
                    need(act, "gap", it)
                    done("gate", act.activation(egap[:], gap[:], ACT.Exp))

            begin(act, step, "z_ln0", "z_n0")
            act.wait_ge(vec_in, 16 * 12)
            act.activation(tanh_g[:], gates_in[:], ACT.Tanh).then_inc(gates, 1)
            begin(act, step, "a_xnT")

            walk(act, step)

        @block.vector
        def _(dve):
            credit(dve, names[70:])
            def split_weights():
                dve.wait_ge(setup_in, 16 * 6)
                for n, p in (("wv1", wv1_p), ("wv2", wv2_p), ("fc1", fc1_p), ("fc2", fc2_p)):
                    ins = dve.tensor_copy(p[0][:], raw_w[n])
                ins.then_inc(const_v, 1)
                dve.wait_ge(const_v, 3)
                for n, p in (("wv1", wv1_p), ("wv2", wv2_p), ("fc1", fc1_p), ("fc2", fc2_p)):
                    ins = dve.tensor_tensor(p[1][:], raw_w[n], p[0][:], ALU.subtract)
                ins.then_inc(const_v, 1)

            def norm_stats(n, it, src):
                for t in range(QT):
                    done(f"bn{n}", dve.bn_stats(stat[n][:, t, :], src[:, t, :]))
                need(dve, f"bn{n}", it)
                settle(dve)
                for t in range(QT):
                    ins = dve.bn_aggr(mv[n][:, t, :], stat[n][:, t, :])
                done(f"mv{n}", ins)
                if n in (0, 1, 4):
                    need(dve, f"rstd{n}", it)
                    done(f"nb{n}", dve.scalar_tensor_tensor(nb[n][:], mv[n][:, :, 0], -1.0, rstd[n][:], ALU.mult,
                                                            ALU.mult))

            def normalise(n, it, src, dst, scale, offset, scaled, ready):
                need(dve, f"mv{n}", it)
                for t in range(QT):
                    ins = dve.scalar_tensor_tensor(src[:, t, :], src[:, t, :], mv[n][:, t, 0:1], scale[:],
                                                   ALU.subtract, ALU.mult)
                done(scaled, ins)
                need(dve, scaled, it)
                need(dve, f"rstd{n}", it)
                for t in range(QT):
                    ins = dve.scalar_tensor_tensor(dst[:, t, :], src[:, t, :], rstd[n][:, t:t + 1], offset(t),
                                                   ALU.mult, ALU.add)
                done(ready, ins)

            def count(n, tiles, s, at, it, width, key, mask):
                e, nz, lp, ln, mk = ("e1_p", "nz1", "len1_p", "len1", "mask1") if n == 0 else \
                    ("e2_p", "nz2", "len2_p", "len2", "mask2")
                need(dve, e, it)
                ins = dve.tensor_scalar(nz_k[n][:], bank_of("M", s, 0, at)[:, 0:tiles], 0.0, None, ALU.not_equal)
                done(nz, ins)
                need(dve, lp, it)
                ins = dve.tensor_reduce(length[n][:], bank_of("M", s, 1, at)[:, 0:tiles], AX.X, ALU.add)
                done(ln, ins)
                need(dve, ln, it)
                done(mk, dve.tensor_scalar(mask[:], key[:], length[n][:], MASKED, ALU.is_ge, ALU.mult))

            def invert(n, it, last_total):
                name = f"inv{n + 1}"
                need(dve, last_total, it)
                done(name, dve.tensor_scalar(some[n][:], length[n][:], 1.0, None, ALU.min))
                need(dve, name, it, 0)
                done(name, dve.tensor_scalar(full[n][:], total[n][:], some[n][:], None, ALU.mult))
                need(dve, name, it, 1)
                done(name, dve.reciprocal(inv[n][:], full[n][:]))
                need(dve, name, it, 2)

            def step(s, it, at):
                if s in EVACUATE:
                    pool, _, t, high, low, _ = EVACUATE[s]
                    for k in range(FILLS[pool][s]):
                        need(dve, high, it, number(s, k))
                        dst, w = where(s, k, t[1])
                        hi, _ = where(s, k, t[0])
                        ins = dve.tensor_tensor(dst, bank_of(pool, s, k, at)[:, 0:w], hi, ALU.subtract)
                        done(low, ins)
                if s == "z_ln0":
                    need(dve, "x_in", it)
                    norm_stats(0, it, x_sb)
                if s == "b_len":
                    count(1, KT, s, at, it, SK, key2, mask2)
                if s == "a_len":
                    count(0, QT, s, at, it, SELF_W, key1, mask1)
                if s in ("b_s2a", "b_s2b"):
                    b0 = 0 if s == "b_s2a" else 2
                    if b0 == 0:
                        need(dve, "mask2", it)
                        before(dve, "p2T_p", it)
                    for n in range(2):
                        t = b0 + n
                        need(dve, "s2_p", it, t)
                        settle(dve)
                        ins = dve.tensor_tensor_reduce(sm2[:, t, :], bank_of("S", s, n, at)[:], mask2[:], 1.0,
                                                       -3.4e38, ALU.add, ALU.max, top[1][:, t:t + 1])
                        done("sm2", ins)
                    need(dve, "sm2", it, b0 + 1)
                    done("nmax2", dve.tensor_scalar(ntop[1][:, b0:b0 + 2], top[1][:, b0:b0 + 2], -SCALE, None,
                                                    ALU.mult))
                if s == "a_s1":
                    need(dve, "mask1", it)
                    for t in range(QT):
                        if t in (0, 3):
                            need(dve, "s1_p", it, t // 3)
                            settle(dve)
                        bank = bank_of("S", s, t // 3, at)
                        w = P * (t + 1)
                        o = q_seg[t] + (P if t == 2 else 0) - (q_seg[3] if t == 3 else 0)
                        done("sm1", dve.tensor_tensor_reduce(
                            sm1[:, q_seg[t]:q_seg[t] + w], bank[:, o:o + w], mask1[:, q_seg[t]:q_seg[t] + w], 1.0,
                            -3.4e38, ALU.add, ALU.max, top[0][:, t:t + 1]))
                    need(dve, "sm1", it)
                    done("nmax1", dve.tensor_scalar(ntop[0][:], top[0][:], -SCALE, None, ALU.mult))
                    if it.j is None and it.offset == 0:
                        split_weights()
                if s == "c_fc2":
                    need(dve, "x3b", it)
                    before(dve, "x4_out", it)
                    for h in range(2):
                        need(dve, "fc2_p", it, h)
                        src = bank_of("M", s, h, at)[:].rearrange("p (t d) -> p t d", t=2)
                        ins = dve.tensor_tensor(x4[:, 2 * h:2 * h + 2, :], src, x3b[:, 2 * h:2 * h + 2, :], ALU.add)
                        done("y3", ins)
                if s == "c_ln3":
                    need(dve, "y3", it)
                    norm_stats(3, it, x4)
                if s == "b_n2":
                    normalise(2, it, x3, x3, vec["g2"], lambda t: vec["o2"][:], "yg2", "x3")
                if s == "c_x4":
                    if it.j is None and it.offset == 0:
                        dve.wait_ge(const_p, 16 + 2 * QT)
                    need(dve, "xro", it)
                    normalise(3, it, x4, x4, vec["g3"], lambda t: xr[:, t, :], "yg3", "x4")
                if s == "c_ln4":
                    need(dve, "x4", it)
                    norm_stats(4, it, x4)
                if s in ("b_z2", "a_z1"):
                    n, z, y, res, dst = (1, "z2_p", "y2", x2, x3) if s == "b_z2" else (0, "z1_p", "y1", xn, y1)
                    invert(n, it, "p2" if n else "p1")
                    if n:
                        before(dve, "x3T_p", it)
                        before(dve, "x3b", it)
                    for t in range(QT):
                        if t % 2 == 0:
                            need(dve, z, it, t // 2)
                        o = (t % 2) * D
                        ins = dve.scalar_tensor_tensor(dst[:, t, :], bank_of("M", s, t // 2, at)[:, o:o + D],
                                                       inv[n][:, t:t + 1], res[:, t, :], ALU.mult, ALU.add)
                        done(y, ins)
                if s == "a_ln1":
                    need(dve, "y1", it)
                    norm_stats(1, it, y1)
                if s == "b_ln2":
                    need(dve, "y2", it)
                    norm_stats(2, it, x3)
                r = [0]

                def link(ins):
                    done("route", ins)
                    need(dve, "route", it, r[0])
                    r[0] += 1

                if s == "c_x4T" and it.j is None and it.offset == B - 1:
                    for n, (part, raw) in enumerate(((g["w1_first"], first_raw[0]), (g["w2_first"], first_raw[1]))):
                        dve.wait_ge(g["w_split"], n + 1)
                        dve.tensor_tensor(part[1][:], raw, part[0][:], ALU.subtract)
                if s == "c_logits":
                    need(dve, "logits_p", it)
                    ins = dve.tensor_copy(lg[:], bank_of("M", s, 0, at)[:, 0:QT * E].rearrange(
                        "p (t e) -> p t e", t=QT))
                    done("logits", ins)
                    need(dve, "logits", it)
                    settle(dve)
                    for t in range(QT):
                        ins = dve.max(best[:, t, :], lg[:, t, :])
                    link(ins)
                    settle(dve)
                    for t in range(QT):
                        ins = dve.max_index(besti[:, t, :], best[:, t, :], lg[:, t, :])
                    link(ins)
                    link(dve.tensor_copy(pick[:], besti[:, :, 0:2]))
                    before(dve, "rank_p", it)
                    for k in range(2):
                        ins = dve.tensor_tensor(hot[:, :, k, :], iota_e[:].unsqueeze(1).to_broadcast([P, QT, E]),
                                                pick[:, :, k:k + 1].to_broadcast([P, QT, E]), ALU.is_equal)
                    link(ins)
                    done("gap", dve.tensor_tensor(gap[:], best[:, :, 1], best[:, :, 0], ALU.subtract))
                    link(dve.tensor_reduce(newly[:], hot[:].rearrange("p t k e -> p (k e) t"), AX.X, ALU.add))
                    link(dve.tensor_copy(rows[:, :, TOKEN].bitcast(I32), token[:]))
                if s == "c_rank":
                    need(dve, "rank_p", it)
                    r[0] = 6
                    bank = bank_of("M", s, 0, at)
                    link(dve.tensor_tensor(rsel[:], bank[:, 0:QT * 2 * E].rearrange(
                        "p (t k e) -> p t k e", t=QT, k=2), hot[:], ALU.mult))
                    ins = dve.tensor_reduce(rank[:], rsel[:], AX.X, ALU.add)
                    ins = dve.tensor_tensor(taken[:], taken[:], newly[:], ALU.add)
                    ins = dve.tensor_scalar(token[:], token[:], float(S), None, ALU.add)
                    link(ins)
                if s == "c_slots":
                    r[0] = 8
                    need(dve, "gate", it)
                    ins = dve.tensor_scalar(den[:], egap[:], 1.0, None, ALU.add)
                    dve.tensor_scalar(keep[:], rank[:], float(CAP), None, ALU.is_le)
                    dve.tensor_scalar(over[:], rank[:], float(CAP), SKIP, ALU.is_gt, ALU.mult)
                    link(dve.scalar_tensor_tensor(slotf[:], pick[:], float(SLOTS), rank[:], ALU.mult, ALU.add))
                    dve.reciprocal(gate[:, :, 0], den[:])
                    link(dve.tensor_tensor(slotf[:], slotf[:], slot_off[:], ALU.add))
                    dve.tensor_tensor(gate[:, :, 1], gate[:, :, 0], egap[:], ALU.mult)
                    link(dve.tensor_tensor(slotf[:], slotf[:], over[:], ALU.add))
                    link(dve.scalar_tensor_tensor(rows[:, :, WEIGHT:WEIGHT + 2], gate[:], tanh_g[:, 1:2], keep[:],
                                                  ALU.mult, ALU.mult))
                    done("slots", dve.tensor_scalar(slot[:], slotf[:].rearrange("p t k -> p (t k)"), 0.0, 2 * SKIP,
                                                    ALU.max, ALU.min))

            begin(dve, step, "z_ln0", "z_n0")
            for i, n in enumerate(("wq1", "wk1", "wq2", "wk2")):
                dve.wait_ge(wT_p, i + 1)
                dve.tensor_copy(wT[n], pool_t[i % 2][:].rearrange("p (c d) -> p c d", c=DC)).then_inc(wT_v, 1)
            dve.wait_ge(wT_p, 5)
            dve.tensor_copy(b1T[:], pool_m[0][:, 0:E * FC + DC]).then_inc(wT_v, 1)
            begin(dve, step, "a_xnT")
            for i, p in enumerate((a1, a2)):
                dve.wait_ge(a_p, i + 1)
                src = pool_s[i][:, 0:DC * D].rearrange("p (c d) -> p c d", c=DC)
                dve.tensor_copy(p[0][:], src).then_inc(const_v, 1)
                dve.wait_ge(const_v, 1 + i)
                dve.tensor_tensor(p[1][:], src, p[0][:], ALU.subtract).then_inc(a_v, 1)
            dve.wait_ge(const_p, 14 + 2 * QT)

            walk(dve, step)


def experts(nc, g):
    (w1, w2, b2, out, xs, ident, b1T, w_in) = (g[n] for n in (
        "w1", "w2", "b2", "out", "xs", "ident", "b1T", "w_in"))
    D, E, F, DC, FC, T, SLOTS, ROW, TOKEN, WEIGHT, CAP, W_IN = (g[n] for n in (
        "D", "E", "F", "DC", "FC", "T", "SLOTS", "ROW", "TOKEN", "WEIGHT", "CAP", "W_IN"))
    CH = 2 * P
    NCH = SLOTS // CH
    PAIR = 2 * NCH
    TILES = SLOTS // P
    YS = 4
    HF = FC // 2
    assert SLOTS % CH == 0 and E % 2 == 0

    with ExitStack() as ctx:
        def sb(name, shape, dt=F32):
            return ctx.enter_context(nc.sbuf_tensor(name, shape, dt))

        def psum(name, shape):
            return ctx.enter_context(nc.psum_tensor(name, shape, F32))

        def sem(name):
            return ctx.enter_context(nc.semaphore(name))

        w1_p = [g["w1_first"], [sb(f"w1_1{h}", [P, DC, F], F16) for h in "hl"]]
        w2_p = [g["w2_first"], [sb(f"w2_1{h}", [P, FC, D], F16) for h in "hl"]]
        w_raw = g["raw_weights"](sb("w_raw", [P, DC * F + FC * D]))
        w1_raw, w2_raw = w_raw
        b2_bc = [sb(f"b2_bc{n}", [P, D]) for n in range(2)]
        slot_x = [sb(f"slot_x{n}", [P, TILES, ROW]) for n in range(2)]
        xT_p = [[sb(f"sxT_{n}{h}", [P, DC, CH], F16) for h in "hl"] for n in range(2)]
        hid = [sb(f"hid{n}", [P, 2, CH]) for n in range(2)]
        hid_p = [[sb(f"hid_{n}{h}", [P, FC, CH], F16) for h in "hl"] for n in range(2)]
        yb = [sb(f"yb{n}", [P, D]) for n in range(2)]
        ys = [sb(f"ys{n}", [P, D]) for n in range(YS)]
        bias = [sb(f"bias{n}", [P, FC]) for n in range(2)]
        bank_x = [psum(f"bank_x{n}", [P, DC, CH]) for n in range(2)]
        bank_h = [psum(f"bank_h{n}", [P, 2, CH]) for n in range(4)]
        bank_y = [psum(f"bank_y{n}", [P, 2, D]) for n in range(2)]

        N = {"w_h": 4, "w_l": 4, "b2_in0": 1, "b2_in1": 1, "head_in0": 1, "head_in1": 1, "tail_in0": 1,
             "tail_in1": 1, "xT_f": PAIR, "xT_h": PAIR, "xT_l": PAIR,
             "h_f": PAIR * HF, "gelu": PAIR * HF, "hid_h": PAIR * HF, "hid_l": PAIR * HF, "y_f": PAIR,
             "y_b": 2 * PAIR, "y_w": 2 * PAIR, "added": 2 * PAIR, "bias": 2, "ys_free": 2 * PAIR}
        DMAS = ("b2_in0", "b2_in1", "head_in0", "head_in1", "tail_in0", "tail_in1", "added")
        ev = {n: sem("e_" + n) for n in N}
        settled = sem("e_settled")

        def unit(n):
            return 16 if n in DMAS else 1

        def done(n, ins):
            ins.then_inc(ev[n], unit(n))

        CREDIT = 64

        def upto(eng, n, j, k):
            eng.wait_ge(ev[n], j * (N[n] * unit(n)) + (CREDIT + k * unit(n)))

        def credit(eng, names):
            for n in names:
                if n != "added":
                    eng.sem_inc(ev[n], CREDIT)

        names = list(N)
        block = ctx.enter_context(nc.Block())

        @block.sync
        def _(sp):
            credit(sp, names[0:4])

            xs_v = xs.rearrange("(e t p) d -> e p t d", p=P, t=TILES)

            def load_slots(j, h):
                upto(sp, "ys_free", j, 2 * NCH * (h - 1))
                done(f"head_in{h % 2}", sp.dma_start(slot_x[h % 2][:, 0:2, :], xs_v[j * 2 + h][:, 0:2, :]))
                done(f"tail_in{h % 2}", sp.dma_start(slot_x[h % 2][:, 2:, :], xs_v[j * 2 + h][:, 2:, :]))

            def two_experts(j, last):
                for h in range(2):
                    if not (last and h == 1):
                        load_slots(j, h + 1)
                    upto(sp, "y_b", j, 2 * NCH * (h - 1))
                    done(f"b2_in{h}", sp.dma_start(b2_bc[h][:], b2[j * 2 + h].partition_broadcast(P)))
                    if not (last and h == 1):
                        upto(sp, "w_l", j, 2 * h + 2)
                        g["load_expert"](sp, j * 2 + (h + 1), w_raw)

            load_slots(0, 0)
            with sp.Fori(0, E // 2 - 1) as j:
                two_experts(j, False)
            two_experts(E // 2 - 1, True)

        @block.gpsimd
        def _(pool):
            credit(pool, names[4:8])

            def two_experts(j, last):
                for n in range(PAIR):
                    h = n // NCH
                    for t in range(2):
                        k = 2 * n + t
                        upto(pool, "y_w", j, k + 1)
                        pool.sem_inc(settled, 1)
                        tile = n % NCH * 2 + t
                        done("added", pool.indirect_dma_start(
                            out, bass.IndirectOffsetOnAxis(ap=slot_x[h][:, tile, TOKEN:TOKEN + 1].bitcast(U32), axis=0),
                            ys[k % YS][:], None, compute_op=ALU.add, oob_is_err=True))
                        pool.wait_ge(ev["added"], j * (16 * 2 * PAIR) + 16 * (k + 1))
                        pool.sem_inc(ev["ys_free"], 1)

            with pool.Fori(0, E // 2 - 1) as j:
                two_experts(j, False)
            two_experts(E // 2 - 1, True)

        @block.tensor
        def _(pe):
            credit(pe, names[8:12])

            def turn(j, n):
                h, c = n // NCH, n % NCH
                if c < 2:
                    upto(pe, f"{'tail' if c else 'head'}_in{h % 2}", j, h // 2 + 1)
                upto(pe, "xT_l", j, n - 1)
                for d in range(DC):
                    for t in range(2):
                        m = pe.transpose(bank_x[n % 2][:, d, t * P:(t + 1) * P],
                                         slot_x[h % 2][:, 2 * c + t, d * P:(d + 1) * P], ident[:])
                done("xT_f", m)

            def two_experts(j, last):
                for n in range(PAIR):
                    h = n // NCH
                    if n % NCH == 0:
                        upto(pe, "w_l", j, 2 * h + 2)
                    upto(pe, "xT_l", j, n + 1)
                    for b in range(HF):
                        k = n * HF + b
                        upto(pe, "hid_l", j, k - 3)
                        bank = bank_h[k % 4]
                        for f2 in range(2):
                            f = 2 * b + f2
                            for d in range(DC):
                                fs = slice(f * P, (f + 1) * P)
                                m = mm3(pe, bank[:, f2, :], (w1_p[h][0][:, d, fs], w1_p[h][1][:, d, fs]),
                                        (xT_p[n % 2][0][:, d, :], xT_p[n % 2][1][:, d, :]), d == 0, d == DC - 1)
                        done("h_f", m)
                    if not (last and n == PAIR - 1):
                        turn(j, n + 1)
                    upto(pe, "y_b", j, 2 * n - 2)
                    for t in range(2):
                        for f in range(FC):
                            if t == 0 and f % 2 == 0:
                                upto(pe, "hid_l", j, n * HF + f // 2 + 1)
                            ts = slice(t * P, (t + 1) * P)
                            m = mm3(pe, bank_y[n % 2][:, t, :],
                                    (hid_p[n % 2][0][:, f, ts], hid_p[n % 2][1][:, f, ts]),
                                    (w2_p[h][0][:, f, :], w2_p[h][1][:, f, :]), f == 0, f == FC - 1)
                    done("y_f", m)

            turn(0, 0)
            with pe.Fori(0, E // 2 - 1) as j:
                two_experts(j, False)
            two_experts(E // 2 - 1, True)

        @block.scalar
        def _(act):
            credit(act, names[12:14])

            def split_high(j, h):
                act.wait_ge(w_in, j * (2 * W_IN) + W_IN * (h + 1))
                upto(act, "y_f", j, NCH * (h - 1))
                done("bias", act.activation(bias[h % 2][:], b1T[:, bass.ds((j * 2 + h) * FC, FC)], ACT.Copy))
                done("w_h", act.activation(w1_p[h % 2][0][:], w1_raw, ACT.Copy))

            def split_high2(j, h):
                done("w_h", act.activation(w2_p[h % 2][0][:], w2_raw, ACT.Copy))

            def two_experts(j, last):
                for n in range(PAIR):
                    h = n // NCH
                    if n % NCH == 0:
                        upto(act, "bias", j, h + 1)
                    for b in range(HF):
                        k = n * HF + b
                        upto(act, "h_f", j, k + 1)
                        upto(act, "hid_l", j, k - 1)
                        for f2 in range(2):
                            f = 2 * b + f2
                            m = act.activation(hid[b % 2][:, f2, :], bank_h[k % 4][:, f2, :], ACT.Gelu,
                                               bias=bias[h][:, f:f + 1])
                        done("gelu", m)
                    if not (last and n == PAIR - 1):
                        slots_high(j, n + 1)
                    if n % NCH == 1 and not (last and h == 1):
                        split_high(j, h + 1)
                    if n % NCH == 2 and not (last and h == 1):
                        split_high2(j, h + 1)

            def slots_high(j, n):
                upto(act, "xT_f", j, n + 1)
                upto(act, "h_f", j, HF * (n - 1))
                done("xT_h", act.activation(xT_p[n % 2][0][:], bank_x[n % 2][:], ACT.Copy))

            act.sem_inc(ev["w_h"], 2)
            done("bias", act.activation(bias[0][:], b1T[:, 0:FC], ACT.Copy))
            act.activation(bias[1][:, 0:1], ident[:, 0:1], ACT.Gelu)
            slots_high(0, 0)
            with act.Fori(0, E // 2 - 1) as j:
                two_experts(j, False)
            two_experts(E // 2 - 1, True)

        @block.vector
        def _(dve):
            credit(dve, names[14:])

            def split_low(j, h, n):
                upto(dve, "w_h", j, 2 * h + n + 1)
                part, raw = ((w1_p, w1_raw), (w2_p, w2_raw))[n]
                done("w_l", dve.tensor_tensor(part[h % 2][1][:], raw, part[h % 2][0][:], ALU.subtract))

            def slots_low(j, n):
                upto(dve, "xT_h", j, n + 1)
                done("xT_l", dve.tensor_tensor(xT_p[n % 2][1][:], bank_x[n % 2][:], xT_p[n % 2][0][:],
                                               ALU.subtract))

            def two_experts(j, last):
                for n in range(PAIR):
                    h = n // NCH
                    for b in range(HF):
                        k = n * HF + b
                        upto(dve, "gelu", j, k + 1)
                        if b == 0:
                            upto(dve, "y_f", j, n - 1)
                        fs = slice(2 * b, 2 * b + 2)
                        done("hid_h", dve.tensor_copy(hid_p[n % 2][0][:, fs, :], hid[b % 2][:]))
                        upto(dve, "hid_h", j, k + 1)
                        done("hid_l", dve.tensor_tensor(hid_p[n % 2][1][:, fs, :], hid[b % 2][:],
                                                        hid_p[n % 2][0][:, fs, :], ALU.subtract))
                    if not (last and n == PAIR - 1):
                        slots_low(j, n + 1)
                    upto(dve, "y_f", j, n + 1)
                    if n % NCH == 0:
                        upto(dve, f"b2_in{h}", j, 1)
                    for t in range(2):
                        k = 2 * n + t
                        done("y_b", dve.tensor_tensor(yb[t][:], bank_y[n % 2][:, t, :], b2_bc[h][:], ALU.add))
                        upto(dve, "y_b", j, k + 1)
                        upto(dve, "ys_free", j, k - YS + 1)
                        choice = (n % NCH * 2 + t) // (CAP // P)
                        weight = slot_x[h][:, n % NCH * 2 + t, WEIGHT + choice:WEIGHT + choice + 1]
                        done("y_w", dve.tensor_scalar(ys[k % YS][:], yb[t][:], weight, None, ALU.mult))
                    if n % NCH in (1, 2) and not (last and h == 1):
                        split_low(j, h + 1, n % NCH - 1)

            dve.sem_inc(ev["w_l"], 2)
            slots_low(0, 0)
            with dve.Fori(0, E // 2 - 1) as j:
                two_experts(j, False)
            two_experts(E // 2 - 1, True)


_INS = ['x', 'ctx_1024', 'g_xattn', 'g_ffn', 'L0_xattn_Wq1', 'L0_xattn_Wk1', 'L0_xattn_Wv1', 'L0_xattn_Wq2',
        'L0_xattn_Wk2', 'L0_xattn_Wv2', 'L0_xattn_fc1_w', 'L0_xattn_fc1_b', 'L0_xattn_fc2_w', 'L0_xattn_fc2_b',
        'L0_xattn_ln1_g', 'L0_xattn_ln1_b', 'L0_xattn_ln2_g', 'L0_xattn_ln2_b', 'L0_xattn_ln3_g', 'L0_xattn_ln3_b',
        'L0_ffn_Wr', 'L0_ffn_W1', 'L0_ffn_b1', 'L0_ffn_W2', 'L0_ffn_b2']


def kernel(**inputs):
    import numpy as _np
    import concourse.bacc as _bacc
    from concourse import mybir as _mybir
    from concourse.bass_utils import run_bass_kernel_spmd as _run

    nc = _bacc.Bacc("TRN2", target_bir_lowering=False, num_devices=1)
    arrays, args = {}, []
    for name in _INS:
        a = _np.ascontiguousarray(inputs[name])
        arrays[f"in_{name}_dram"] = a
        args.append(nc.dram_tensor(f"in_{name}_dram", a.shape, _mybir.dt.from_np(a.dtype), kind="ExternalInput").ap())
    b, s, d = inputs["x"].shape
    tokens, experts_ = b * s, inputs["L0_ffn_Wr"].shape[1]
    out = nc.dram_tensor("out_0_dram", (tokens + 128, d), _mybir.dt.float32, kind="ExternalOutput").ap()
    slots = experts_ * 2 * int(tokens * 1.25 / experts_)
    xs = nc.dram_tensor("slot_rows", (slots, d + 4), _mybir.dt.float32, kind="Internal").ap()
    flamingo_moe_kernel(nc, *args, out, xs)
    r = _run(nc, [arrays], core_ids=[0])
    return r.results[0]["out_0_dram"][:tokens].reshape(b, s, d)
```
